# Optimizing a Trainium2 kernel written in Bass

```python
import numpy as np
import jax
import jax.numpy as jnp

def _softmax(x, axis=-1):
    return jax.nn.softmax(x, axis=axis)

def _gelu(x):
    return jax.nn.gelu(x, approximate=True)

def _silu(x):
    return jax.nn.silu(x)

def _sigmoid(x):
    return jax.nn.sigmoid(x)

def _layernorm(x, axis=-1, eps=1e-05):
    m = jnp.mean(x, axis=axis, keepdims=True)
    v = jnp.var(x, axis=axis, keepdims=True)
    return (x - m) / jnp.sqrt(v + eps)

def _scatter_add(tgt, idx, src, axis=0):
    return tgt.at[idx].add(src)

def _segment_sum(src, seg, n):
    return jax.ops.segment_sum(src, seg, n)
kernel_name = 'mk_decoder_preln_d1_seqx_r8_06d996'

def setup_inputs(seed: int=0):
    np.random.seed(seed)
    _w = jnp.asarray

    def _rec_inputs():
        import jax
        import jax.numpy as jnp
        _rk = jax.random.key(seed)
        x = 7.22e-05 + 1 * jax.random.normal(jax.random.fold_in(_rk, 1), (4, 256, 256), jnp.float32)
        _lenS = 256 - jax.random.randint(jax.random.fold_in(_rk, 7), (4,), 0, max(1, 256 // 4) + 1, jnp.int32)
        _lenS2 = 256 - jax.random.randint(jax.random.fold_in(_rk, 8), (4,), 0, max(1, 256 // 4) + 1, jnp.int32)
        _ctx_1024P = jax.random.normal(jax.random.fold_in(_rk, 11), (4, 16, 128), jnp.float32)
        _ctx_1024c = jax.random.dirichlet(jax.random.fold_in(_rk, 511), 0.3 * jnp.ones((16,), jnp.float32), (4, 256))
        _ctx_1024t = jnp.einsum('bsk,bkd->bsd', _ctx_1024c, _ctx_1024P)
        _ctx_1024t = _ctx_1024t * jax.lax.rsqrt(jnp.mean(jnp.square(_ctx_1024t)) + 1e-12) * 0.953939
        ctx_1024 = 2.81802e-05 + 1.00001 * (_ctx_1024t + 0.3 * jax.random.normal(jax.random.fold_in(_rk, 611), (4, 256, 128), jnp.float32))
        return (x, ctx_1024)
    x, ctx_1024 = _rec_inputs()

    def _L0_attn_setup():
        import jax, jax.numpy as jnp
        import numpy as np
        N_HEADS = 16
        NEG_INF = -1e+30
        key = jax.random.key(seed)
        ks = jax.random.split(key, 5)
        B, S, D = (2, 256, 256)
        scale_w = 1.0 / np.sqrt(D)
        return {'x': jax.random.normal(ks[0], (B, S, D), dtype=jnp.float32), 'Wq': jax.random.normal(ks[1], (D, D), dtype=jnp.float32) * scale_w, 'Wk': jax.random.normal(ks[2], (D, D), dtype=jnp.float32) * scale_w, 'Wv': jax.random.normal(ks[3], (D, D), dtype=jnp.float32) * scale_w, 'Wo': jax.random.normal(ks[4], (D, D), dtype=jnp.float32) * scale_w}
    _L0_attn_all = _L0_attn_setup()
    _L0_attn_in = {k: v for k, v in _L0_attn_all.items() if k in ('Wq', 'Wk', 'Wv', 'Wo')}
    del _L0_attn_all

    def _L0_xattn_setup():
        import jax, jax.numpy as jnp
        import numpy as np
        key = jax.random.key(seed)
        ks = jax.random.split(key, 6)
        B, L, N, C, D = (8, 64, 256, 128, 128)
        return {'teacher_logits': jax.random.normal(ks[0], (B, L, N), dtype=jnp.float32), 'teacher_features': jax.random.normal(ks[1], (B, N, C), dtype=jnp.float32), 'Wq': jax.random.normal(ks[2], (D, C), dtype=jnp.float32) * (1.0 / np.sqrt(C)), 'bq': jnp.zeros((D,), dtype=jnp.float32), 'Wk': jax.random.normal(ks[3], (D, C), dtype=jnp.float32) * (1.0 / np.sqrt(C)), 'bk': jnp.zeros((D,), dtype=jnp.float32)}
    _L0_xattn_all = _L0_xattn_setup()
    _L0_xattn_in = {k: v for k, v in _L0_xattn_all.items() if k in ('Wq', 'bq', 'Wk', 'bk')}
    del _L0_xattn_all

    def _L0_ffn_setup():
        import jax, jax.numpy as jnp
        import numpy as np
        B, T, D = (2, 128, 256)
        E, F, K = (64, 64, 4)
        S, HS = (2, 64 * 4)
        key = jax.random.key(seed)
        ks = jax.random.split(key, 9)
        s = 0.02
        f32 = jnp.float32
        return {'x': jax.random.normal(ks[0], (B, T, D), f32), 'router_w': jax.random.normal(ks[1], (D, E), f32) * s, 'router_bias': jnp.zeros((E,), f32), 'wg': jax.random.normal(ks[2], (E, D, F), f32) * s, 'wu': jax.random.normal(ks[3], (E, D, F), f32) * s, 'wd': jax.random.normal(ks[4], (E, F, D), f32) * s, 'swg': jax.random.normal(ks[5], (S, D, HS), f32) * s, 'swu': jax.random.normal(ks[6], (S, D, HS), f32) * s, 'swd': jax.random.normal(ks[7], (S, HS, D), f32) * s}
    _L0_ffn_all = _L0_ffn_setup()
    _L0_ffn_in = {k: v for k, v in _L0_ffn_all.items() if k in ('router_w', 'router_bias', 'wg', 'wu', 'wd', 'swg', 'swu', 'swd')}
    del _L0_ffn_all
    return {'x': x, 'ctx_1024': ctx_1024, 'L0_attn_Wq': _L0_attn_in['Wq'], 'L0_attn_Wk': _L0_attn_in['Wk'], 'L0_attn_Wv': _L0_attn_in['Wv'], 'L0_attn_Wo': _L0_attn_in['Wo'], 'L0_xattn_Wq': _L0_xattn_in['Wq'], 'L0_xattn_bq': _L0_xattn_in['bq'], 'L0_xattn_Wk': _L0_xattn_in['Wk'], 'L0_xattn_bk': _L0_xattn_in['bk'], 'L0_ffn_router_w': _L0_ffn_in['router_w'], 'L0_ffn_router_bias': _L0_ffn_in['router_bias'], 'L0_ffn_wg': _L0_ffn_in['wg'], 'L0_ffn_wu': _L0_ffn_in['wu'], 'L0_ffn_wd': _L0_ffn_in['wd'], 'L0_ffn_swg': _L0_ffn_in['swg'], 'L0_ffn_swu': _L0_ffn_in['swu'], 'L0_ffn_swd': _L0_ffn_in['swd']}

def reference(x, ctx_1024, L0_attn_Wq, L0_attn_Wk, L0_attn_Wv, L0_attn_Wo, L0_xattn_Wq, L0_xattn_bq, L0_xattn_Wk, L0_xattn_bk, L0_ffn_router_w, L0_ffn_router_bias, L0_ffn_wg, L0_ffn_wu, L0_ffn_wd, L0_ffn_swg, L0_ffn_swu, L0_ffn_swd):
    import jax
    import jax.numpy as jnp

    def _L0_attn_ref(x, Wq, Wk, Wv, Wo):
        import jax, jax.numpy as jnp
        import numpy as np
        N_HEADS = 16
        NEG_INF = -1e+30
        B, S, D = x.shape
        H = N_HEADS
        dk = D // H
        scale = 1.0 / np.sqrt(dk)

        def heads(w):
            return (x @ w).reshape(B, S, H, dk)
        q = heads(Wq)
        k = heads(Wk)
        v = heads(Wv)
        scores = jnp.einsum('bqhd,bkhd->bhqk', q, k) * scale
        causal = jnp.tril(jnp.ones((S, S), dtype=bool))
        scores = jnp.where(causal, scores, NEG_INF)
        p = jax.nn.softmax(scores, axis=-1)
        o = jnp.einsum('bhqk,bkhd->bqhd', p, v).reshape(B, S, D)
        return o @ Wo

    def _L0_xattn_ref(teacher_logits, teacher_features, Wq, bq, Wk, bk):
        import jax, jax.numpy as jnp
        import numpy as np
        query = jnp.einsum('bnc,dc->bnd', teacher_features, Wq) + bq
        key = jnp.einsum('bnc,dc->bnd', teacher_features, Wk) + bk
        energy = jnp.einsum('bnd,bmd->bnm', query, key)
        attention = jax.nn.softmax(energy, axis=-1)
        x_m = jnp.einsum('bln,bmn->blm', teacher_logits, attention)
        return x_m

    def _L0_ffn_ref(x, router_w, router_bias, wg, wu, wd, swg, swu, swd):
        import jax, jax.numpy as jnp
        import numpy as np
        B, T, D = (2, 128, 256)
        E, F, K = (64, 64, 4)
        S, HS = (2, 64 * 4)
        b, t, d = x.shape
        flat = x.reshape(b * t, d)
        n = flat.shape[0]
        logits = flat @ router_w
        scores = jax.nn.softmax(logits, axis=-1)
        _, topk_idx = jax.lax.top_k(logits + router_bias, K)
        topk_scores = jnp.take_along_axis(scores, topk_idx, axis=-1)
        topk_scores = topk_scores / topk_scores.sum(axis=-1, keepdims=True)
        comb = jnp.zeros((n, E), dtype=flat.dtype).at[jnp.arange(n)[:, None], topk_idx].set(topk_scores)
        g = jax.nn.silu(jnp.einsum('nd,edf->nef', flat, wg))
        u = jnp.einsum('nd,edf->nef', flat, wu)
        routed = jnp.einsum('ne,nef,efd->nd', comb, g * u, wd)
        sg = jax.nn.silu(jnp.einsum('nd,sdh->nsh', flat, swg))
        su = jnp.einsum('nd,sdh->nsh', flat, swu)
        shared = jnp.einsum('nsh,shd->nd', sg * su, swd)
        return (routed + shared).reshape(b, t, d)
    x = x + _L0_attn_ref(_layernorm(x, axis=-1), L0_attn_Wq, L0_attn_Wk, L0_attn_Wv, L0_attn_Wo)
    x = x + _L0_xattn_ref(_layernorm(x, axis=-1), ctx_1024, L0_xattn_Wq, L0_xattn_bq, L0_xattn_Wk, L0_xattn_bk)
    x = x + _L0_ffn_ref(_layernorm(x, axis=-1), L0_ffn_router_w, L0_ffn_router_bias, L0_ffn_wg, L0_ffn_wu, L0_ffn_wd, L0_ffn_swg, L0_ffn_swu, L0_ffn_swd)
    return x

_drawn_inputs = setup_inputs


def setup_inputs(seed=0):
    import zlib

    import numpy as np

    out = dict(_drawn_inputs(seed))
    spreads = {'L0_xattn_bq': (0.0, 0.1), 'L0_xattn_bk': (0.0, 0.8), 'L0_ffn_router_bias': (0.0, 0.8)}
    factors = {'L0_ffn_router_w': 8.0,
     'L0_ffn_wg': 8.0,
     'L0_ffn_wu': 8.0,
     'L0_ffn_wd': 8.0,
     'L0_ffn_swg': 3.142,
     'L0_ffn_swu': 3.109,
     'L0_ffn_swd': 3.111}
    for name, (base, spread) in spreads.items():
        noise = np.random.default_rng([zlib.crc32(name.encode()), seed]).standard_normal(out[name].shape)
        drawn = base * np.exp(spread * noise) if base else spread * noise
        out[name] = jnp.asarray(drawn.astype(out[name].dtype))
    for name, factor in factors.items():
        out[name] = (out[name] * factor).astype(out[name].dtype)
    return out
```

```python
from contextlib import ExitStack

import concourse.bass as bass
from concourse import mybir

P = 128
ALU = mybir.AluOpType
ACT = mybir.ActivationFunctionType
F32 = mybir.dt.float32
BF16 = mybir.dt.bfloat16
I32 = mybir.dt.int32
U32 = mybir.dt.uint32
AX = mybir.AxisListType

HEADS = 16
EPS = 1e-5
MASKED = -1e30
TOP = 4
PARTS = 6
MISC_BANKS = 4
PT_SLOTS = 8
ROW_SLOTS = 4
SKIPPED = 8192


def stage_order(batches):
    order = [("ln1_stats", 0), ("ln1_apply", 0), ("x_weights",)]
    last = batches - 1
    for k in range(batches + 2):
        if k <= last:
            order += [("x_turn", k), ("qk", k, 0), ("qk", k, 1), ("v", k)]
            if k < last:
                order += [("ln1_stats", k + 1), ("ln1_apply", k + 1)]
        if 1 <= k <= last + 1:
            order += [("m_turn", k - 1), ("ctx_turn", k - 1), ("ctx_qk", k - 1)]
        if k <= last:
            order += [("stack", k, t, x, half) for t in range(2) for x in range(2) for half in range(2)]
        fill = {}
        if k >= 2:
            fill = {0: [("o_back", k - 2, 0), ("o_back", k - 2, 1)], 2: [("o_turn", k - 2)], 4: [("wo", k - 2), ("ln2_stats", k - 2)],
                    6: [("ln2_apply", k - 2), ("ln2_turn", k - 2)], 8: [("xattn", k - 2), ("ln3_stats", k - 2)],
                    10: [("ln3_apply", k - 2), ("ln3_turn", k - 2)], 12: [("router", k - 2)], 14: [("choose", k - 2)]}
        if 1 <= k <= last + 1:
            fill.setdefault(1, []).append(("energy", k - 1))
            fill.setdefault(7, []).append(("att_turn", k - 1))
        if k == last + 2:
            fill[1] = [("sh_up", 0)]
            fill[3] = [("sh_up", 1)]
            fill[5] = [("sh_up", 2)]
            fill[7] = [("sh_up", 3)]
            fill[9] = [("sh_down", 0), ("sh_down", 1)]
            fill[11] = [("sh_down", 2)]
            fill[13] = [("sh_down", 3)]
        for h in range(HEADS):
            if k <= last:
                order.append(("scores", k, h))
            if 1 <= k <= last + 1:
                order.append(("probs", k - 1, h))
                if h % 2 == 1:
                    order.append(("causal", k - 1, h // 2))
                if h % 4 == 1 and h > 4:
                    order.append(("pv", k - 1, h // 4 - 1))
            order += fill.get(h, [])
        if k <= last:
            order.append(("m_parts", k))
        if 1 <= k <= last + 1:
            order.append(("pv", k - 1, HEADS // 4 - 1))
    order += [("rank",), ("sh_up", 4), ("starts",), ("sh_up", 5), ("tiles",), ("positions",)]
    order += [("sh_up", 6), ("sh_up", 7)] + [("sh_down", T) for T in range(4, 8)]
    return order


IN_MISC = ("x_weights", "x_turn", "qk", "v", "m_turn", "ctx_turn", "ctx_qk", "stack", "energy", "att_turn",
           "o_back", "o_turn", "wo", "ln2_turn", "xattn", "ln3_turn", "router", "pv", "sh_down", "rank", "starts", "tiles")


def decoder_layer(nc, x, ctx, wq, wk, wv, wo, xwq, xbq, xwk, xbk, rw, rb, wg, wu, wd, swg, swu, swd, out):
    B, S, D = x.shape
    C = ctx.shape[2]
    E, _, F = wg.shape
    SH, _, HS = swg.shape
    DK = D // HEADS
    N = B * S
    NT = N // P
    TB = S // P
    DC = D // P
    HC = SH * HS // P
    PAIRS = N * TOP
    MAX_TILES = PAIRS // P + E
    MAX_TILES = -(-MAX_TILES // 4) * 4
    ROW = D + 2
    SCALE = float(DK) ** -0.5
    assert TB == 2 and DC == 2 and C == P and HEADS * DK == D and F * 2 == P and D == 2 * P and HC == 4

    ORDER = stage_order(B)
    MISC = {s: i for i, s in enumerate([s for s in ORDER if s[0] in IN_MISC])}

    with ExitStack() as stack:
        def sb(name, shape, dt=F32):
            return stack.enter_context(nc.sbuf_tensor("sb_" + name, shape, dt))

        def sem(name):
            return stack.enter_context(nc.semaphore(name))

        def bank(name):
            return stack.enter_context(nc.psum_tensor("ps_" + name, [P, 512], F32))

        score_banks = [bank("s0"), bank("s1")]
        prob_banks = [bank("p0"), bank("p1")]
        misc = [bank(f"m{i}") for i in range(MISC_BANKS)]

        rows_dram = nc.dram_tensor("rows_scratch", (PAIRS + P, ROW), F32, kind="Internal").ap()
        y_dram = nc.dram_tensor("y_scratch", (PAIRS, D), F32, kind="Internal").ap()

        shared_region = sb("attention_or_down", [P, E * D])
        at = [0]

        def part(words):
            at[0] += words
            return shared_region[:, at[0] - words:at[0]]
        stacks = [part(2 * HEADS * S // 2).bitcast(BF16).rearrange("p (x h t) -> p x h t", x=2, h=HEADS) for _ in range(2)]
        pt = part(PT_SLOTS * 3 * P).rearrange("p (s c) -> p s c", s=PT_SLOTS)
        stk = [part(HEADS * PARTS * DK).bitcast(BF16).rearrange("p (x h r d) -> p x h r d", x=2, h=HEADS, r=PARTS)
               for _ in range(2)]
        v_ones = [part(TB * HEADS * 32).rearrange("p (t h j) -> p t h j", t=TB, h=HEADS) for _ in range(2)]
        down_w = shared_region[0:F, :].rearrange("p (e n) -> p e n", e=E)

        gate_up = sb("gate_up", [P, DC, E, 2 * F])
        sh_g = sb("sh_g", [P, DC, SH * HS])
        sh_u = sb("sh_u", [P, DC, SH * HS])
        w_qkv = sb("w_qkv", [P, DC, 3 * D])
        wq_flat = w_qkv[:, :, :].rearrange("p c n -> p (c n)")
        sh_d = wq_flat[:, 0:HC * D].rearrange("p (j n) -> p j n", j=HC)
        w_o = sb("w_o", [P, DC, D])
        xres = sb("xres", [P, NT, D])
        flat = sb("flat", [P, NT, D])
        flat_t = sb("flat_t", [P, DC, N])
        rows_or_at = sb("rows_or_at", [P, ROW_SLOTS * ROW])
        att_t = rows_or_at[:, 0:2 * DC * S].rearrange("p (b c m) -> p b c m", b=2, c=DC)
        row_out = rows_or_at[:, :].rearrange("p (s r) -> p s r", s=ROW_SLOTS)
        chosen = sb("chosen", [P, NT, TOP, E], BF16)
        o_t = sb("o_t", [P, 4, S])
        tok = sb("tok", [P, TB, D])
        feat = sb("feat", [P, DC, S])
        early = sb("early", [P, 3 * 1024])
        part1 = early[:, 0:256].bitcast(BF16)
        part2 = early[:, 256:512].bitcast(BF16)
        rest = early[:, 512:1024]
        ctx_sb = early[:, 1024:1280].rearrange("p (t c) -> p t c", t=TB)
        ctx_t = early[:, 1280:1536]
        ctx_qk = early[:, 1536:2048].rearrange("p (x t) -> p x t", x=2)
        att = early[:, 2048:2560].rearrange("p (t n) -> p t n", t=TB)
        x_t = early[:, 2560:3072].rearrange("p (c t) -> p c t", c=DC)
        hid = early[:, 0:2048].rearrange("p (j t) -> p j t", j=HC)
        sil = early[:, 2048:3072].rearrange("p (s t) -> p s t", s=2)
        o_flat = o_t[:, :, :].rearrange("p g t -> p (g t)")
        x_w = o_flat[:, 0:2 * C].rearrange("p (x c) -> p x c", x=2)
        x_wt = sb("x_wt", [P, 2, C])
        x_bias = sb("x_bias", [P, 2])
        r_w = sb("r_w", [P, DC, E])
        r_bias = sb("r_bias", [P, E])

        ident = sb("ident", [P, P])
        ident_b = sb("ident_b", [P, P], BF16)
        mask_b = sb("mask_b", [P, 2, P], BF16)
        before_b = sb("before_b", [P, P], BF16)
        ones_b = sb("ones_b", [P, P], BF16)
        ones = sb("ones", [P, P])
        before = sb("before", [E, E])
        upto = sb("upto", [E, E])
        iota_e = sb("iota_e", [P, E])
        iota_t = sb("iota_t", [P, MAX_TILES])
        iota_p = sb("iota_p", [P, 1])
        neg_half = sb("neg_half", [P, 2])
        pair_info = sb("pair_info", [P, NT * TOP, 2])
        bn = sb("bn", [P, TB, 6])
        mv = sb("mv", [P, TB, 2])
        rstd = sb("rstd", [P, 2])
        m_raw = sb("m_raw", [P, HEADS, 3])
        m_neg = sb("m_neg", [P, TB, HEADS])
        m_rest = sb("m_rest", [P, TB, HEADS])
        m_part = sb("m_part", [P, TB, 3, HEADS], BF16)
        m_t = sb("m_t", [3 * HEADS, S], BF16)
        o_rec = sb("o_rec", [P, HEADS])
        e_max = sb("e_max", [P, 4])
        e_sum = sb("e_sum", [P, 4])
        logits = sb("logits", [P, TB, E])
        biased = sb("biased", [P, TB, E])
        expd = sb("expd", [P, TB, E])
        top8 = sb("top8", [P, TB, 8])
        top_i = sb("top_i", [P, TB, 8], U32)
        top_f = sb("top_f", [P, TB, 8])
        r_max = sb("r_max", [P, 2])
        r_sum = sb("r_sum", [P, 2])
        top_s = sb("top_s", [P, TB, TOP])
        top_sum = sb("top_sum", [P, 2])
        chose = sb("chose", [P, NT, E], BF16)
        cnt = sb("cnt", [E, 8])
        cnt_i = sb("cnt_i", [E, 1], I32)
        cnt_q = sb("cnt_q", [P, 1], I32)
        wide = o_flat[0:E, 0:3 * P].rearrange("p (r c) -> p r c", r=3)
        in_tile = o_flat[0:E, 384:384 + 2 * MAX_TILES].rearrange("p (r c) -> p r c", r=2)
        tile_f = o_flat[:, 640:640 + 2 * MAX_TILES].rearrange("p (r c) -> p r c", r=2)
        rank_sb = feat[:, :, :].rearrange("p c t -> p (c t)").rearrange("p (t e) -> p t e", t=NT)
        penalty = sb("penalty", [P, MAX_TILES])
        tile_i = sb("tile_i", [P, 2 * MAX_TILES + 1], I32)
        pos_i = sb("pos_i", [P, NT * TOP], I32)
        prod = tok[:, :, :].rearrange("p t (k e) -> p t k e", k=TOP)
        pos_f = sb("pos_f", [P, NT * TOP])

        row_in = early[:, 0:4 * ROW].rearrange("p (s r) -> p s r", s=4)
        y_out = early[:, 4 * ROW:4 * ROW + 4 * D].rearrange("p (s n) -> p s n", s=4)
        xt_in = wq_flat[:, 0:2 * D].rearrange("p (s c t) -> p s c t", s=2, c=DC)
        sil_in = wq_flat[:, 512:640].rearrange("p (s f) -> p s f", s=2)
        h_in = wq_flat[:, 640:768].rearrange("p (s f) -> p s f", s=2)
        ht_in = wq_flat[0:F, 768:1024].rearrange("p (s t) -> p s t", s=2)
        pair_i = sb("pair_i", [P, 4], I32)
        pair_w = sb("pair_w", [P, 4])
        y_back = gate_up[:, :, :, :].rearrange("p c e f -> p (c e f)")[:, 0:NT * TOP * D] \
            .rearrange("p (t k n) -> p t k n", t=NT, k=TOP)

        x_in = [sem(f"x_in{b}") for b in range(B)]
        qkv_in, wo_in, xw_in, xb_in, r_in, shg_in, shd_in = map(sem, ("qkv_in", "wo_in", "xw_in", "xb_in", "r_in", "shg_in", "shd_in"))
        gu_in, dw_in, tail_in = map(sem, ("gu_in", "dw_in", "tail_in"))
        ctx_in = sem("ctx_in")
        misc_full = [sem(f"misc_full{i}") for i in range(MISC_BANKS)]
        misc_free = [sem(f"misc_free{i}") for i in range(MISC_BANKS)]
        (consts, ident_ok, var_ok, rstd_ok, ln1_ok, tok_ok, feat_ok, xt_ok, part1_ok, rest_ok, part2_ok, stk_ok, stk3_ok, stk_used,
         v_ok, stack_ok_d, stack_ok_a, m_part_ok, mt_ok, m_rows, dve, pool, act) = map(sem, (
             "consts", "ident_ok", "var_ok", "rstd_ok", "ln1_ok", "tok_ok", "feat_ok", "xt_ok", "part1_ok", "rest_ok", "part2_ok",
             "stk_ok", "stk3_ok", "stk_used", "v_ok", "stack_ok_d", "stack_ok_a", "m_part_ok", "mt_ok", "m_rows",
             "dve", "pool", "act"))
        (scores_full, scores_used, probs_full, probs_used, causal_ok, pv_done, ot_ok, ctxt_ok, ctxqk_ok, emax_ok, esum_ok, att_ok,
         attt_ok, res_ok, flatt_ok, logits_ok, expd_ok, chose_ok, info_ok) = map(sem, (
             "scores_full", "scores_used", "probs_full", "probs_used", "causal_ok", "pv_done", "ot_ok", "ctxt_ok", "ctxqk_ok",
             "emax_ok", "esum_ok", "att_ok", "attt_ok", "res_ok", "flatt_ok", "logits_ok", "expd_ok", "chose_ok", "info_ok"))
        (up_full, sil_ok, hid_ok, down_done, count_ok, span_ok, tiles_ok, pos_ok, iota_ok, xwt_ok) = map(sem, (
            "up_full", "sil_ok", "hid_ok", "down_done", "count_ok", "span_ok", "tiles_ok", "pos_ok", "iota_ok", "xwt_ok"))
        rows_filled = sem("rows_filled")
        row_sent = [sem(f"row_sent{i}") for i in range(ROW_SLOTS)]
        row_here = [sem(f"row_here{i}") for i in range(4)]
        y_sent = [sem(f"y_sent{i}") for i in range(4)]
        (turned, xt_here, gu_done, sil_here, h_here, h_turned, ht_here, y_done, y_here, pair_here) = map(sem, (
            "turned", "xt_here", "gu_done", "sil_here", "h_here", "h_turned", "ht_here", "y_done", "y_here", "pair_here"))
        y_loaded = [sem(f"y_loaded{T}") for T in range(NT)]
        sum_ok, stored = sem("sum_ok"), sem("stored")

        def misc_take(eng, s):
            i = MISC[s]
            if i >= MISC_BANKS:
                eng.wait_ge(misc_free[i % MISC_BANKS], i // MISC_BANKS)
            return misc[i % MISC_BANKS]

        def misc_wait(eng, s):
            i = MISC[s]
            eng.wait_ge(misc_full[i % MISC_BANKS], i // MISC_BANKS + 1)
            return misc[i % MISC_BANKS]

        def full(s):
            return misc_full[MISC[s] % MISC_BANKS]

        def free(s):
            return misc_free[MISC[s] % MISC_BANKS]

        def as_bf16(b):
            return b[:, :].bitcast(BF16)

        def key_blocks(blocks, h):
            v = blocks.rearrange("p (a c) -> p a c", a=3)
            return (v[:, 1::-1, :], v[:, 2, :]) if h % 2 == 0 else (v[:, 1:3, :], v[:, 0, :])

        block = stack.enter_context(nc.Block())
        NG = HEADS // 4

        @block.sync
        def _(sp):
            for b in range(B):
                sp.dma_start(xres[:, b * TB:(b + 1) * TB, :], x[b].rearrange("(t p) d -> p t d", p=P)).then_inc(x_in[b], 16)
                if b == 0:
                    for i, w in enumerate((wq, wk, wv)):
                        sp.dma_start(w_qkv[:, :, i * D:(i + 1) * D], w.rearrange("(c p) n -> p c n", p=P)).then_inc(qkv_in, 16)
            sp.dma_start(x_w[:, 0, :], xwq).then_inc(xw_in, 16)
            sp.dma_start(x_w[:, 1, :], xwk).then_inc(xw_in, 16)
            sp.dma_start(x_bias[:, 0:1], xbq.rearrange("(p o) -> p o", o=1)).then_inc(xb_in, 16)
            sp.dma_start(x_bias[:, 1:2], xbk.rearrange("(p o) -> p o", o=1)).then_inc(xb_in, 16)
            sp.dma_start(w_o[:, :, :], wo.rearrange("(c p) n -> p c n", p=P)).then_inc(wo_in, 16)
            sp.dma_start(r_w[:, :, :], rw.rearrange("(c p) n -> p c n", p=P)).then_inc(r_in, 16)
            sp.dma_start(r_bias[:, :], rb.rearrange("(o e) -> o e", o=1).broadcast_to([P, E])).then_inc(r_in, 16)
            for s in range(SH):
                sp.dma_start(sh_g[:, :, s * HS:(s + 1) * HS], swg[s].rearrange("(c p) h -> p c h", p=P)).then_inc(shg_in, 16)
                sp.dma_start(sh_u[:, :, s * HS:(s + 1) * HS], swu[s].rearrange("(c p) h -> p c h", p=P)).then_inc(shg_in, 16)
            half = E // 2
            late = [(c, e0, i, w) for e0 in (0, half) for c in range(DC) for i, w in enumerate((wg, wu))]
            loads = 0

            def load_experts(n):
                nonlocal loads
                for c, e0, i, w in late[loads:loads + n]:
                    sp.dma_start(gate_up[:, c, e0:e0 + half, i * F:(i + 1) * F],
                                 w[e0:e0 + half, c * P:(c + 1) * P, :].rearrange("e p f -> p e f")).then_inc(gu_in, 16)
                loads += n

            for s in ORDER:
                if s[0] == "ctx_turn":
                    b = s[1]
                    if b >= 1:
                        sp.wait_ge(ctxt_ok, b)
                    sp.dma_start(ctx_sb, ctx[b].rearrange("(t p) c -> p t c", p=P)).then_inc(ctx_in, 16)
                if s[0] == "m_turn":
                    b = s[1]
                    sp.wait_ge(mt_ok, b + 1)
                    for r in range(3):
                        sp.dma_start(stacks[b % 2][96 + r:97 + r, 0, :, :], m_t[HEADS * r:HEADS * (r + 1), :]).then_inc(m_rows, 16)
                    load_experts(2)
                    if b == B - 1:
                        misc_wait(sp, ("v", B - 1))
                        for i in range(SH):
                            sp.dma_start(sh_d[:, i * (HS // P):(i + 1) * (HS // P), :],
                                         swd[i].rearrange("(j p) n -> p j n", p=P)).then_inc(shd_in, 16)
            sp.wait_ge(pv_done, B * NG)
            sp.wait_ge(ln1_ok, 2 * B)
            sp.dma_start(rows_dram[PAIRS:PAIRS + P, :], flat[:, :, :].rearrange("p t d -> p (t d)")[:, 0:ROW]).then_inc(tail_in, 16)
            for e0 in range(0, E, 16):
                sp.dma_start(down_w[:, e0:e0 + 16, :], wd[e0:e0 + 16].rearrange("e f n -> f e n")).then_inc(dw_in, 16)
            for i in range(ROW_SLOTS):
                sp.wait_ge(row_sent[i], 16 * NT * TOP // ROW_SLOTS)
            sp.wait_ge(tail_in, 16)
            sp.wait_ge(tiles_ok, 1)
            sp.wait_ge(down_done, NT)
            last = nc.sync.value_load(tile_i[0:1, 2 * MAX_TILES:2 * MAX_TILES + 1], min_val=7, max_val=MAX_TILES // 4 - 1)
            quads = last + 1

            def load_rows(q, j, i):
                first = nc.sync.value_load(tile_i[0:1, bass.ds(i + MAX_TILES, 1)], min_val=0, max_val=PAIRS)
                if not (isinstance(i, int) and i < 4):
                    sp.wait_ge(turned, i - 3)
                    sp.wait_ge(pair_here, i - 3)
                sp.dma_start(row_in[:, j, :], rows_dram[bass.ds(first, P), :]).then_inc(row_here[j], 16)

            for j in range(4):
                load_rows(0, j, j)
            with sp.Fori(1, quads) as q:
                for j in range(4):
                    load_rows(q, j, q * 4 + j)
            for j in range(4):
                sp.wait_ge(y_sent[j], quads * 16)
            for T in range(NT):
                sp.dma_start(y_back[:, T, :, :], y_dram[T * P * TOP:(T + 1) * P * TOP, :].rearrange("(p k) n -> p k n", k=TOP)) \
                    .then_inc(y_loaded[T], 16)
            for T in range(NT):
                sp.wait_ge(sum_ok, T + 1)
                b, t = divmod(T, TB)
                sp.dma_start(out[b, t * P:(t + 1) * P, :], xres[:, T, :]).then_inc(stored, 16)
            sp.wait_ge(stored, 16 * NT)

        @block.tensor
        def _(pe):
            def turn(dst, src, idm, s, last):
                ins = pe.transpose(dst, src, idm)
                if last:
                    ins.then_inc(full(s), 1)

            def turn_feat(s, src):
                b = misc_take(pe, s)
                for c in range(DC):
                    for t in range(TB):
                        turn(b[:, (c * TB + t) * P:(c * TB + t + 1) * P], src[:, t, c * P:(c + 1) * P], ident[:, :], s,
                             c == DC - 1 and t == TB - 1)

            pe.wait_ge(consts, 1)
            for s in ORDER:
                stage, a = s[0], s[1:]
                if stage == "x_weights":
                    pe.wait_ge(xw_in, 32)
                    b = misc_take(pe, s)
                    for i in range(2):
                        turn(b[:, i * P:(i + 1) * P], x_w[:, i, :], ident[:, :], s, i == 1)
                elif stage == "x_turn":
                    pe.wait_ge(ln1_ok, a[0] + 1)
                    turn_feat(s, flat[:, a[0] * TB:(a[0] + 1) * TB, :])
                elif stage == "qk":
                    k, t = a
                    if k == 0 and t == 0:
                        pe.wait_ge(qkv_in, 48)
                    pe.wait_ge(xt_ok, k + 1)
                    b = misc_take(pe, s)
                    for c in range(DC):
                        ins = pe.matmul(b[:, :], x_t[:, c, t * P:(t + 1) * P], w_qkv[:, c, 0:2 * D], start=c == 0, stop=c == DC - 1)
                    ins.then_inc(full(s), 1)
                elif stage == "v":
                    b = misc_take(pe, s)
                    for t in range(TB):
                        for c in range(DC):
                            ins = pe.matmul(b[:, t * D:(t + 1) * D], x_t[:, c, t * P:(t + 1) * P], w_qkv[:, c, 2 * D:3 * D],
                                            start=c == 0, stop=c == DC - 1)
                    ins.then_inc(full(s), 1)
                elif stage == "stack":
                    k, t, xx, half = a
                    pe.wait_ge(stk_ok, 2 * k + t + 1)
                    pe.wait_ge(stk3_ok, 2 * k + t + 1)
                    b = as_bf16(misc_take(pe, s))
                    for i in range(8):
                        ins = pe.transpose(b[0:PARTS * DK, i * P:(i + 1) * P],
                                           stk[t][:, xx, half * 8 + i, :, :].rearrange("p r d -> p (r d)"), ident_b[:, :])
                    ins.then_inc(full(s), 1)
                elif stage == "scores":
                    k, h = a
                    n = k * HEADS + h
                    if h == 0:
                        pe.wait_ge(stack_ok_d, 4 * (k + 1))
                        pe.wait_ge(stack_ok_a, 4 * (k + 1))
                    if n >= 2:
                        pe.wait_ge(scores_used, n - 1)
                    sq, b = stacks[k % 2], score_banks[n % 2]
                    R = PARTS * DK
                    pe.matmul(b[:, 0:2 * P], sq[0:R, 0, h, P:2 * P], sq[0:R, 1, h, :], start=True, stop=False, skip_group_check=True)
                    pe.matmul(b[:, 2 * P:3 * P], sq[0:R, 0, h, 0:P], sq[0:R, 1, h, 0:P], start=False, stop=False, skip_group_check=True)
                    pe.matmul(b[:, P:3 * P], ident_b[:, :], mask_b[:, :, :].rearrange("p a b -> p (a b)"),
                              start=False, stop=True, skip_group_check=True).then_inc(scores_full, 1)
                elif stage == "m_turn":
                    k, = a
                    pe.wait_ge(m_part_ok, k + 1)
                    b = as_bf16(misc_take(pe, s))
                    for t in range(TB):
                        turn(b[0:3 * HEADS, t * P:(t + 1) * P], m_part[:, t, :, :].rearrange("p r h -> p (r h)"), ident_b[:, :], s, t == 1)
                elif stage == "probs":
                    k, h = a
                    n = k * HEADS + h
                    if h == 0:
                        pe.wait_ge(m_rows, 48 * (k + 1))
                    if n >= 2:
                        pe.wait_ge(probs_used, n - 1)
                    sq, b = stacks[k % 2], prob_banks[n % 2]
                    R = PARTS * DK + 3
                    first, second = key_blocks(b[:, 0:3 * P], h)
                    pe.matmul(first, sq[0:R, 1, h, 0:P], sq[0:R, 0, h, :], start=True, stop=True, skip_group_check=True)
                    pe.matmul(second, sq[0:R, 1, h, P:2 * P], sq[0:R, 0, h, P:2 * P], start=False, stop=True,
                              skip_group_check=True).then_inc(probs_full, 1)
                elif stage == "pv":
                    k, g = a
                    pe.wait_ge(causal_ok, k * 8 + 2 * g + 2)
                    if g == 0:
                        pe.wait_ge(v_ok, k + 1)
                    b = misc_take(pe, s)
                    for j in range(4):
                        h = 4 * g + j
                        pe.matmul(b[32 * j:32 * j + 32, 0:2 * P], v_ones[k % 2][:, 0, h, :], key_blocks(pt[:, h % PT_SLOTS, :], h)[0],
                                  start=True, stop=False, skip_group_check=True)
                    for j in range(4):
                        h = 4 * g + j
                        ins = pe.matmul(b[32 * j:32 * j + 32, P:2 * P], v_ones[k % 2][:, 1, h, :], key_blocks(pt[:, h % PT_SLOTS, :], h)[1],
                                        start=False, stop=True, skip_group_check=True)
                    ins.then_inc(full(s), 1)
                elif stage == "o_back":
                    k, t = a
                    if t == 0:
                        pe.wait_ge(ot_ok, NG * (k + 1))
                    b = misc_take(pe, s)
                    for g in range(NG):
                        turn(b[:, g * P:(g + 1) * P], o_t[:, g, t * P:(t + 1) * P], ident[:, :], s, g == NG - 1)
                elif stage == "o_turn":
                    pe.wait_ge(tok_ok, 2 * a[0] + 1)
                    turn_feat(s, tok)
                elif stage == "wo":
                    k, = a
                    if k == 0:
                        pe.wait_ge(wo_in, 16)
                    pe.wait_ge(feat_ok, 2 * k + 1)
                    b = misc_take(pe, s)
                    for t in range(TB):
                        for c in range(DC):
                            ins = pe.matmul(b[:, t * D:(t + 1) * D], feat[:, c, t * P:(t + 1) * P], w_o[:, c, :], start=c == 0, stop=c == DC - 1)
                    ins.then_inc(full(s), 1)
                elif stage == "ln2_turn":
                    pe.wait_ge(tok_ok, 2 * a[0] + 2)
                    turn_feat(s, tok)
                elif stage == "ctx_turn":
                    k, = a
                    pe.wait_ge(ctx_in, 16 * (k + 1))
                    b = misc_take(pe, s)
                    for t in range(TB):
                        turn(b[:, t * P:(t + 1) * P], ctx_sb[:, t, :], ident[:, :], s, t == 1)
                elif stage == "ctx_qk":
                    k, = a
                    pe.wait_ge(ctxt_ok, k + 1)
                    if k == 0:
                        pe.wait_ge(xwt_ok, 1)
                    b = misc_take(pe, s)
                    for i in range(2):
                        ins = pe.matmul(b[:, i * S:(i + 1) * S], x_wt[:, i, :], ctx_t, start=True, stop=True)
                    ins.then_inc(full(s), 1)
                elif stage == "energy":
                    k, = a
                    pe.wait_ge(ctxqk_ok, k + 1)
                    b = misc_take(pe, s)
                    for t in range(TB):
                        ins = pe.matmul(b[:, t * S:(t + 1) * S], ctx_qk[:, 0, t * P:(t + 1) * P], ctx_qk[:, 1, :], start=True, stop=True)
                    ins.then_inc(full(s), 1)
                elif stage == "att_turn":
                    pe.wait_ge(att_ok, a[0] + 1)
                    turn_feat(s, att)
                elif stage == "xattn":
                    k, = a
                    pe.wait_ge(attt_ok, k + 1)
                    pe.wait_ge(feat_ok, 2 * k + 2)
                    b = misc_take(pe, s)
                    for t in range(TB):
                        for c in range(DC):
                            ins = pe.matmul(b[:, t * S:(t + 1) * S], feat[:, c, t * P:(t + 1) * P], att_t[:, k % 2, c, :],
                                            start=c == 0, stop=c == DC - 1)
                    ins.then_inc(full(s), 1)
                elif stage == "ln3_turn":
                    pe.wait_ge(ln1_ok, B + a[0] + 1)
                    turn_feat(s, flat[:, a[0] * TB:(a[0] + 1) * TB, :])
                elif stage == "router":
                    k, = a
                    if k == 0:
                        pe.wait_ge(r_in, 32)
                    pe.wait_ge(flatt_ok, k + 1)
                    b = misc_take(pe, s)
                    for t in range(TB):
                        T = k * TB + t
                        for c in range(DC):
                            ins = pe.matmul(b[:, t * E:(t + 1) * E], flat_t[:, c, T * P:(T + 1) * P], r_w[:, c, :], start=c == 0, stop=c == DC - 1)
                    ins.then_inc(full(s), 1)
                elif stage == "sh_up":
                    i, = a
                    tokens, j = divmod(i, HC)
                    if i == 0:
                        pe.wait_ge(shg_in, 16 * 2 * SH)
                        pe.wait_ge(scores_used, B * HEADS)
                        pe.wait_ge(probs_used, B * HEADS)
                    if i == HC:
                        pe.wait_ge(flatt_ok, B)
                    if i >= 2:
                        pe.wait_ge(hid_ok, i - 1)
                    bg, bu = (score_banks, prob_banks)[i % 2]
                    for b, w in ((bg, sh_g), (bu, sh_u)):
                        for c in range(DC):
                            ins = pe.matmul(b[:, :], w[:, c, j * P:(j + 1) * P], flat_t[:, c, tokens * 512:(tokens + 1) * 512],
                                            start=c == 0, stop=c == DC - 1)
                    ins.then_inc(up_full, 1)
                elif stage == "sh_down":
                    T, = a
                    if T == 0:
                        pe.wait_ge(shd_in, 16 * SH)
                    pe.wait_ge(hid_ok, HC * (T // 4 + 1))
                    b = misc_take(pe, s)
                    for j in range(HC):
                        ins = pe.matmul(b[:, 0:D], hid[:, j, (T % 4) * P:(T % 4 + 1) * P], sh_d[:, j, :], start=j == 0, stop=j == HC - 1)
                    ins.then_inc(full(s), 1)
                elif stage == "rank":
                    pe.wait_ge(chose_ok, B)
                    b = misc_take(pe, s)
                    for T in range(NT):
                        pe.matmul(b[:, T * E:(T + 1) * E], before_b[:, :], chose[:, T, :], start=T == 0, stop=False, skip_group_check=True)
                        for T2 in range(T):
                            ins = pe.matmul(b[:, T * E:(T + 1) * E], ones_b[:, :], chose[:, T2, :], start=False, stop=T2 == NT - 2,
                                            skip_group_check=True)
                    ins.then_inc(full(s), 1)
                elif stage == "starts":
                    b = misc_take(pe, s)
                    for T in range(NT):
                        ins = pe.matmul(b[0:E, 0:1], chose[:, T, :], ones_b[:, 0:1], start=T == 0, stop=T == NT - 1)
                    ins.then_inc(count_ok, 1)
                    pe.wait_ge(span_ok, 1)
                    pe.matmul(b[0:E, 0:1], upto[:, :], cnt[:, 1:2], start=True, stop=True)
                    pe.matmul(b[0:E, 1:2], before[:, :], cnt[:, 0:1], start=True, stop=True)
                    pe.matmul(b[:, 64:64 + E], wide[:, 0, :], before[:, :], start=True, stop=True).then_inc(full(s), 1)
                elif stage == "tiles":
                    pe.wait_ge(span_ok, 2)
                    b = misc_take(pe, s)
                    M = MAX_TILES
                    pe.matmul(b[:, 0:M], ones[0:E, :], in_tile[:, 0, :], start=True, stop=True)
                    pe.matmul(b[:, M:2 * M], wide[:, 1, :], in_tile[:, 1, :], start=True, stop=True)
                    pe.matmul(b[:, 2 * M:3 * M], wide[:, 2, :], in_tile[:, 1, :], start=True, stop=True)
                    pe.matmul(b[:, 3 * M:3 * M + 1], ones[0:E, :], cnt[:, 1:2], start=True, stop=True).then_inc(full(s), 1)

            pe.wait_ge(tiles_ok, 1)
            for i in range(MISC_BANKS):
                pe.wait_ge(misc_free[i], len([u for u in MISC.values() if u % MISC_BANKS == i]))
            pe.wait_ge(hid_ok, 2 * HC)
            pe.wait_ge(gu_in, 16 * 8)
            pe.wait_ge(dw_in, 16 * (E // 16))
            last = nc.tensor.value_load(tile_i[0:1, 2 * MAX_TILES:2 * MAX_TILES + 1], min_val=7, max_val=MAX_TILES // 4 - 1)
            quads = last + 1
            xt_b, gu_b, ht_b, y_b = score_banks, prob_banks, misc[0:2], misc[2:4]

            def expert_of(i):
                return nc.tensor.value_load(tile_i[0:1, bass.ds(i, 1)], min_val=0, max_val=E - 1)

            def turn_rows(q, j, i):
                pe.wait_ge(row_here[j], q * 16 + 16)
                if not isinstance(i, int) or i >= 2:
                    pe.wait_ge(xt_here, i - 1)
                pe.transpose(xt_b[j % 2][:, 0:P], row_in[:, j, 0:P], ident[:, :])
                pe.transpose(xt_b[j % 2][:, P:2 * P], row_in[:, j, P:2 * P], ident[:, :]).then_inc(turned, 1)

            def gate_and_up(j, i):
                e = expert_of(i)
                pe.wait_ge(xt_here, i + 1)
                if not isinstance(i, int) or i >= 2:
                    pe.wait_ge(h_here, i - 1)
                b = gu_b[j % 2]
                for c in range(DC):
                    ins = pe.matmul(b[:, 0:2 * F], xt_in[:, j % 2, c, :], gate_up[:, c, bass.ds(e, 1), :], start=c == 0, stop=c == DC - 1)
                ins.then_inc(gu_done, 1)

            def turn_h(j, i):
                dynamic = not isinstance(i, int)
                here, copied = (nc.tensor.to_reg(i + 1), nc.tensor.to_reg(i - 1)) if dynamic else (i + 1, i - 1)
                pe.wait_ge(tiles_ok, 1)
                pe.wait_ge(h_here, here)
                if dynamic or i >= 2:
                    pe.wait_ge(ht_here, copied)
                pe.transpose(ht_b[j % 2][0:F, 0:P], h_in[:, j % 2, :], ident[:, :]).then_inc(h_turned, 1)

            def down(j, i):
                e = expert_of(i)
                pe.wait_ge(ht_here, i + 1)
                if not isinstance(i, int) or i >= 2:
                    pe.wait_ge(y_here, i - 1)
                pe.matmul(y_b[j % 2][:, 0:D], ht_in[:, j % 2, :], down_w[:, bass.ds(e, 1), :], start=True, stop=True).then_inc(y_done, 1)

            for j in range(4):
                turn_rows(0, j, j)
                if j >= 1:
                    gate_and_up(j - 1, j - 1)
                if j >= 2:
                    turn_h(j - 2, j - 2)
                if j >= 3:
                    down(j - 3, j - 3)
            with pe.Fori(1, quads) as q:
                for j in range(4):
                    i = q * 4 + j
                    turn_rows(q, j, i)
                    gate_and_up(j + 3, i - 1)
                    turn_h(j + 2, i - 2)
                    down(j + 1, i - 3)
            end = last * 4
            gate_and_up(3, end + 3)
            turn_h(2, end + 2)
            down(1, end + 1)
            turn_h(3, end + 3)
            down(2, end + 2)
            down(3, end + 3)

        @block.scalar
        def _(eng):
            A = nc.scalar

            for s in ORDER:
                stage, a = s[0], s[1:]
                if stage == "x_weights":
                    b = misc_wait(eng, s)
                    A.copy(x_wt[:, :, :], b[:, 0:2 * C].rearrange("p (x c) -> p x c", x=2)).then_inc(xwt_ok, 1)
                    eng.wait_ge(xwt_ok, 1)
                    eng.sem_inc(free(s), 1)
                elif stage == "x_turn":
                    k, = a
                    b = misc_wait(eng, s)
                    if k >= 1:
                        misc_wait(eng, ("v", k - 1))
                    A.copy(x_t, b[:, :].rearrange("p (c t) -> p c t", c=DC)).then_inc(xt_ok, 1)
                    eng.wait_ge(xt_ok, k + 1)
                    eng.sem_inc(free(s), 1)
                elif stage == "qk":
                    k, t = a
                    b = misc_wait(eng, s)
                    n = 2 * k + t
                    if n >= 1:
                        eng.wait_ge(stk_ok, n)
                    A.copy(part1, b[:, :]).then_inc(part1_ok, 1)
                elif stage == "v":
                    k, = a
                    b = misc_wait(eng, s)
                    if k >= 2:
                        eng.wait_ge(pv_done, NG * (k - 1))
                    if k == 0:
                        eng.wait_ge(consts, 1)
                    A.copy(v_ones[k % 2][:, :, :, 0:DK], b[:, :].rearrange("p (t h d) -> p t h d", t=TB, h=HEADS)).then_inc(v_ok, 1)
                    eng.wait_ge(v_ok, k + 1)
                    eng.sem_inc(free(s), 1)
                elif stage == "stack":
                    k, t, xx, half = a
                    if half == 1:
                        b = as_bf16(misc_wait(eng, s))
                        if k >= 2:
                            eng.wait_ge(probs_full, HEADS * (k - 1))
                        A.copy(stacks[k % 2][0:PARTS * DK, xx, 8:16, t * P:(t + 1) * P],
                               b[0:PARTS * DK, :].rearrange("p (h t) -> p h t", h=8)).then_inc(stack_ok_a, 1)
                        eng.wait_ge(stack_ok_a, 4 * k + 2 * t + xx + 1)
                        eng.sem_inc(free(s), 1)
                elif stage == "m_turn":
                    k, = a
                    b = as_bf16(misc_wait(eng, s))
                    if k >= 1:
                        eng.wait_ge(m_rows, 48 * k)
                    A.copy(m_t[:, :], b[0:3 * HEADS, 0:S]).then_inc(mt_ok, 1)
                    eng.wait_ge(mt_ok, k + 1)
                    eng.sem_inc(free(s), 1)
                elif stage == "probs":
                    k, h = a
                    n = k * HEADS + h
                    eng.wait_ge(probs_full, n + 1)
                    if n >= PT_SLOTS:
                        eng.wait_ge(pv_done, (n - PT_SLOTS) // 4 + 1)
                    A.activation(pt[:, h % PT_SLOTS, :], prob_banks[n % 2][:, 0:3 * P], ACT.Exp, scale=SCALE).then_inc(probs_used, 1)
                elif stage == "pv":
                    k, g = a
                    b = misc_wait(eng, s)
                    eng.sem_inc(pv_done, 1)
                    if g == 0 and k >= 1:
                        misc_wait(eng, ("o_back", k - 1, 1))
                    A.copy(o_t[:, g, :], b[:, 0:S]).then_inc(ot_ok, 1)
                    eng.wait_ge(ot_ok, NG * k + g + 1)
                    eng.sem_inc(free(s), 1)
                elif stage in ("o_turn", "ln2_turn"):
                    k, = a
                    b = misc_wait(eng, s)
                    n = 2 * k + (stage == "ln2_turn") + 1
                    if n >= 2:
                        misc_wait(eng, ("wo", k) if stage == "ln2_turn" else ("xattn", k - 1))
                    A.copy(feat[:, :, :], b[:, :].rearrange("p (c t) -> p c t", c=DC)).then_inc(feat_ok, 1)
                    eng.wait_ge(feat_ok, n)
                    eng.sem_inc(free(s), 1)
                elif stage == "ctx_turn":
                    k, = a
                    b = misc_wait(eng, s)
                    if k >= 1:
                        misc_wait(eng, ("ctx_qk", k - 1))
                    A.copy(ctx_t, b[:, 0:S]).then_inc(ctxt_ok, 1)
                    eng.wait_ge(ctxt_ok, k + 1)
                    eng.sem_inc(free(s), 1)
                elif stage == "ctx_qk":
                    k, = a
                    if k == 0:
                        eng.wait_ge(xb_in, 32)
                    b = misc_wait(eng, s)
                    if k >= 1:
                        misc_wait(eng, ("energy", k - 1))
                    A.activation(ctx_qk[:, 0, :], b[:, 0:S], ACT.Identity, bias=x_bias[:, 0:1])
                    A.activation(ctx_qk[:, 1, :], b[:, S:2 * S], ACT.Identity, bias=x_bias[:, 1:2]).then_inc(ctxqk_ok, 1)
                    eng.wait_ge(ctxqk_ok, k + 1)
                    eng.sem_inc(free(s), 1)
                elif stage == "energy":
                    k, = a
                    eng.wait_ge(emax_ok, k + 1)
                    b = misc_wait(eng, s)
                    if k >= 1:
                        misc_wait(eng, ("att_turn", k - 1))
                    for t in range(TB):
                        ins = A.activation(att[:, t, :], b[:, t * S:(t + 1) * S], ACT.Exp, bias=e_max[:, 2 + t:3 + t],
                                           accum_out=e_sum[:, t:t + 1])
                    ins.then_inc(esum_ok, 1)
                    eng.wait_ge(esum_ok, k + 1)
                    eng.sem_inc(free(s), 1)
                elif stage == "att_turn":
                    k, = a
                    b = misc_wait(eng, s)
                    if k >= 2:
                        misc_wait(eng, ("xattn", k - 2))
                    A.copy(att_t[:, k % 2, :, :], b[:, :].rearrange("p (c m) -> p c m", c=DC)).then_inc(attt_ok, 1)
                    eng.wait_ge(attt_ok, k + 1)
                    eng.sem_inc(free(s), 1)
                elif stage == "ln3_turn":
                    k, = a
                    b = misc_wait(eng, s)
                    A.copy(flat_t[:, :, k * S:(k + 1) * S], b[:, :].rearrange("p (c t) -> p c t", c=DC)).then_inc(flatt_ok, 1)
                    eng.wait_ge(flatt_ok, k + 1)
                    eng.sem_inc(free(s), 1)
                elif stage == "router":
                    k, = a
                    eng.wait_ge(logits_ok, k + 1)
                    if k >= 1:
                        eng.wait_ge(chose_ok, k)
                    for t in range(TB):
                        ins = A.activation(expd[:, t, :], logits[:, t, :], ACT.Exp, bias=r_max[:, t:t + 1], accum_out=r_sum[:, t:t + 1])
                    ins.then_inc(expd_ok, 1)
                elif stage == "sh_up":
                    i, = a
                    eng.wait_ge(up_full, i + 1)
                    if i >= 2:
                        eng.wait_ge(hid_ok, i - 1)
                    b = (score_banks, prob_banks)[i % 2][0]
                    A.activation(sil[:, i % 2, :], b[:, :], ACT.Silu).then_inc(sil_ok, 1)
            eng.wait_ge(info_ok, B)
            misc_wait(eng, ("xattn", B - 1))
            for n in range(NT * TOP):
                T, slot = n // TOP, n % ROW_SLOTS
                if n >= ROW_SLOTS:
                    eng.wait_ge(row_sent[slot], 16 * (n // ROW_SLOTS))
                A.copy(row_out[:, slot, 0:D], flat[:, T, :])
                A.copy(row_out[:, slot, D:ROW], pair_info[:, n, :]).then_inc(rows_filled, 1)
            eng.wait_ge(tiles_ok, 1)
            last = nc.scalar.value_load(tile_i[0:1, 2 * MAX_TILES:2 * MAX_TILES + 1], min_val=7, max_val=MAX_TILES // 4 - 1)
            quads = last + 1
            gu_b, y_b = prob_banks, misc[2:4]

            def silu(j, i):
                eng.wait_ge(gu_done, i + 1)
                if not isinstance(i, int) or i >= 2:
                    eng.wait_ge(h_here, i - 1)
                A.activation(sil_in[:, j % 2, :], gu_b[j % 2][:, 0:F], ACT.Silu).then_inc(sil_here, 1)

            def weigh(q, j, i):
                eng.wait_ge(y_done, i + 1)
                if not isinstance(i, int) or i >= 4:
                    eng.wait_ge(y_sent[j], q * 16)
                A.activation(y_out[:, j, :], y_b[j % 2][:, 0:D], ACT.Copy, scale=pair_w[:, j:j + 1]).then_inc(y_here, 1)

            def step(q, j):
                silu((j + 3) % 4, q * 4 + j - 1)
                weigh(q - 1 if j < 3 else q, (j + 1) % 4, q * 4 + j - 3)

            for j in range(1, 4):
                silu(j - 1, j - 1)
            weigh(0, 0, 0)
            for j in range(4):
                step(1, j)
            with eng.Fori(2, quads) as q:
                for j in range(4):
                    step(q, j)
            end = last * 4
            silu(3, end + 3)
            weigh(last, 1, end + 1)
            weigh(last, 2, end + 2)
            weigh(last, 3, end + 3)

        @block.vector
        def _(eng):
            V = nc.vector
            steps = [0]

            def then(ins):
                steps[0] += 1
                ins.then_inc(dve, 1)
                eng.wait_ge(dve, steps[0])

            def stats(k, b_):
                for t in range(TB):
                    ins = V.bn_stats(bn[:, t, :], xres[:, b_ * TB + t, :])
                then(ins)
                for t in range(TB):
                    ins = V.bn_aggr(mv[:, t, :], bn[:, t, :])
                then(ins)
                V.tensor_scalar(mv[:, :, 1], mv[:, :, 1], EPS, None, ALU.add).then_inc(var_ok, 1)

            norm = [0]

            def apply(b_, dst, done):
                norm[0] += 1
                eng.wait_ge(rstd_ok, norm[0])
                for t in range(TB):
                    ins = V.tensor_scalar(dst[:, t, :], xres[:, b_ * TB + t, :], mv[:, t, 0:1], rstd[:, t:t + 1],
                                          ALU.subtract, ALU.mult)
                ins.then_inc(done, 1)

            res = [0]
            for s in ORDER:
                stage, a = s[0], s[1:]
                if stage in ("ln1_stats", "ln2_stats", "ln3_stats"):
                    k, = a
                    if stage == "ln1_stats":
                        eng.wait_ge(x_in[k], 16)
                    stats(stage, k)
                elif stage == "ln1_apply":
                    k, = a
                    apply(k, flat[:, k * TB:(k + 1) * TB, :], ln1_ok)
                elif stage == "ln2_apply":
                    apply(a[0], tok, tok_ok)
                elif stage == "ln3_apply":
                    k, = a
                    apply(k, flat[:, k * TB:(k + 1) * TB, :], ln1_ok)
                elif stage == "qk":
                    k, t = a
                    n = 2 * k + t
                    eng.wait_ge(part1_ok, n + 1)
                    b = misc_wait(eng, s)
                    if n >= 1:
                        eng.wait_ge(stk3_ok, n)
                    V.tensor_tensor(rest, b[:, :], part1, ALU.subtract).then_inc(rest_ok, 1)
                    eng.wait_ge(rest_ok, n + 1)
                    eng.sem_inc(free(s), 1)
                    V.tensor_copy(part2, rest).then_inc(part2_ok, 1)
                    if k >= 1:
                        misc_wait(eng, ("stack", k - 1, t, 1, 1))
                    p1 = part1.rearrange("p (x h d) -> p x h d", x=2, h=HEADS)
                    p2 = part2.rearrange("p (x h d) -> p x h d", x=2, h=HEADS)
                    q_, k_ = stk[t][:, 0], stk[t][:, 1]
                    for r in range(3):
                        V.tensor_copy(q_[:, :, r, :], p1[:, 0])
                    for r in (0, 3, 5):
                        V.tensor_copy(k_[:, :, r, :], p1[:, 1])
                    eng.wait_ge(part2_ok, n + 1)
                    for r in (3, 4):
                        V.tensor_copy(q_[:, :, r, :], p2[:, 0])
                    for r in (1, 4):
                        ins = V.tensor_copy(k_[:, :, r, :], p2[:, 1])
                    ins.then_inc(stk_ok, 1)
                elif stage == "stack":
                    k, t, xx, half = a
                    if half == 0:
                        b = as_bf16(misc_wait(eng, s))
                        if k >= 2:
                            eng.wait_ge(probs_full, HEADS * (k - 1))
                        V.tensor_copy(stacks[k % 2][0:PARTS * DK, xx, 0:8, t * P:(t + 1) * P],
                                      b[0:PARTS * DK, :].rearrange("p (h t) -> p h t", h=8)).then_inc(stack_ok_d, 1)
                        eng.wait_ge(stack_ok_d, 4 * k + 2 * t + xx + 1)
                        eng.sem_inc(free(s), 1)
                elif stage == "scores":
                    k, h = a
                    n = k * HEADS + h
                    eng.wait_ge(scores_full, n + 1)
                    V.reduce_max(m_raw[:, h, :], score_banks[n % 2][:, 0:3 * P].rearrange("p (a b) -> p a b", a=3), AX.X) \
                        .then_inc(scores_used, 1)
                elif stage == "m_parts":
                    k, = a
                    eng.wait_ge(scores_used, HEADS * (k + 1))
                    if k >= 1:
                        misc_wait(eng, ("m_turn", k - 1))
                    V.tensor_scalar(m_neg[:, 0, :], m_raw[:, :, 2], -1.0, None, ALU.mult)
                    then(V.tensor_tensor(m_neg[:, 1, :], m_raw[:, :, 0], m_raw[:, :, 1], ALU.max))
                    then(V.tensor_scalar(m_neg[:, 1, :], m_neg[:, 1, :], -1.0, None, ALU.mult))
                    then(V.tensor_copy(m_part[:, :, 0, :], m_neg[:, :, :]))
                    then(V.tensor_tensor(m_rest[:, :, :], m_neg[:, :, :], m_part[:, :, 0, :], ALU.subtract))
                    then(V.tensor_copy(m_part[:, :, 1, :], m_rest[:, :, :]))
                    V.tensor_tensor(m_part[:, :, 2, :], m_rest[:, :, :], m_part[:, :, 1, :], ALU.subtract).then_inc(m_part_ok, 1)
                elif stage == "o_back":
                    k, t = a
                    b = misc_wait(eng, s)
                    heads = b[:, :].rearrange("p (h j) -> p h j", j=32)
                    if t == 0 and k >= 1:
                        misc_wait(eng, ("ln2_turn", k - 1))
                    then(V.reciprocal(o_rec[:, :], heads[:, :, DK]))
                    ins = V.tensor_tensor(tok[:, t, :].rearrange("p (h d) -> p h d", h=HEADS), heads[:, :, 0:DK],
                                          o_rec[:, :].unsqueeze(2).to_broadcast([P, HEADS, DK]), ALU.mult)
                    then(ins)
                    eng.sem_inc(free(s), 1)
                    if t == 1:
                        eng.sem_inc(tok_ok, 1)
                elif stage in ("wo", "xattn"):
                    k, = a
                    b = misc_wait(eng, s)
                    xs = xres[:, k * TB:(k + 1) * TB, :]
                    then(V.tensor_tensor(xs, b[:, :].rearrange("p (t n) -> p t n", t=TB), xs, ALU.add))
                    eng.sem_inc(free(s), 1)
                elif stage == "energy":
                    k, = a
                    b = misc_wait(eng, s)
                    then(V.reduce_max(e_max[:, 0:2], b[:, :].rearrange("p (t n) -> p t n", t=TB), AX.X))
                    V.tensor_scalar(e_max[:, 2:4], e_max[:, 0:2], -1.0, None, ALU.mult).then_inc(emax_ok, 1)
                elif stage == "att_turn":
                    k, = a
                    eng.wait_ge(esum_ok, k + 1)
                    then(V.reciprocal(e_sum[:, 2:4], e_sum[:, 0:2]))
                    for t in range(TB):
                        ins = V.tensor_scalar(att[:, t, :], att[:, t, :], e_sum[:, 2 + t:3 + t], None, ALU.mult)
                    ins.then_inc(att_ok, 1)
                elif stage == "router":
                    k, = a
                    b = misc_wait(eng, s)
                    if k == 0:
                        eng.wait_ge(r_in, 32)
                    then(V.tensor_copy(logits[:, :, :], b[:, 0:TB * E].rearrange("p (t e) -> p t e", t=TB)))
                    eng.sem_inc(free(s), 1)
                    then(V.reduce_max(r_max[:, :], logits[:, :, :], AX.X))
                    V.tensor_scalar(r_max[:, :], r_max[:, :], -1.0, None, ALU.mult).then_inc(logits_ok, 1)
                    then(V.tensor_tensor(biased[:, :, :], logits[:, :, :], r_bias[:, :].unsqueeze(1).to_broadcast([P, TB, E]), ALU.add))
                    for t in range(TB):
                        ins = V.max(top8[:, t, :], biased[:, t, :])
                    then(ins)
                    for t in range(TB):
                        ins = V.max_index(top_i[:, t, :], top8[:, t, :], biased[:, t, :])
                    then(ins)
                    then(V.tensor_copy(top_f[:, :, :], top_i[:, :, :]))
                elif stage == "choose":
                    k, = a
                    T0 = k * TB
                    eng.wait_ge(iota_ok, 1)
                    for t in range(TB):
                        ins = V.tensor_tensor(chosen[:, T0 + t, :, :], iota_e[:, :].unsqueeze(1).to_broadcast([P, TOP, E]),
                                              top_f[:, t, 0:TOP].unsqueeze(2).to_broadcast([P, TOP, E]), ALU.is_equal)
                    then(ins)
                    for t in range(TB):
                        with nc.allow_low_precision(reason="sums of at most four ones"):
                            V.reduce_sum(chose[:, T0 + t, :], chosen[:, T0 + t, :, :].rearrange("p k e -> p e k"), AX.X)
                    eng.wait_ge(expd_ok, k + 1)
                    misc_wait(eng, ("ln2_turn", k))
                    for t in range(TB):
                        ins = V.tensor_tensor(prod[:, t], chosen[:, T0 + t, :, :], expd[:, t, :].unsqueeze(1).to_broadcast([P, TOP, E]), ALU.mult)
                    then(ins)
                    V.reduce_sum(top_s[:, :, :], prod, AX.X)
                    then(V.reciprocal(r_sum[:, :], r_sum[:, :]))
                    then(V.tensor_tensor(top_s[:, :, :], top_s[:, :, :], r_sum[:, :].unsqueeze(2).to_broadcast([P, TB, TOP]), ALU.mult))
                    then(V.reduce_sum(top_sum[:, :], top_s[:, :, :], AX.X))
                    then(V.reciprocal(top_sum[:, :], top_sum[:, :]))
                    then(V.tensor_tensor(pair_info[:, T0 * TOP:(T0 + TB) * TOP, 1].rearrange("p (t k) -> p t k", t=TB), top_s[:, :, :],
                                         top_sum[:, :].unsqueeze(2).to_broadcast([P, TB, TOP]), ALU.mult))
                    eng.sem_inc(chose_ok, 1)
                    eng.sem_inc(info_ok, 1)
                elif stage == "sh_up":
                    i, = a
                    tokens, j = divmod(i, HC)
                    eng.wait_ge(sil_ok, i + 1)
                    if i == HC:
                        misc_wait(eng, ("sh_down", 3))
                    b = (score_banks, prob_banks)[i % 2][1]
                    V.tensor_tensor(hid[:, j, :], b[:, :], sil[:, i % 2, :], ALU.mult).then_inc(hid_ok, 1)
                elif stage == "sh_down":
                    T, = a
                    b = misc_wait(eng, s)
                    then(V.tensor_tensor(xres[:, T, :], b[:, 0:D], xres[:, T, :], ALU.add))
                    eng.sem_inc(free(s), 1)
                    eng.sem_inc(down_done, 1)
                elif stage == "rank":
                    b = misc_wait(eng, s)
                    then(V.tensor_copy(rank_sb[:, :, :], b[:, :].rearrange("p (t e) -> p t e", t=NT)))
                    eng.sem_inc(free(s), 1)
                elif stage == "starts":
                    bi = MISC[s] % MISC_BANKS
                    b = misc[bi]
                    eng.wait_ge(count_ok, 1)
                    then(V.tensor_copy(cnt[:, 0:1], b[0:E, 0:1]))
                    then(V.tensor_scalar(cnt_i[:, :], cnt[:, 0:1], float(P - 1), None, ALU.add))
                    then(V.tensor_scalar(cnt_i[:, :], cnt_i[:, :], P.bit_length() - 1, None, ALU.arith_shift_right))
                    V.tensor_copy(cnt[:, 1:2], cnt_i[:, :])
                    then(V.tensor_scalar(wide[:, 0, :], ones[0:E, :], cnt[:, 0:1], None, ALU.mult))
                    eng.sem_inc(span_ok, 1)
                    misc_wait(eng, s)
                    then(V.tensor_copy(cnt[:, 2:4], b[0:E, 0:2]))
                    then(V.tensor_tensor(rank_sb[:, :, :], rank_sb[:, :, :],
                                         b[:, 64:64 + E].unsqueeze(1).to_broadcast([P, NT, E]), ALU.add))
                    eng.sem_inc(free(s), 1)
                    then(V.tensor_tensor(cnt[:, 4:5], cnt[:, 2:3], cnt[:, 1:2], ALU.subtract))
                    then(V.tensor_scalar(cnt[:, 5:6], cnt[:, 4:5], float(P), None, ALU.mult))
                    V.tensor_tensor(cnt[:, 6:7], cnt[:, 3:4], cnt[:, 5:6], ALU.subtract)
                    then(V.tensor_tensor(cnt[:, 7:8], cnt[:, 0:1], cnt[:, 5:6], ALU.add))
                    for i in range(2):
                        V.tensor_scalar(wide[:, 1 + i, :], ones[0:E, :], cnt[:, 6 + i:7 + i], None, ALU.mult)
                    V.tensor_scalar(in_tile[:, 0, :], iota_t[0:E, :], cnt[:, 2:3], None, ALU.is_ge)
                    then(V.tensor_scalar(in_tile[:, 1, :], iota_t[0:E, :], cnt[:, 4:5], None, ALU.is_ge))
                    then(V.tensor_tensor(in_tile[:, 1, :], in_tile[:, 1, :], in_tile[:, 0, :], ALU.subtract))
                    eng.sem_inc(span_ok, 1)
                elif stage == "tiles":
                    M = MAX_TILES
                    b = misc_wait(eng, s)
                    V.tensor_scalar(tile_i[:, 0:M], b[:, 0:M], float(E - 1), None, ALU.min)
                    V.scalar_tensor_tensor(out=tile_f[:, 0, :], in0=iota_t[:, :], scalar=float(P), in1=b[:, M:2 * M], op0=ALU.mult, op1=ALU.add)
                    V.scalar_tensor_tensor(out=tile_f[:, 1, :], in0=iota_t[:, :], scalar=-float(P), in1=b[:, 2 * M:3 * M], op0=ALU.mult, op1=ALU.add)
                    then(V.tensor_scalar(cnt_q[:, :], b[:, 3 * M:3 * M + 1], -1.0, None, ALU.add))
                    eng.sem_inc(free(s), 1)
                    V.tensor_scalar(tile_i[:, 2 * M:2 * M + 1], cnt_q[:, :], 2, None, ALU.arith_shift_right)
                    V.tensor_scalar(tile_i[:, M:2 * M], tile_f[:, 0, :], float(PAIRS), None, ALU.min)
                    then(V.tensor_scalar(penalty[:, :], tile_f[:, 1, :], iota_p[:, 0:1], float(SKIPPED), ALU.is_le, ALU.mult))
                    eng.sem_inc(tiles_ok, 1)
                elif stage == "positions":
                    for T in range(NT):
                        buf = prod[:, T % 2]
                        if T >= 2:
                            eng.wait_ge(dve, steps[0])
                        then(V.tensor_tensor(buf, chosen[:, T, :, :], rank_sb[:, T, :].unsqueeze(1).to_broadcast([P, TOP, E]), ALU.mult))
                        ins = V.reduce_sum(pos_f[:, T * TOP:(T + 1) * TOP], buf, AX.X)
                        if T == NT - 1:
                            then(ins)
                    V.tensor_copy(pos_i[:, :], pos_f[:, :]).then_inc(pos_ok, 1)
            xt_b, gu_b, ht_b = score_banks, prob_banks, misc[0:2]
            last = nc.vector.value_load(tile_i[0:1, 2 * MAX_TILES:2 * MAX_TILES + 1], min_val=7, max_val=MAX_TILES // 4 - 1)
            quads = last + 1

            def take_rows(q, j, i):
                eng.wait_ge(row_here[j], q * 16 + 16)
                if not isinstance(i, int) or i >= 4:
                    eng.wait_ge(y_sent[j], q * 16)
                V.tensor_copy(pair_w[:, j:j + 1], row_in[:, j, D + 1:D + 2])
                V.tensor_tensor(pair_i[:, j:j + 1], row_in[:, j, D:D + 1], penalty[:, bass.ds(i, 1)], ALU.add).then_inc(pair_here, 1)

            def keep_turned(j, i):
                eng.wait_ge(turned, i + 1)
                if not isinstance(i, int) or i >= 2:
                    eng.wait_ge(gu_done, i - 1)
                V.tensor_copy(xt_in[:, j % 2, :, :], xt_b[j % 2][:, 0:2 * P].rearrange("p (c t) -> p c t", c=DC)).then_inc(xt_here, 1)

            def hidden(j, i):
                eng.wait_ge(sil_here, i + 1)
                if not isinstance(i, int) or i >= 2:
                    eng.wait_ge(h_turned, i - 1)
                V.tensor_tensor(h_in[:, j % 2, :], gu_b[j % 2][:, F:2 * F], sil_in[:, j % 2, :], ALU.mult).then_inc(h_here, 1)

            def keep_h(j, i):
                eng.wait_ge(h_turned, i + 1)
                if not isinstance(i, int) or i >= 2:
                    eng.wait_ge(y_done, i - 1)
                V.tensor_copy(ht_in[:, j % 2, :], ht_b[j % 2][0:F, 0:P]).then_inc(ht_here, 1)

            for j in range(4):
                keep_turned(j, j)
                take_rows(0, j, j)
                if j >= 1:
                    hidden(j - 1, j - 1)
                if j >= 2:
                    keep_h(j - 2, j - 2)
            with eng.Fori(1, quads) as q:
                for j in range(4):
                    i = q * 4 + j
                    keep_turned(j, i)
                    take_rows(q, j, i)
                    hidden(j + 3, i - 1)
                    keep_h(j + 2, i - 2)
            end = last * 4
            hidden(3, end + 3)
            keep_h(2, end + 2)
            keep_h(3, end + 3)
            for T in range(NT):
                eng.wait_ge(y_loaded[T], 16)
                then(V.tensor_tensor(y_back[:, T, 0:2, :], y_back[:, T, 0:2, :], y_back[:, T, 2:4, :], ALU.add))
                then(V.tensor_tensor(y_back[:, T, 0, :], y_back[:, T, 0, :], y_back[:, T, 1, :], ALU.add))
                V.tensor_tensor(xres[:, T, :], xres[:, T, :], y_back[:, T, 0, :], ALU.add).then_inc(sum_ok, 1)

        @block.gpsimd
        def _(eng):
            G = nc.gpsimd
            steps = [0]

            def then(ins):
                steps[0] += 1
                ins.then_inc(pool, 1)
                eng.wait_ge(pool, steps[0])

            G.memset(ident[:, :], 0.0)
            G.memset(mask_b[:, :, :], 0.0)
            G.memset(ones[:, :], 1.0)
            G.memset(ones_b[:, :], 1.0)
            G.memset(neg_half[:, :], -0.5)
            for v in v_ones:
                then(G.memset(v[:, :, :, DK:32], 1.0))
            for st in stacks:
                then(G.memset(st[96:99, 1, :, :], 1.0))
            then(G.memset(iota_p[:, :], 0.0))
            G.affine_select(out=ident[:, :], in_=ident[:, :], pattern=[[-1, P]], compare_op=ALU.not_equal, fill=1.0, base=0, channel_multiplier=1)
            G.affine_select(out=mask_b[:, :, :], in_=mask_b[:, :, :], pattern=[[0, 2], [-1, P]], compare_op=ALU.is_ge, fill=MASKED, base=0,
                            channel_multiplier=1)
            then(G.affine_select(out=before_b[:, :], in_=ones_b[:, :], pattern=[[1, P]], compare_op=ALU.is_gt, fill=0.0, base=0,
                                 channel_multiplier=-1))
            G.affine_select(out=before[:, :], in_=ones[0:E, 0:E], pattern=[[1, E]], compare_op=ALU.is_gt, fill=0.0, base=0, channel_multiplier=-1)
            then(G.affine_select(out=upto[:, :], in_=ones[0:E, 0:E], pattern=[[1, E]], compare_op=ALU.is_ge, fill=0.0, base=0,
                                 channel_multiplier=-1))
            then(G.tensor_copy(ident_b[:, :], ident[:, :]))
            eng.sem_inc(consts, 1)

            def iotas():
                G.iota(iota_e[:, :], pattern=[[1, E]], base=0, channel_multiplier=0, allow_small_or_imprecise_dtypes=True)
                G.iota(iota_t[:, :], pattern=[[1, MAX_TILES]], base=0, channel_multiplier=0, allow_small_or_imprecise_dtypes=True)
                G.iota(iota_p[:, :], pattern=[[0, 1]], base=0, channel_multiplier=1, allow_small_or_imprecise_dtypes=True)
                then(G.iota(pair_info[:, :, 0].rearrange("p (t k) -> p t k", t=NT), pattern=[[P * TOP, NT], [1, TOP]], base=0,
                            channel_multiplier=TOP, allow_small_or_imprecise_dtypes=True))
                eng.sem_inc(iota_ok, 1)

            norm = 0
            for s in ORDER:
                stage, a = s[0], s[1:]
                if stage in ("ln1_stats", "ln2_stats", "ln3_stats"):
                    norm += 1
                    eng.wait_ge(var_ok, norm)
                    G.tensor_tensor(rstd[:, :], mv[:, :, 1], neg_half[:, :], ALU.pow).then_inc(rstd_ok, 1)
                    if norm == 1:
                        iotas()
                elif stage == "qk":
                    k, t = a
                    n = 2 * k + t
                    eng.wait_ge(part2_ok, n + 1)
                    if k >= 1:
                        misc_wait(eng, ("stack", k - 1, t, 1, 1))
                    r_ = rest.rearrange("p (x h d) -> p x h d", x=2, h=HEADS)
                    p2 = part2.rearrange("p (x h d) -> p x h d", x=2, h=HEADS)
                    G.tensor_tensor(stk[t][:, 0, :, 5, :], r_[:, 0], p2[:, 0], ALU.subtract)
                    G.tensor_tensor(stk[t][:, 1, :, 2, :], r_[:, 1], p2[:, 1], ALU.subtract).then_inc(stk3_ok, 1)
                elif stage == "causal":
                    k, i = a
                    eng.wait_ge(probs_used, k * HEADS + 2 * i + 2)
                    lo = (2 * i) % PT_SLOTS
                    v = pt[:, lo:lo + 2, :].rearrange("p s c -> p (s c)")[:, P:5 * P].rearrange("p (a c) -> p a c", a=4)
                    G.affine_select(out=v, in_=v, pattern=[[0, 4], [1, P]], compare_op=ALU.is_ge, fill=0.0, base=0,
                                    channel_multiplier=-1).then_inc(causal_ok, 1)
            eng.wait_ge(pos_ok, 1)
            for n in range(NT * TOP):
                slot = n % ROW_SLOTS
                eng.wait_ge(rows_filled, n + 1)
                G.indirect_dma_start(rows_dram, bass.IndirectOffsetOnAxis(pos_i[:, n:n + 1], 0), row_out[:, slot, :], None) \
                    .then_inc(row_sent[slot], 16)
            last = nc.gpsimd.value_load(tile_i[0:1, 2 * MAX_TILES:2 * MAX_TILES + 1], min_val=7, max_val=MAX_TILES // 4 - 1)
            quads = last + 1

            bound = nc.gpsimd.to_reg(PAIRS - 1)

            def send(j, i):
                here = i + 1 if isinstance(i, int) else nc.gpsimd.to_reg(i + 1)
                eng.wait_ge(pos_ok, 1)
                eng.wait_ge(y_here, here)
                G.indirect_dma_start(y_dram, bass.IndirectOffsetOnAxis(pair_i[:, j:j + 1], 0), y_out[:, j, :], None,
                                     bounds_check=bound, oob_is_err=False).then_inc(y_sent[j], 16)

            for j in range(4):
                send(j, j)
            with eng.Fori(1, quads) as q:
                for j in range(4):
                    send(j, q * 4 + j)


_INS = ['x', 'ctx_1024', 'L0_attn_Wq', 'L0_attn_Wk', 'L0_attn_Wv', 'L0_attn_Wo', 'L0_xattn_Wq', 'L0_xattn_bq', 'L0_xattn_Wk',
        'L0_xattn_bk', 'L0_ffn_router_w', 'L0_ffn_router_bias', 'L0_ffn_wg', 'L0_ffn_wu', 'L0_ffn_wd', 'L0_ffn_swg', 'L0_ffn_swu',
        'L0_ffn_swd']


def kernel(**inputs):
    import numpy as np
    import concourse.bacc as bacc
    from concourse.bass_utils import run_bass_kernel_spmd

    nc = bacc.Bacc("TRN2", target_bir_lowering=False, num_devices=1)
    arrays, args = {}, []
    for name in _INS:
        a = np.ascontiguousarray(inputs[name])
        arrays[f"in_{name}"] = a
        args.append(nc.dram_tensor(f"in_{name}", a.shape, mybir.dt.from_np(a.dtype), kind="ExternalInput").ap())
    args.append(nc.dram_tensor("out_0", arrays["in_x"].shape, F32, kind="ExternalOutput").ap())
    decoder_layer(nc, *args)
    r = run_bass_kernel_spmd(nc, [arrays], core_ids=[0])
    return r.results[0]["out_0"]
```

```python
from contextlib import ExitStack

import concourse.bass as bass
from concourse import mybir

P = 128
ALU = mybir.AluOpType
ACT = mybir.ActivationFunctionType
F32 = mybir.dt.float32
BF16 = mybir.dt.bfloat16
I32 = mybir.dt.int32
U32 = mybir.dt.uint32
AX = mybir.AxisListType

HEADS = 16
EPS = 1e-5
TOP = 4
MASKED = -1e30
PARTS = 6
MISC_BANKS = 4
GROUP = 8
Y_SLOTS = 4
PT_SLOTS = 8
ROW_SLOTS = TOP
SKIPPED = 8192


def stage_order(batches):
    last = batches - 1
    order = [("ln1_stats", 0), ("ln1_apply", 0), ("x_turn", 0), ("qk", 0, 0), ("stack_parts", 0, 0), ("qk", 0, 1), ("stack_parts", 0, 1),
             ("x_weights",)]
    for k in range(batches + 1):
        if k >= 1:
            order.append(("m_turn", k - 1))
        if k >= 2:
            order += [("o_back", k - 2, 0), ("o_back", k - 2, 1)]
        if k <= last:
            order += [("stack", k, t, x, half) for t in range(2) for x in range(2) for half in range(2)]
            order.append(("v", k))
        fill = {h: [] for h in range(HEADS)}

        def at(h, *stages):
            fill[h] += stages

        if k >= 2:
            at(0, ("o_turn", k - 2))
        if k < last:
            at(0, ("ln1_stats", k + 1))
        if 1 <= k <= last + 1:
            at(1, ("ctx_turn", k - 1))
        if k >= 2:
            at(2, ("wo", k - 2), ("ln2_stats", k - 2))
        if k < last:
            at(2, ("ln1_apply", k + 1))
        if 1 <= k <= last + 1:
            at(3, ("ctx_qk", k - 1))
        if k < last:
            at(4, ("x_turn", k + 1))
        if k >= 2:
            at(5, ("ln2_apply", k - 2))
            at(6, ("ln2_turn", k - 2))
        if k < last:
            at(6, ("qk", k + 1, 0))
        if 1 <= k <= last + 1:
            at(7, ("energy", k - 1))
        if k < last:
            at(8, ("stack_parts", k + 1, 0))
        if k >= 2:
            at(8, ("xattn", k - 2), ("ln3_stats", k - 2))
        if 1 <= k <= last + 1:
            at(9, ("energy_exp", k - 1))
        if k < last:
            at(10, ("qk", k + 1, 1))
        if k >= 2:
            at(11, ("ln3_apply", k - 2))
            at(12, ("ln3_turn", k - 2))
        if 1 <= k <= last + 1:
            at(11, ("att_scale", k - 1))
        if k < last:
            at(12, ("stack_parts", k + 1, 1))
        if 1 <= k <= last + 1:
            at(13, ("att_turn", k - 1))
        if k >= 2:
            at(14, ("router", k - 2))
            at(15, ("hot", k - 2))
        for h in range(HEADS):
            if k <= last:
                order.append(("scores", k, h))
            if k >= 1:
                order.append(("probs", k - 1, h))
                if h % 2 == 1:
                    order.append(("causal", k - 1, h // 2))
                if h % 4 == 1 and h > 4:
                    order.append(("pv", k - 1, h // 4 - 1))
            order += fill[h]
        if k <= last:
            order.append(("m_parts", k))
        if k >= 2:
            order.append(("choose", k - 2))
        if k >= 1:
            order.append(("pv", k - 1, HEADS // 4 - 1))
    b = last
    order += [("o_back", b, 0), ("o_back", b, 1), ("o_turn", b), ("wo", b), ("ln2_stats", b), ("ln2_apply", b), ("sh_up", 0), ("ln2_turn", b),
              ("xattn", b), ("ln3_stats", b), ("ln3_apply", b), ("sh_up", 1), ("ln3_turn", b), ("router", b), ("hot", b), ("sh_up", 2),
              ("choose", b), ("rank",), ("starts",), ("tiles",), ("positions",)]
    order += [("rows", 0), ("sh_up", 3), ("rows", 1)] + [("sh_down", T) for T in range(4)] + [("rows", 2)]
    for j in range(4):
        order += [("sh_up", 4 + j), ("rows", 3 + j)]
    order += [("rows", 7)] + [("sh_down", T) for T in range(4, 8)]
    return order


IN_MISC = ("x_weights", "x_turn", "qk", "v", "m_turn", "ctx_turn", "ctx_qk", "stack", "energy", "att_turn",
           "o_back", "o_turn", "wo", "ln2_turn", "xattn", "ln3_turn", "router", "pv", "sh_down", "rank", "starts", "tiles")


def decoder_layer(nc, x, ctx, wq, wk, wv, wo, xwq, xbq, xwk, xbk, rw, rb, wg, wu, wd, swg, swu, swd, out):
    B, S, D = x.shape
    C = ctx.shape[2]
    E, _, F = wg.shape
    SH, _, HS = swg.shape
    DK = D // HEADS
    N = B * S
    NT = N // P
    TB = S // P
    DC = D // P
    HC = SH * HS // P
    PAIRS = N * TOP
    MAX_TILES = -(-(PAIRS // P + E) // GROUP) * GROUP
    MIN_LAST = (PAIRS // P - 1) // GROUP
    MAX_LAST = MAX_TILES // GROUP - 1
    ROW = D + 2
    SCALE = float(DK) ** -0.5
    assert TB == 2 and DC == 2 and C == P and HEADS * DK == D and F * 2 == P and D == 2 * P and HC == 4

    ORDER = stage_order(B)
    NORM = {s[0][:3] + str(s[1]): i for i, s in enumerate([s for s in ORDER if s[0].endswith("_stats")])}
    MISC = {s: i for i, s in enumerate([s for s in ORDER if s[0] in IN_MISC])}

    with ExitStack() as stack:
        def sb(name, shape, dt=F32):
            return stack.enter_context(nc.sbuf_tensor("sb_" + name, shape, dt))

        def sem(name):
            return stack.enter_context(nc.semaphore(name))

        def bank(name):
            return stack.enter_context(nc.psum_tensor("ps_" + name, [P, 512], F32))

        score_banks = [bank("s0"), bank("s1")]
        prob_banks = [bank("p0"), bank("p1")]
        misc = [bank(f"m{i}") for i in range(MISC_BANKS)]

        rows_dram = nc.dram_tensor("rows_scratch", (PAIRS + P, ROW), F32, kind="Internal").ap()
        y_dram = nc.dram_tensor("y_scratch", (PAIRS, D), F32, kind="Internal").ap()

        shared_region = sb("attention_or_down", [P, E * D])
        at = [0]

        def part(words):
            at[0] += words
            return shared_region[:, at[0] - words:at[0]]
        stacks = [part(2 * HEADS * S // 2).bitcast(BF16).rearrange("p (x h t) -> p x h t", x=2, h=HEADS) for _ in range(2)]
        pt = part(PT_SLOTS * 3 * P).rearrange("p (s c) -> p s c", s=PT_SLOTS)
        stk = [part(HEADS * PARTS * DK).bitcast(BF16).rearrange("p (x h r d) -> p x h r d", x=2, h=HEADS, r=PARTS)
               for _ in range(2)]
        v_ones = [part(TB * HEADS * 32).rearrange("p (t h j) -> p t h j", t=TB, h=HEADS) for _ in range(2)]
        down_w = shared_region[0:F, :].rearrange("p (e n) -> p e n", e=E)

        gate_up = sb("gate_up", [P, E, 2, DC * F])
        sh_g = sb("sh_g", [P, DC, SH * HS])
        sh_u = sb("sh_u", [P, DC, SH * HS])
        w_qkv = sb("w_qkv", [P, DC, 3 * D])
        wq_flat = w_qkv[:, :, :].rearrange("p c n -> p (c n)")
        sh_d = wq_flat[:, 0:HC * D].rearrange("p (j n) -> p j n", j=HC)
        w_o = sb("w_o", [P, DC, D])
        xres = sb("xres", [P, NT, D])
        flat = sb("flat", [P, NT, D])
        flat_t = sb("flat_t", [P, DC, N])
        rows_or_at = sb("rows_or_at", [P, ROW_SLOTS * ROW])
        att_t = rows_or_at[:, 0:2 * DC * S].rearrange("p (b c m) -> p b c m", b=2, c=DC)
        row_out = rows_or_at[:, :].rearrange("p (s r) -> p s r", s=ROW_SLOTS)
        chosen = sb("chosen", [P, NT, TOP, E], BF16)
        o_t = sb("o_t", [P, 4, S])
        tok = sb("tok", [P, TB, D])
        feat = sb("feat", [P, DC, S])
        early = sb("early", [P, 3 * 1024])
        part1 = early[:, 0:256].bitcast(BF16)
        part2 = early[:, 256:512].bitcast(BF16)
        rest = early[:, 512:1024]
        ctx_sb = early[:, 1024:1280].rearrange("p (t c) -> p t c", t=TB)
        ctx_t = early[:, 1280:1536]
        ctx_qk = early[:, 1536:2048].rearrange("p (x t) -> p x t", x=2)
        att = early[:, 2048:2560].rearrange("p (t n) -> p t n", t=TB)
        x_t = early[:, 2560:3072].rearrange("p (c t) -> p c t", c=DC)
        hid = early[:, 0:2048].rearrange("p (j t) -> p j t", j=HC)
        sil = early[:, 2048:3072].rearrange("p (s t) -> p s t", s=2)
        o_flat = o_t[:, :, :].rearrange("p g t -> p (g t)")
        x_w = o_flat[:, 0:2 * C].rearrange("p (x c) -> p x c", x=2)
        x_wt = sb("x_wt", [P, 2, C])
        x_bias = sb("x_bias", [P, 2])
        r_w = sb("r_w", [P, DC, E])
        r_bias = sb("r_bias", [P, E])

        ident = sb("ident", [P, P])
        ident_b = sb("ident_b", [P, P], BF16)
        mask_b = sb("mask_b", [P, 2, P], BF16)
        before_b = sb("before_b", [P, P], BF16)
        ones_b = sb("ones_b", [P, P], BF16)
        ones = sb("ones", [P, P])
        before = sb("before", [E, E])
        upto = sb("upto", [E, E])
        iota_e = sb("iota_e", [P, E])
        iota_t = sb("iota_t", [P, MAX_TILES])
        iota_p = sb("iota_p", [P, 1])
        neg_half = sb("neg_half", [P, 2])
        pair_info = sb("pair_info", [P, NT * TOP, 2])
        bn = sb("bn", [P, 3, TB, 6])
        mv = sb("mv", [P, 3, TB, 2])
        rstd = sb("rstd", [P, 3, TB])
        shift = sb("shift", [P, 3, TB])
        m_raw = sb("m_raw", [P, HEADS, 3])
        m_max = sb("m_max", [P, TB, HEADS])
        m_rest = sb("m_rest", [P, TB, HEADS])
        m_part = sb("m_part", [P, TB, 3, HEADS], BF16)
        m_t = sb("m_t", [3 * HEADS, S], BF16)
        o_rec = sb("o_rec", [P, HEADS])
        e_max = sb("e_max", [P, 4])
        e_sum = sb("e_sum", [P, 4])
        logits = sb("logits", [P, TB, E])
        biased = sb("biased", [P, TB, E])
        expd = sb("expd", [P, TB, E])
        top8 = sb("top8", [P, TB, 8])
        top_i = sb("top_i", [P, TB, 8], U32)
        top_f = sb("top_f", [P, TB, 8])
        r_max = sb("r_max", [P, 2])
        r_sum = sb("r_sum", [P, 2])
        top_s = sb("top_s", [P, TB, TOP])
        top_sum = sb("top_sum", [P, 2])
        chose = sb("chose", [P, NT, E], BF16)
        cnt = sb("cnt", [E, 8])
        cnt_i = sb("cnt_i", [E, 1], I32)
        cnt_q = sb("cnt_q", [P, 1], I32)
        wide = o_flat[0:E, 0:3 * P].rearrange("p (r c) -> p r c", r=3)
        in_tile = o_flat[0:E, 384:384 + 2 * MAX_TILES].rearrange("p (r c) -> p r c", r=2)
        tile_f = o_flat[:, 640:640 + 2 * MAX_TILES].rearrange("p (r c) -> p r c", r=2)
        rank_sb = feat[:, :, :].rearrange("p c t -> p (c t)").rearrange("p (t e) -> p t e", t=NT)
        penalty = sb("penalty", [P, MAX_TILES])
        tile_i = sb("tile_i", [P, 2 * MAX_TILES + 1], I32)
        pos_i = sb("pos_i", [P, NT * TOP], I32)
        exp_hot = feat[:, :, :].rearrange("p c t -> p (c t)").rearrange("p (t k e) -> p t k e", t=TB, k=TOP)
        prod = tok[:, :, :].rearrange("p t (k e) -> p t k e", k=TOP)
        pos_f = sb("pos_f", [P, NT * TOP])

        row_in = early[:, 0:GROUP * ROW].rearrange("p (s r) -> p s r", s=GROUP)
        y_out = o_flat[:, 0:Y_SLOTS * D].rearrange("p (s n) -> p s n", s=Y_SLOTS)
        xt_in = wq_flat[:, 0:2 * D].rearrange("p (s c t) -> p s c t", s=2, c=DC)
        sil_in = wq_flat[:, 512:640].rearrange("p (s f) -> p s f", s=2)
        h_in = wq_flat[:, 640:768].rearrange("p (s f) -> p s f", s=2)
        ht_in = wq_flat[0:F, 768:1024].rearrange("p (s t) -> p s t", s=2)
        pair_i = sb("pair_i", [P, GROUP], I32)
        pair_w = sb("pair_w", [P, GROUP])
        y_back = gate_up[:, :, :, :].rearrange("p e x f -> p (e x f)")[:, 0:NT * TOP * D] \
            .rearrange("p (t k n) -> p t k n", t=NT, k=TOP)

        x_in = [sem(f"x_in{b}") for b in range(B)]
        qkv_in, wo_in, xw_in, xb_in, r_in, shg_in, shd_in = map(sem, ("qkv_in", "wo_in", "xw_in", "xb_in", "r_in", "shg_in", "shd_in"))
        gu_in, dw_in, tail_in = map(sem, ("gu_in", "dw_in", "tail_in"))
        ctx_in = sem("ctx_in")
        misc_full = [sem(f"misc_full{i}") for i in range(MISC_BANKS)]
        misc_free = [sem(f"misc_free{i}") for i in range(MISC_BANKS)]
        (consts, ident_ok, var_ok, rstd_ok, ln1_ok, tok_ok, feat_ok, xt_ok, part1_ok, rest_ok, part2_ok, stk_ok, stk3_ok, stk_used,
         v_ok, stack_ok_d, stack_ok_a, m_part_ok, mt_ok, m_rows, dve, pool, act) = map(sem, (
             "consts", "ident_ok", "var_ok", "rstd_ok", "ln1_ok", "tok_ok", "feat_ok", "xt_ok", "part1_ok", "rest_ok", "part2_ok",
             "stk_ok", "stk3_ok", "stk_used", "v_ok", "stack_ok_d", "stack_ok_a", "m_part_ok", "mt_ok", "m_rows",
             "dve", "pool", "act"))
        (scores_full, scores_used, probs_full, probs_used, causal_ok, pv_done, ot_ok, ctxt_ok, ctxqk_ok, emax_ok, esum_ok, att_ok,
         attt_ok, res_ok, flatt_ok, logits_ok, expd_ok, chose_ok, info_ok) = map(sem, (
             "scores_full", "scores_used", "probs_full", "probs_used", "causal_ok", "pv_done", "ot_ok", "ctxt_ok", "ctxqk_ok",
             "emax_ok", "esum_ok", "att_ok", "attt_ok", "res_ok", "flatt_ok", "logits_ok", "expd_ok", "chose_ok", "info_ok"))
        (up_full, sil_ok, hid_ok, down_done, count_ok, span_ok, tiles_ok, pos_ok, iota_ok, xwt_ok) = map(sem, (
            "up_full", "sil_ok", "hid_ok", "down_done", "count_ok", "span_ok", "tiles_ok", "pos_ok", "iota_ok", "xwt_ok"))
        erec_ok, hot_ok, exp_hot_ok = map(sem, ("erec_ok", "hot_ok", "exp_hot_ok"))
        rows_filled = sem("rows_filled")
        row_sent = [sem(f"row_sent{i}") for i in range(ROW_SLOTS)]
        row_here = [sem(f"row_here{i}") for i in range(GROUP)]
        y_sent = [sem(f"y_sent{i}") for i in range(Y_SLOTS)]
        (turned, xt_here, gu_done, sil_here, h_here, h_turned, ht_here, y_done, y_here, pair_here) = map(sem, (
            "turned", "xt_here", "gu_done", "sil_here", "h_here", "h_turned", "ht_here", "y_done", "y_here", "pair_here"))
        y_loaded = [sem(f"y_loaded{T}") for T in range(NT)]
        sum_ok, stored = sem("sum_ok"), sem("stored")

        def misc_take(eng, s):
            i = MISC[s]
            if i >= MISC_BANKS:
                eng.wait_ge(misc_free[i % MISC_BANKS], i // MISC_BANKS)
            return misc[i % MISC_BANKS]

        def misc_wait(eng, s):
            i = MISC[s]
            eng.wait_ge(misc_full[i % MISC_BANKS], i // MISC_BANKS + 1)
            return misc[i % MISC_BANKS]

        def full(s):
            return misc_full[MISC[s] % MISC_BANKS]

        def free(s):
            return misc_free[MISC[s] % MISC_BANKS]

        def as_bf16(b):
            return b[:, :].bitcast(BF16)

        def key_blocks(blocks, h):
            v = blocks.rearrange("p (a c) -> p a c", a=3)
            return (v[:, 1::-1, :], v[:, 2, :]) if h % 2 == 0 else (v[:, 1:3, :], v[:, 0, :])

        block = stack.enter_context(nc.Block())
        NG = HEADS // 4

        @block.sync
        def _(sp):
            for b in range(B):
                sp.dma_start(xres[:, b * TB:(b + 1) * TB, :], x[b].rearrange("(t p) d -> p t d", p=P)).then_inc(x_in[b], 16)
                if b == 0:
                    for i, w in enumerate((wq, wk, wv)):
                        sp.dma_start(w_qkv[:, :, i * D:(i + 1) * D], w.rearrange("(c p) n -> p c n", p=P)).then_inc(qkv_in, 16)
            sp.dma_start(x_w[:, 0, :], xwq).then_inc(xw_in, 16)
            sp.dma_start(x_w[:, 1, :], xwk).then_inc(xw_in, 16)
            sp.dma_start(x_bias[:, 0:1], xbq.rearrange("(p o) -> p o", o=1)).then_inc(xb_in, 16)
            sp.dma_start(x_bias[:, 1:2], xbk.rearrange("(p o) -> p o", o=1)).then_inc(xb_in, 16)
            sp.dma_start(w_o[:, :, :], wo.rearrange("(c p) n -> p c n", p=P)).then_inc(wo_in, 16)
            sp.dma_start(r_w[:, :, :], rw.rearrange("(c p) n -> p c n", p=P)).then_inc(r_in, 16)
            sp.dma_start(r_bias[:, :], rb.rearrange("(o e) -> o e", o=1).broadcast_to([P, E])).then_inc(r_in, 16)
            for s in range(SH):
                sp.dma_start(sh_g[:, :, s * HS:(s + 1) * HS], swg[s].rearrange("(c p) h -> p c h", p=P)).then_inc(shg_in, 16)
                sp.dma_start(sh_u[:, :, s * HS:(s + 1) * HS], swu[s].rearrange("(c p) h -> p c h", p=P)).then_inc(shg_in, 16)
            late = [(e0, i, w) for e0 in range(0, E, 8) for i, w in enumerate((wg, wu))]
            loads = 0

            def load_experts(n):
                nonlocal loads
                for e0, i, w in late[loads:loads + n]:
                    sp.dma_start(gate_up[:, e0:e0 + 8, i, :], w[e0:e0 + 8].rearrange("e (p c) f -> p e (c f)", p=P)).then_inc(gu_in, 16)
                loads += n

            for s in ORDER:
                if s[0] == "m_turn":
                    b = s[1]
                    sp.wait_ge(mt_ok, b + 1)
                    load_experts(4)
                    if b == B - 1:
                        misc_wait(sp, ("v", B - 1))
                        for i in range(SH):
                            sp.dma_start(sh_d[:, i * (HS // P):(i + 1) * (HS // P), :],
                                         swd[i].rearrange("(j p) n -> p j n", p=P)).then_inc(shd_in, 16)
            sp.wait_ge(pv_done, B * NG)
            sp.wait_ge(ln1_ok, 2 * B)
            sp.dma_start(rows_dram[PAIRS:PAIRS + P, :], flat[:, :, :].rearrange("p t d -> p (t d)")[:, 0:ROW]).then_inc(tail_in, 16)
            for e0 in range(0, E, 16):
                sp.dma_start(down_w[:, e0:e0 + 16, :], wd[e0:e0 + 16].rearrange("e f n -> f e n")).then_inc(dw_in, 16)
            for i in range(ROW_SLOTS):
                sp.wait_ge(row_sent[i], 16 * NT * TOP // ROW_SLOTS)
            sp.wait_ge(tail_in, 16)
            sp.wait_ge(tiles_ok, 1)
            sp.wait_ge(down_done, NT)
            last = nc.sync.value_load(tile_i[0:1, 2 * MAX_TILES:2 * MAX_TILES + 1], min_val=MIN_LAST, max_val=MAX_LAST)
            groups = last + 1

            def load_rows(j, i):
                first = nc.sync.value_load(tile_i[0:1, bass.ds(i + MAX_TILES, 1)], min_val=0, max_val=PAIRS)
                if not isinstance(i, int):
                    sp.wait_ge(turned, i - GROUP + 1)
                    sp.wait_ge(pair_here, i - GROUP + 1)
                sp.dma_start(row_in[:, j, :], rows_dram[bass.ds(first, P), :]).then_inc(row_here[j], 16)

            for j in range(GROUP):
                load_rows(j, j)
            with sp.Fori(1, groups) as q:
                for j in range(GROUP):
                    load_rows(j, q * GROUP + j)
            for j in range(Y_SLOTS):
                sp.wait_ge(y_sent[j], groups * (16 * GROUP // Y_SLOTS))
            for T in range(NT):
                sp.dma_start(y_back[:, T, :, :], y_dram[T * P * TOP:(T + 1) * P * TOP, :].rearrange("(p k) n -> p k n", k=TOP)) \
                    .then_inc(y_loaded[T], 16)
            for T in range(NT):
                sp.wait_ge(sum_ok, T + 1)
                b, t = divmod(T, TB)
                sp.dma_start(out[b, t * P:(t + 1) * P, :], xres[:, T, :]).then_inc(stored, 16)
            sp.wait_ge(stored, 16 * NT)

        @block.tensor
        def _(pe):
            def turn(dst, src, idm, s, last):
                ins = pe.transpose(dst, src, idm)
                if last:
                    ins.then_inc(full(s), 1)

            def turn_feat(s, src):
                b = misc_take(pe, s)
                for c in range(DC):
                    for t in range(TB):
                        turn(b[:, (c * TB + t) * P:(c * TB + t + 1) * P], src[:, t, c * P:(c + 1) * P], ident[:, :], s,
                             c == DC - 1 and t == TB - 1)

            pe.wait_ge(ident_ok, 1)
            for s in ORDER:
                stage, a = s[0], s[1:]
                if stage == "x_weights":
                    pe.wait_ge(xw_in, 32)
                    b = misc_take(pe, s)
                    for i in range(2):
                        turn(b[:, i * P:(i + 1) * P], x_w[:, i, :], ident[:, :], s, i == 1)
                elif stage == "x_turn":
                    pe.wait_ge(ln1_ok, a[0] + 1)
                    turn_feat(s, flat[:, a[0] * TB:(a[0] + 1) * TB, :])
                elif stage == "qk":
                    k, t = a
                    if k == 0 and t == 0:
                        pe.wait_ge(qkv_in, 48)
                    pe.wait_ge(xt_ok, k + 1)
                    b = misc_take(pe, s)
                    for c in range(DC):
                        ins = pe.matmul(b[:, :], x_t[:, c, t * P:(t + 1) * P], w_qkv[:, c, 0:2 * D], start=c == 0, stop=c == DC - 1)
                    ins.then_inc(full(s), 1)
                elif stage == "v":
                    b = misc_take(pe, s)
                    for t in range(TB):
                        for c in range(DC):
                            ins = pe.matmul(b[:, t * D:(t + 1) * D], x_t[:, c, t * P:(t + 1) * P], w_qkv[:, c, 2 * D:3 * D],
                                            start=c == 0, stop=c == DC - 1)
                    ins.then_inc(full(s), 1)
                elif stage == "stack":
                    k, t, xx, half = a
                    if k == 0:
                        pe.wait_ge(consts, 1)
                    pe.wait_ge(stk_ok, 2 * k + t + 1)
                    pe.wait_ge(stk3_ok, 2 * k + t + 1)
                    b = as_bf16(misc_take(pe, s))
                    for i in range(8):
                        ins = pe.transpose(b[0:PARTS * DK, i * P:(i + 1) * P],
                                           stk[t][:, xx, half * 8 + i, :, :].rearrange("p r d -> p (r d)"), ident_b[:, :])
                    ins.then_inc(full(s), 1)
                elif stage == "scores":
                    k, h = a
                    n = k * HEADS + h
                    if h == 0:
                        pe.wait_ge(stack_ok_d, 4 * (k + 1))
                        pe.wait_ge(stack_ok_a, 4 * (k + 1))
                    if n >= 2:
                        pe.wait_ge(scores_used, n - 1)
                    sq, b = stacks[k % 2], score_banks[n % 2]
                    R = PARTS * DK
                    pe.matmul(b[:, 0:2 * P], sq[0:R, 0, h, P:2 * P], sq[0:R, 1, h, :], start=True, stop=False, skip_group_check=True)
                    pe.matmul(b[:, 2 * P:3 * P], sq[0:R, 0, h, 0:P], sq[0:R, 1, h, 0:P], start=False, stop=False, skip_group_check=True)
                    pe.matmul(b[:, P:3 * P], ident_b[:, :], mask_b[:, :, :].rearrange("p a b -> p (a b)"),
                              start=False, stop=True, skip_group_check=True).then_inc(scores_full, 1)
                elif stage == "m_turn":
                    k, = a
                    pe.wait_ge(m_part_ok, k + 1)
                    b = as_bf16(misc_take(pe, s))
                    for t in range(TB):
                        turn(b[0:3 * HEADS, t * P:(t + 1) * P], m_part[:, t, :, :].rearrange("p r h -> p (r h)"), ident_b[:, :], s, t == 1)
                elif stage == "probs":
                    k, h = a
                    n = k * HEADS + h
                    if h == 0:
                        pe.wait_ge(m_rows, 48 * (k + 1))
                    if n >= 2:
                        pe.wait_ge(probs_used, n - 1)
                    sq, b = stacks[k % 2], prob_banks[n % 2]
                    R = PARTS * DK + 3
                    first, second = key_blocks(b[:, 0:3 * P], h)
                    pe.matmul(first, sq[0:R, 1, h, 0:P], sq[0:R, 0, h, :], start=True, stop=True, skip_group_check=True)
                    pe.matmul(second, sq[0:R, 1, h, P:2 * P], sq[0:R, 0, h, P:2 * P], start=False, stop=True,
                              skip_group_check=True).then_inc(probs_full, 1)
                elif stage == "pv":
                    k, g = a
                    pe.wait_ge(causal_ok, k * 8 + 2 * g + 2)
                    if g == 0:
                        pe.wait_ge(v_ok, k + 1)
                    b = misc_take(pe, s)
                    for j in range(4):
                        h = 4 * g + j
                        pe.matmul(b[32 * j:32 * j + 32, 0:2 * P], v_ones[k % 2][:, 0, h, :], key_blocks(pt[:, h % PT_SLOTS, :], h)[0],
                                  start=True, stop=False, skip_group_check=True)
                    for j in range(4):
                        h = 4 * g + j
                        ins = pe.matmul(b[32 * j:32 * j + 32, P:2 * P], v_ones[k % 2][:, 1, h, :], key_blocks(pt[:, h % PT_SLOTS, :], h)[1],
                                        start=False, stop=True, skip_group_check=True)
                    ins.then_inc(full(s), 1)
                elif stage == "o_back":
                    k, t = a
                    if t == 0:
                        pe.wait_ge(ot_ok, NG * (k + 1))
                    b = misc_take(pe, s)
                    for g in range(NG):
                        turn(b[:, g * P:(g + 1) * P], o_t[:, g, t * P:(t + 1) * P], ident[:, :], s, g == NG - 1)
                elif stage == "o_turn":
                    pe.wait_ge(tok_ok, 2 * a[0] + 1)
                    turn_feat(s, tok)
                elif stage == "wo":
                    k, = a
                    if k == 0:
                        pe.wait_ge(wo_in, 16)
                    pe.wait_ge(feat_ok, 2 * k + 1)
                    b = misc_take(pe, s)
                    for t in range(TB):
                        for c in range(DC):
                            ins = pe.matmul(b[:, t * D:(t + 1) * D], feat[:, c, t * P:(t + 1) * P], w_o[:, c, :], start=c == 0, stop=c == DC - 1)
                    ins.then_inc(full(s), 1)
                elif stage == "ln2_turn":
                    pe.wait_ge(tok_ok, 2 * a[0] + 2)
                    turn_feat(s, tok)
                elif stage == "ctx_turn":
                    k, = a
                    pe.wait_ge(ctx_in, 16 * (k + 1))
                    b = misc_take(pe, s)
                    for t in range(TB):
                        turn(b[:, t * P:(t + 1) * P], ctx_sb[:, t, :], ident[:, :], s, t == 1)
                elif stage == "ctx_qk":
                    k, = a
                    pe.wait_ge(ctxt_ok, k + 1)
                    if k == 0:
                        pe.wait_ge(xwt_ok, 1)
                    b = misc_take(pe, s)
                    for i in range(2):
                        ins = pe.matmul(b[:, i * S:(i + 1) * S], x_wt[:, i, :], ctx_t, start=True, stop=True)
                    ins.then_inc(full(s), 1)
                elif stage == "energy":
                    k, = a
                    pe.wait_ge(ctxqk_ok, k + 1)
                    b = misc_take(pe, s)
                    for t in range(TB):
                        ins = pe.matmul(b[:, t * S:(t + 1) * S], ctx_qk[:, 0, t * P:(t + 1) * P], ctx_qk[:, 1, :], start=True, stop=True)
                    ins.then_inc(full(s), 1)
                elif stage == "att_turn":
                    pe.wait_ge(att_ok, a[0] + 1)
                    turn_feat(s, att)
                elif stage == "xattn":
                    k, = a
                    pe.wait_ge(attt_ok, k + 1)
                    pe.wait_ge(feat_ok, 2 * k + 2)
                    b = misc_take(pe, s)
                    for t in range(TB):
                        for c in range(DC):
                            ins = pe.matmul(b[:, t * S:(t + 1) * S], feat[:, c, t * P:(t + 1) * P], att_t[:, k % 2, c, :],
                                            start=c == 0, stop=c == DC - 1)
                    ins.then_inc(full(s), 1)
                elif stage == "ln3_turn":
                    pe.wait_ge(ln1_ok, B + a[0] + 1)
                    turn_feat(s, flat[:, a[0] * TB:(a[0] + 1) * TB, :])
                elif stage == "router":
                    k, = a
                    if k == 0:
                        pe.wait_ge(r_in, 32)
                    pe.wait_ge(flatt_ok, k + 1)
                    b = misc_take(pe, s)
                    for t in range(TB):
                        T = k * TB + t
                        for c in range(DC):
                            ins = pe.matmul(b[:, t * E:(t + 1) * E], flat_t[:, c, T * P:(T + 1) * P], r_w[:, c, :], start=c == 0, stop=c == DC - 1)
                    ins.then_inc(full(s), 1)
                elif stage == "sh_up":
                    i, = a
                    tokens, j = divmod(i, HC)
                    if i == 0:
                        pe.wait_ge(shg_in, 16 * 2 * SH)
                        pe.wait_ge(scores_used, B * HEADS)
                        pe.wait_ge(probs_used, B * HEADS)
                    if i == HC:
                        pe.wait_ge(flatt_ok, B)
                    if i >= 2:
                        pe.wait_ge(hid_ok, i - 1)
                    bg, bu = (score_banks, prob_banks)[i % 2]
                    for b, w in ((bg, sh_g), (bu, sh_u)):
                        for c in range(DC):
                            ins = pe.matmul(b[:, :], w[:, c, j * P:(j + 1) * P], flat_t[:, c, tokens * 512:(tokens + 1) * 512],
                                            start=c == 0, stop=c == DC - 1)
                    ins.then_inc(up_full, 1)
                elif stage == "sh_down":
                    T, = a
                    if T == 0:
                        pe.wait_ge(shd_in, 16 * SH)
                    pe.wait_ge(hid_ok, HC * (T // 4 + 1))
                    b = misc_take(pe, s)
                    for j in range(HC):
                        ins = pe.matmul(b[:, 0:D], hid[:, j, (T % 4) * P:(T % 4 + 1) * P], sh_d[:, j, :], start=j == 0, stop=j == HC - 1)
                    ins.then_inc(full(s), 1)
                elif stage == "rank":
                    pe.wait_ge(chose_ok, B)
                    b = misc_take(pe, s)
                    for T in range(NT):
                        pe.matmul(b[:, T * E:(T + 1) * E], before_b[:, :], chose[:, T, :], start=T == 0, stop=False, skip_group_check=True)
                        for T2 in range(T):
                            ins = pe.matmul(b[:, T * E:(T + 1) * E], ones_b[:, :], chose[:, T2, :], start=False, stop=T2 == NT - 2,
                                            skip_group_check=True)
                    ins.then_inc(full(s), 1)
                elif stage == "starts":
                    b = misc_take(pe, s)
                    for T in range(NT):
                        ins = pe.matmul(b[0:E, 0:1], chose[:, T, :], ones_b[:, 0:1], start=T == 0, stop=T == NT - 1)
                    ins.then_inc(count_ok, 1)
                    pe.wait_ge(span_ok, 1)
                    pe.matmul(b[0:E, 0:1], upto[:, :], cnt[:, 1:2], start=True, stop=True)
                    pe.matmul(b[0:E, 1:2], before[:, :], cnt[:, 0:1], start=True, stop=True)
                    pe.matmul(b[:, 64:64 + E], wide[:, 0, :], before[:, :], start=True, stop=True).then_inc(full(s), 1)
                elif stage == "tiles":
                    pe.wait_ge(span_ok, 2)
                    b = misc_take(pe, s)
                    M = MAX_TILES
                    pe.matmul(b[:, 0:M], ones[0:E, :], in_tile[:, 0, :], start=True, stop=True)
                    pe.matmul(b[:, M:2 * M], wide[:, 1, :], in_tile[:, 1, :], start=True, stop=True)
                    pe.matmul(b[:, 2 * M:3 * M], wide[:, 2, :], in_tile[:, 1, :], start=True, stop=True)
                    pe.matmul(b[:, 3 * M:3 * M + 1], ones[0:E, :], cnt[:, 1:2], start=True, stop=True).then_inc(full(s), 1)

            pe.wait_ge(tiles_ok, 1)
            for i in range(MISC_BANKS):
                pe.wait_ge(misc_free[i], len([u for u in MISC.values() if u % MISC_BANKS == i]))
            pe.wait_ge(hid_ok, 2 * HC)
            pe.wait_ge(gu_in, 16 * 2 * (E // 8))
            pe.wait_ge(dw_in, 16 * (E // 16))
            last = nc.tensor.value_load(tile_i[0:1, 2 * MAX_TILES:2 * MAX_TILES + 1], min_val=MIN_LAST, max_val=MAX_LAST)
            groups = last + 1
            xt_b, gu_b, ht_b, y_b = score_banks, prob_banks, misc[0:2], misc[2:4]

            expert = [nc.tensor.alloc_register(f"expert_{j}") for j in range(GROUP)]


            def read_expert(j, i):
                nc.tensor.reg_load(expert[j], tile_i[0:1, bass.ds(i, 1)])

            def expert_of(j):
                return nc.tensor.snap(expert[j], min_val=0, max_val=E - 1)

            def turn_rows(q, j, i):
                pe.wait_ge(row_here[j], q * 16 + 16)
                rows = row_in[:, j, 0:D].rearrange("p (m c) -> p c m", c=DC)
                pe.transpose(xt_b[j % 2][:, 0:P], rows[:, 0, :], ident[:, :])
                pe.transpose(xt_b[j % 2][:, P:2 * P], rows[:, 1, :], ident[:, :]).then_inc(turned, 1)

            def gate_and_up(j, i):
                e = expert_of(j)
                pe.wait_ge(xt_here, i + 1)
                b = gu_b[j % 2]
                for c in range(DC):
                    ins = pe.matmul(b[:, 0:2 * F], xt_in[:, j % 2, c, :], gate_up[:, bass.ds(e, 1), :, c * F:(c + 1) * F],
                                    start=c == 0, stop=c == DC - 1)
                ins.then_inc(gu_done, 1)

            def turn_h(j, i):
                here = i + 1 if isinstance(i, int) else nc.tensor.to_reg(i + 1)
                pe.wait_ge(tiles_ok, 1)
                pe.wait_ge(h_here, here)
                pe.transpose(ht_b[j % 2][0:F, 0:P], h_in[:, j % 2, :], ident[:, :]).then_inc(h_turned, 1)

            def down(j, i):
                e = expert_of(j)
                pe.wait_ge(ht_here, i + 1)
                if not isinstance(i, int) or i >= 2:
                    pe.wait_ge(y_here, i - 1)
                pe.matmul(y_b[j % 2][:, 0:D], ht_in[:, j % 2, :], down_w[:, bass.ds(e, 1), :], start=True, stop=True).then_inc(y_done, 1)

            for j in range(GROUP):
                read_expert(j, j)
                turn_rows(0, j, j)
                if j >= 1:
                    gate_and_up(j - 1, j - 1)
                if j >= 2:
                    turn_h(j - 2, j - 2)
                if j >= 3:
                    down(j - 3, j - 3)
            with pe.Fori(1, groups) as q:
                for j in range(GROUP):
                    i = q * GROUP + j
                    read_expert(j, i)
                    turn_rows(q, j, i)
                    gate_and_up(j - 1, i - 1)
                    turn_h(j - 2, i - 2)
                    down(j - 3, i - 3)
            end = groups * GROUP
            gate_and_up(-1, end - 1)
            turn_h(-2, end - 2)
            down(-3, end - 3)
            turn_h(-1, end - 1)
            down(-2, end - 2)
            down(-1, end - 1)

        @block.scalar
        def _(eng):
            A = nc.scalar

            def load_context(b_):
                eng.dma_start(ctx_sb, ctx[b_].rearrange("(t p) c -> p t c", p=P)).then_inc(ctx_in, 16)

            load_context(0)
            for s in ORDER:
                stage, a = s[0], s[1:]
                if stage in ("ln1_apply", "ln2_apply", "ln3_apply"):
                    k, = a
                    kind = int(stage[2]) - 1
                    eng.wait_ge(rstd_ok, NORM[stage[:3] + str(k)] + 1)
                    dst, done = (tok, tok_ok) if kind == 1 else (flat[:, k * TB:(k + 1) * TB, :], ln1_ok)
                    for t in range(TB):
                        ins = A.activation(dst[:, t, :], xres[:, k * TB + t, :], ACT.Identity, bias=shift[:, kind, t:t + 1],
                                           scale=rstd[:, kind, t:t + 1])
                    ins.then_inc(done, 1)
                if stage == "x_weights":
                    b = misc_wait(eng, s)
                    A.copy(x_wt[:, :, :], b[:, 0:2 * C].rearrange("p (x c) -> p x c", x=2)).then_inc(xwt_ok, 1)
                    eng.wait_ge(xwt_ok, 1)
                    eng.sem_inc(free(s), 1)
                elif stage == "x_turn":
                    k, = a
                    b = misc_wait(eng, s)
                    if k >= 1:
                        misc_wait(eng, ("v", k - 1))
                    A.copy(x_t, b[:, :].rearrange("p (c t) -> p c t", c=DC)).then_inc(xt_ok, 1)
                    eng.wait_ge(xt_ok, k + 1)
                    eng.sem_inc(free(s), 1)
                elif stage == "qk":
                    k, t = a
                    b = misc_wait(eng, s)
                    n = 2 * k + t
                    if n >= 1:
                        eng.wait_ge(stk_ok, n)
                    A.copy(part1, b[:, :]).then_inc(part1_ok, 1)
                elif stage == "v":
                    k, = a
                    b = misc_wait(eng, s)
                    if k >= 2:
                        eng.wait_ge(pv_done, NG * (k - 1))
                    if k == 0:
                        eng.wait_ge(consts, 1)
                    A.copy(v_ones[k % 2][:, :, :, 0:DK], b[:, :].rearrange("p (t h d) -> p t h d", t=TB, h=HEADS)).then_inc(v_ok, 1)
                    eng.wait_ge(v_ok, k + 1)
                    eng.sem_inc(free(s), 1)
                elif stage == "stack":
                    k, t, xx, half = a
                    if half == 1:
                        b = as_bf16(misc_wait(eng, s))
                        if k >= 2:
                            eng.wait_ge(probs_full, HEADS * (k - 1))
                        A.copy(stacks[k % 2][0:PARTS * DK, xx, 8:16, t * P:(t + 1) * P],
                               b[0:PARTS * DK, :].rearrange("p (h t) -> p h t", h=8)).then_inc(stack_ok_a, 1)
                        eng.wait_ge(stack_ok_a, 4 * k + 2 * t + xx + 1)
                        eng.sem_inc(free(s), 1)
                elif stage == "m_turn":
                    k, = a
                    b = as_bf16(misc_wait(eng, s))
                    if k >= 1:
                        eng.wait_ge(m_rows, 48 * k)
                    A.copy(m_t[:, :], b[0:3 * HEADS, 0:S]).then_inc(mt_ok, 1)
                    eng.wait_ge(mt_ok, k + 1)
                    eng.sem_inc(free(s), 1)
                    for r in range(3):
                        eng.dma_start(stacks[k % 2][96 + r:97 + r, 0, :, :], m_t[HEADS * r:HEADS * (r + 1), :]).then_inc(m_rows, 16)
                elif stage == "probs":
                    k, h = a
                    n = k * HEADS + h
                    eng.wait_ge(probs_full, n + 1)
                    if n >= PT_SLOTS:
                        eng.wait_ge(pv_done, (n - PT_SLOTS) // 4 + 1)
                    A.activation(pt[:, h % PT_SLOTS, :], prob_banks[n % 2][:, 0:3 * P], ACT.Exp, scale=SCALE).then_inc(probs_used, 1)
                elif stage == "pv":
                    k, g = a
                    b = misc_wait(eng, s)
                    eng.sem_inc(pv_done, 1)
                    if g == 0 and k >= 1:
                        misc_wait(eng, ("o_back", k - 1, 1))
                    A.copy(o_t[:, g, :], b[:, 0:S]).then_inc(ot_ok, 1)
                    eng.wait_ge(ot_ok, NG * k + g + 1)
                    eng.sem_inc(free(s), 1)
                elif stage in ("o_turn", "ln2_turn"):
                    k, = a
                    b = misc_wait(eng, s)
                    n = 2 * k + (stage == "ln2_turn") + 1
                    if n >= 2:
                        misc_wait(eng, ("wo", k) if stage == "ln2_turn" else ("xattn", k - 1))
                    if stage == "o_turn" and k >= 1:
                        eng.wait_ge(chose_ok, k)
                    A.copy(feat[:, :, :], b[:, :].rearrange("p (c t) -> p c t", c=DC)).then_inc(feat_ok, 1)
                    eng.wait_ge(feat_ok, n)
                    eng.sem_inc(free(s), 1)
                elif stage == "ctx_turn":
                    k, = a
                    b = misc_wait(eng, s)
                    if k >= 1:
                        misc_wait(eng, ("ctx_qk", k - 1))
                    A.copy(ctx_t, b[:, 0:S]).then_inc(ctxt_ok, 1)
                    eng.wait_ge(ctxt_ok, k + 1)
                    eng.sem_inc(free(s), 1)
                    if k + 1 < B:
                        load_context(k + 1)
                elif stage == "ctx_qk":
                    k, = a
                    if k == 0:
                        eng.wait_ge(xb_in, 32)
                    b = misc_wait(eng, s)
                    if k >= 1:
                        misc_wait(eng, ("energy", k - 1))
                    A.activation(ctx_qk[:, 0, :], b[:, 0:S], ACT.Identity, bias=x_bias[:, 0:1])
                    A.activation(ctx_qk[:, 1, :], b[:, S:2 * S], ACT.Identity, bias=x_bias[:, 1:2]).then_inc(ctxqk_ok, 1)
                    eng.wait_ge(ctxqk_ok, k + 1)
                    eng.sem_inc(free(s), 1)
                elif stage == "energy_exp":
                    k, = a
                    eng.wait_ge(emax_ok, k + 1)
                    b = misc_wait(eng, ("energy", k))
                    if k >= 1:
                        misc_wait(eng, ("att_turn", k - 1))
                    for t in range(TB):
                        ins = A.activation(att[:, t, :], b[:, t * S:(t + 1) * S], ACT.Exp, bias=e_max[:, 2 + t:3 + t],
                                           accum_out=e_sum[:, t:t + 1])
                    ins.then_inc(esum_ok, 1)
                    eng.wait_ge(esum_ok, k + 1)
                    eng.sem_inc(free(("energy", k)), 1)
                elif stage == "att_scale":
                    k, = a
                    eng.wait_ge(erec_ok, k + 1)
                    for t in range(TB):
                        ins = A.activation(att[:, t, :], att[:, t, :], ACT.Copy, scale=e_sum[:, 2 + t:3 + t])
                    ins.then_inc(att_ok, 1)
                elif stage == "att_turn":
                    k, = a
                    b = misc_wait(eng, s)
                    if k >= 2:
                        misc_wait(eng, ("xattn", k - 2))
                    A.copy(att_t[:, k % 2, :, :], b[:, :].rearrange("p (c m) -> p c m", c=DC)).then_inc(attt_ok, 1)
                    eng.wait_ge(attt_ok, k + 1)
                    eng.sem_inc(free(s), 1)
                elif stage == "ln3_turn":
                    k, = a
                    b = misc_wait(eng, s)
                    A.copy(flat_t[:, :, k * S:(k + 1) * S], b[:, :].rearrange("p (c t) -> p c t", c=DC)).then_inc(flatt_ok, 1)
                    eng.wait_ge(flatt_ok, k + 1)
                    eng.sem_inc(free(s), 1)
                elif stage == "router":
                    k, = a
                    eng.wait_ge(logits_ok, k + 1)
                    if k >= 1:
                        eng.wait_ge(chose_ok, k)
                    for t in range(TB):
                        ins = A.activation(expd[:, t, :], logits[:, t, :], ACT.Exp, bias=r_max[:, t:t + 1], accum_out=r_sum[:, t:t + 1])
                    ins.then_inc(expd_ok, 1)
                elif stage == "sh_up":
                    i, = a
                    eng.wait_ge(up_full, i + 1)
                    if i >= 2:
                        eng.wait_ge(hid_ok, i - 1)
                    b = (score_banks, prob_banks)[i % 2][0]
                    A.activation(sil[:, i % 2, :], b[:, :], ACT.Silu).then_inc(sil_ok, 1)
                elif stage == "rows":
                    T, = a
                    if T == 0:
                        eng.wait_ge(info_ok, B)
                        misc_wait(eng, ("xattn", B - 1))
                    for slot in range(TOP):
                        if T >= 1:
                            eng.wait_ge(row_sent[slot], 16 * T)
                        A.copy(row_out[:, slot, 0:D], flat[:, T, :])
                        A.copy(row_out[:, slot, D:ROW], pair_info[:, T * TOP + slot, :]).then_inc(rows_filled, 1)
            eng.wait_ge(tiles_ok, 1)
            last = nc.scalar.value_load(tile_i[0:1, 2 * MAX_TILES:2 * MAX_TILES + 1], min_val=MIN_LAST, max_val=MAX_LAST)
            groups = last + 1
            gu_b, y_b = prob_banks, misc[2:4]

            SENT = 16 * GROUP // Y_SLOTS

            def silu(j, i):
                eng.wait_ge(gu_done, i + 1)
                if not isinstance(i, int) or i >= 2:
                    eng.wait_ge(h_here, i - 1)
                A.activation(sil_in[:, j % 2, :], gu_b[j % 2][:, 0:F], ACT.Silu).then_inc(sil_here, 1)

            def weigh(q, j, i):
                eng.wait_ge(y_done, i + 1)
                if not isinstance(i, int) or i >= Y_SLOTS:
                    eng.wait_ge(y_sent[j % Y_SLOTS], q * SENT + j // Y_SLOTS * 16)
                A.activation(y_out[:, j % Y_SLOTS, :], y_b[j % 2][:, 0:D], ACT.Copy, scale=pair_w[:, j:j + 1]).then_inc(y_here, 1)

            for j in range(1, GROUP):
                silu(j - 1, j - 1)
                if j >= 3:
                    weigh(0, j - 3, j - 3)
            with eng.Fori(1, groups) as q:
                for j in range(GROUP):
                    i = q * GROUP + j
                    silu(j - 1, i - 1)
                    if j >= 3:
                        weigh(q, j - 3, i - 3)
                    else:
                        weigh(q - 1, j - 3 + GROUP, i - 3)
            end = groups * GROUP
            silu(-1, end - 1)
            for j in range(GROUP - 3, GROUP):
                weigh(last, j, last * GROUP + j)

        @block.vector
        def _(eng):
            V = nc.vector
            steps = [0]

            def then(ins):
                steps[0] += 1
                ins.then_inc(dve, 1)
                eng.wait_ge(dve, steps[0])

            def stats(kind, k):
                for t in range(TB):
                    ins = V.bn_stats(bn[:, kind, t, :], xres[:, k * TB + t, :])
                then(ins)
                for t in range(TB):
                    ins = V.bn_aggr(mv[:, kind, t, :], bn[:, kind, t, :])
                then(ins)
                V.tensor_scalar(shift[:, kind, :], mv[:, kind, :, 0], -1.0, None, ALU.mult)
                V.tensor_scalar(mv[:, kind, :, 1], mv[:, kind, :, 1], EPS, None, ALU.add).then_inc(var_ok, 1)

            for s in ORDER:
                stage, a = s[0], s[1:]
                if stage in ("ln1_stats", "ln2_stats", "ln3_stats"):
                    k, = a
                    if stage == "ln1_stats":
                        eng.wait_ge(x_in[k], 16)
                    stats(int(stage[2]) - 1, k)
                elif stage == "qk":
                    k, t = a
                    n = 2 * k + t
                    eng.wait_ge(part1_ok, n + 1)
                    b = misc_wait(eng, s)
                    if n >= 1:
                        eng.wait_ge(stk3_ok, n)
                    V.tensor_tensor(rest, b[:, :], part1, ALU.subtract).then_inc(rest_ok, 1)
                    eng.wait_ge(rest_ok, n + 1)
                    eng.sem_inc(free(s), 1)
                    V.tensor_copy(part2, rest).then_inc(part2_ok, 1)
                elif stage == "stack_parts":
                    k, t = a
                    n = 2 * k + t
                    if k >= 1:
                        misc_wait(eng, ("stack", k - 1, t, 1, 1))
                    p1 = part1.rearrange("p (x h d) -> p x h d", x=2, h=HEADS)
                    p2 = part2.rearrange("p (x h d) -> p x h d", x=2, h=HEADS)

                    def three(v):
                        return v.unsqueeze(2).to_broadcast([P, HEADS, 3, DK])

                    def two(v):
                        return v.unsqueeze(2).to_broadcast([P, HEADS, 2, DK])

                    q_, k_ = stk[t][:, 0], stk[t][:, 1]
                    V.tensor_copy(q_[:, :, 0:3, :], three(p1[:, 0]))
                    V.tensor_copy(k_[:, :, 2:5, :], three(p1[:, 1]))
                    eng.wait_ge(part2_ok, n + 1)
                    V.tensor_copy(q_[:, :, 3::2, :], two(p2[:, 0]))
                    ins = V.tensor_copy(k_[:, :, 1::4, :], two(p2[:, 1]))
                    ins.then_inc(stk_ok, 1)
                elif stage == "stack":
                    k, t, xx, half = a
                    if half == 0:
                        b = as_bf16(misc_wait(eng, s))
                        if k >= 2:
                            eng.wait_ge(probs_full, HEADS * (k - 1))
                        V.tensor_copy(stacks[k % 2][0:PARTS * DK, xx, 0:8, t * P:(t + 1) * P],
                                      b[0:PARTS * DK, :].rearrange("p (h t) -> p h t", h=8)).then_inc(stack_ok_d, 1)
                        eng.wait_ge(stack_ok_d, 4 * k + 2 * t + xx + 1)
                        eng.sem_inc(free(s), 1)
                elif stage == "scores":
                    k, h = a
                    n = k * HEADS + h
                    eng.wait_ge(scores_full, n + 1)
                    V.reduce_max(m_raw[:, h, :], score_banks[n % 2][:, 0:3 * P].rearrange("p (a b) -> p a b", a=3), AX.X) \
                        .then_inc(scores_used, 1)
                elif stage == "m_parts":
                    k, = a
                    eng.wait_ge(scores_used, HEADS * (k + 1))
                    if k >= 1:
                        misc_wait(eng, ("m_turn", k - 1))
                    V.tensor_copy(m_max[:, 0, :], m_raw[:, :, 2])
                    then(V.tensor_tensor(m_max[:, 1, :], m_raw[:, :, 0], m_raw[:, :, 1], ALU.max))
                    then(V.tensor_copy(m_part[:, :, 0, :], m_max[:, :, :]))
                    then(V.tensor_tensor(m_rest[:, :, :], m_max[:, :, :], m_part[:, :, 0, :], ALU.subtract))
                    then(V.tensor_copy(m_part[:, :, 1, :], m_rest[:, :, :]))
                    V.tensor_tensor(m_part[:, :, 2, :], m_rest[:, :, :], m_part[:, :, 1, :], ALU.subtract).then_inc(m_part_ok, 1)
                elif stage == "o_back":
                    k, t = a
                    b = misc_wait(eng, s)
                    heads = b[:, :].rearrange("p (h j) -> p h j", j=32)
                    if t == 0 and k >= 1:
                        misc_wait(eng, ("ln2_turn", k - 1))
                    then(V.reciprocal(o_rec[:, :], heads[:, :, DK]))
                    ins = V.tensor_tensor(tok[:, t, :].rearrange("p (h d) -> p h d", h=HEADS), heads[:, :, 0:DK],
                                          o_rec[:, :].unsqueeze(2).to_broadcast([P, HEADS, DK]), ALU.mult)
                    then(ins)
                    eng.sem_inc(free(s), 1)
                    if t == 1:
                        eng.sem_inc(tok_ok, 1)
                elif stage in ("wo", "xattn"):
                    k, = a
                    b = misc_wait(eng, s)
                    xs = xres[:, k * TB:(k + 1) * TB, :]
                    then(V.tensor_tensor(xs, b[:, :].rearrange("p (t n) -> p t n", t=TB), xs, ALU.add))
                    eng.sem_inc(free(s), 1)
                elif stage == "energy":
                    k, = a
                    b = misc_wait(eng, s)
                    then(V.reduce_max(e_max[:, 0:2], b[:, :].rearrange("p (t n) -> p t n", t=TB), AX.X))
                    V.tensor_scalar(e_max[:, 2:4], e_max[:, 0:2], -1.0, None, ALU.mult).then_inc(emax_ok, 1)
                elif stage == "att_scale":
                    k, = a
                    eng.wait_ge(esum_ok, k + 1)
                    V.reciprocal(e_sum[:, 2:4], e_sum[:, 0:2]).then_inc(erec_ok, 1)
                elif stage == "router":
                    k, = a
                    b = misc_wait(eng, s)
                    if k == 0:
                        eng.wait_ge(r_in, 32)
                    then(V.tensor_copy(logits[:, :, :], b[:, 0:TB * E].rearrange("p (t e) -> p t e", t=TB)))
                    eng.sem_inc(free(s), 1)
                    then(V.reduce_max(r_max[:, :], logits[:, :, :], AX.X))
                    V.tensor_scalar(r_max[:, :], r_max[:, :], -1.0, None, ALU.mult).then_inc(logits_ok, 1)
                    then(V.tensor_tensor(biased[:, :, :], logits[:, :, :], r_bias[:, :].unsqueeze(1).to_broadcast([P, TB, E]), ALU.add))
                    for t in range(TB):
                        ins = V.max(top8[:, t, :], biased[:, t, :])
                    then(ins)
                    for t in range(TB):
                        ins = V.max_index(top_i[:, t, :], top8[:, t, :], biased[:, t, :])
                    then(ins)
                    then(V.tensor_copy(top_f[:, :, :], top_i[:, :, :]))
                elif stage == "hot":
                    k, = a
                    T0 = k * TB
                    eng.wait_ge(iota_ok, 1)
                    for t in range(TB):
                        ins = V.tensor_tensor(chosen[:, T0 + t, :, :], iota_e[:, :].unsqueeze(1).to_broadcast([P, TOP, E]),
                                              top_f[:, t, 0:TOP].unsqueeze(2).to_broadcast([P, TOP, E]), ALU.is_equal)
                    then(ins)
                    eng.sem_inc(hot_ok, 1)
                elif stage == "choose":
                    k, = a
                    T0 = k * TB
                    for t in range(TB):
                        with nc.allow_low_precision(reason="sums of at most four ones"):
                            V.reduce_sum(chose[:, T0 + t, :], chosen[:, T0 + t, :, :].rearrange("p k e -> p e k"), AX.X)
                    eng.wait_ge(exp_hot_ok, k + 1)
                    V.reduce_sum(top_s[:, :, :], exp_hot, AX.X)
                    then(V.reciprocal(r_sum[:, :], r_sum[:, :]))
                    then(V.tensor_tensor(top_s[:, :, :], top_s[:, :, :], r_sum[:, :].unsqueeze(2).to_broadcast([P, TB, TOP]), ALU.mult))
                    then(V.reduce_sum(top_sum[:, :], top_s[:, :, :], AX.X))
                    then(V.reciprocal(top_sum[:, :], top_sum[:, :]))
                    then(V.tensor_tensor(pair_info[:, T0 * TOP:(T0 + TB) * TOP, 1].rearrange("p (t k) -> p t k", t=TB), top_s[:, :, :],
                                         top_sum[:, :].unsqueeze(2).to_broadcast([P, TB, TOP]), ALU.mult))
                    eng.sem_inc(chose_ok, 1)
                    eng.sem_inc(info_ok, 1)
                elif stage == "sh_up":
                    i, = a
                    tokens, j = divmod(i, HC)
                    eng.wait_ge(sil_ok, i + 1)
                    if i == HC:
                        misc_wait(eng, ("sh_down", 3))
                    b = (score_banks, prob_banks)[i % 2][1]
                    V.tensor_tensor(hid[:, j, :], b[:, :], sil[:, i % 2, :], ALU.mult).then_inc(hid_ok, 1)
                elif stage == "sh_down":
                    T, = a
                    b = misc_wait(eng, s)
                    then(V.tensor_tensor(xres[:, T, :], b[:, 0:D], xres[:, T, :], ALU.add))
                    eng.sem_inc(free(s), 1)
                    eng.sem_inc(down_done, 1)
                elif stage == "rank":
                    b = misc_wait(eng, s)
                    then(V.tensor_copy(rank_sb[:, :, :], b[:, :].rearrange("p (t e) -> p t e", t=NT)))
                    eng.sem_inc(free(s), 1)
                elif stage == "starts":
                    bi = MISC[s] % MISC_BANKS
                    b = misc[bi]
                    eng.wait_ge(count_ok, 1)
                    then(V.tensor_copy(cnt[:, 0:1], b[0:E, 0:1]))
                    then(V.tensor_scalar(cnt_i[:, :], cnt[:, 0:1], float(P - 1), None, ALU.add))
                    then(V.tensor_scalar(cnt_i[:, :], cnt_i[:, :], P.bit_length() - 1, None, ALU.arith_shift_right))
                    V.tensor_copy(cnt[:, 1:2], cnt_i[:, :])
                    then(V.tensor_scalar(wide[:, 0, :], ones[0:E, :], cnt[:, 0:1], None, ALU.mult))
                    eng.sem_inc(span_ok, 1)
                    misc_wait(eng, s)
                    then(V.tensor_copy(cnt[:, 2:4], b[0:E, 0:2]))
                    then(V.tensor_tensor(rank_sb[:, :, :], rank_sb[:, :, :],
                                         b[:, 64:64 + E].unsqueeze(1).to_broadcast([P, NT, E]), ALU.add))
                    eng.sem_inc(free(s), 1)
                    then(V.tensor_tensor(cnt[:, 4:5], cnt[:, 2:3], cnt[:, 1:2], ALU.subtract))
                    then(V.tensor_scalar(cnt[:, 5:6], cnt[:, 4:5], float(P), None, ALU.mult))
                    V.tensor_tensor(cnt[:, 6:7], cnt[:, 3:4], cnt[:, 5:6], ALU.subtract)
                    then(V.tensor_tensor(cnt[:, 7:8], cnt[:, 0:1], cnt[:, 5:6], ALU.add))
                    for i in range(2):
                        V.tensor_scalar(wide[:, 1 + i, :], ones[0:E, :], cnt[:, 6 + i:7 + i], None, ALU.mult)
                    V.tensor_scalar(in_tile[:, 0, :], iota_t[0:E, :], cnt[:, 2:3], None, ALU.is_ge)
                    then(V.tensor_scalar(in_tile[:, 1, :], iota_t[0:E, :], cnt[:, 4:5], None, ALU.is_ge))
                    then(V.tensor_tensor(in_tile[:, 1, :], in_tile[:, 1, :], in_tile[:, 0, :], ALU.subtract))
                    eng.sem_inc(span_ok, 1)
                elif stage == "tiles":
                    M = MAX_TILES
                    b = misc_wait(eng, s)
                    V.tensor_scalar(tile_i[:, 0:M], b[:, 0:M], float(E - 1), None, ALU.min)
                    V.scalar_tensor_tensor(out=tile_f[:, 0, :], in0=iota_t[:, :], scalar=float(P), in1=b[:, M:2 * M], op0=ALU.mult, op1=ALU.add)
                    V.scalar_tensor_tensor(out=tile_f[:, 1, :], in0=iota_t[:, :], scalar=-float(P), in1=b[:, 2 * M:3 * M], op0=ALU.mult, op1=ALU.add)
                    then(V.tensor_scalar(cnt_q[:, :], b[:, 3 * M:3 * M + 1], -1.0, None, ALU.add))
                    eng.sem_inc(free(s), 1)
                    V.tensor_scalar(tile_i[:, 2 * M:2 * M + 1], cnt_q[:, :], GROUP.bit_length() - 1, None, ALU.arith_shift_right)
                    V.tensor_scalar(tile_i[:, M:2 * M], tile_f[:, 0, :], float(PAIRS), None, ALU.min)
                    then(V.tensor_scalar(penalty[:, :], tile_f[:, 1, :], iota_p[:, 0:1], float(SKIPPED), ALU.is_le, ALU.mult))
                    eng.sem_inc(tiles_ok, 1)
                elif stage == "positions":
                    for T in range(NT):
                        buf = prod[:, T % 2]
                        if T >= 2:
                            eng.wait_ge(dve, steps[0])
                        then(V.tensor_tensor(buf, chosen[:, T, :, :], rank_sb[:, T, :].unsqueeze(1).to_broadcast([P, TOP, E]), ALU.mult))
                        ins = V.reduce_sum(pos_f[:, T * TOP:(T + 1) * TOP], buf, AX.X)
                        if T == NT - 1:
                            then(ins)
                    V.tensor_copy(pos_i[:, :], pos_f[:, :]).then_inc(pos_ok, 1)
            xt_b, gu_b, ht_b = score_banks, prob_banks, misc[0:2]
            last = nc.vector.value_load(tile_i[0:1, 2 * MAX_TILES:2 * MAX_TILES + 1], min_val=MIN_LAST, max_val=MAX_LAST)
            groups = last + 1

            def take_rows(q, j, i):
                eng.wait_ge(row_here[j], q * 16 + 16)
                if not isinstance(i, int):
                    eng.wait_ge(y_sent[j % Y_SLOTS], q * (16 * GROUP // Y_SLOTS) + 16 * (j // Y_SLOTS - 1))
                V.tensor_copy(pair_w[:, j:j + 1], row_in[:, j, D + 1:D + 2])
                V.tensor_tensor(pair_i[:, j:j + 1], row_in[:, j, D:D + 1], penalty[:, bass.ds(i, 1)], ALU.add).then_inc(pair_here, 1)

            def keep_turned(j, i):
                eng.wait_ge(turned, i + 1)
                V.tensor_copy(xt_in[:, j % 2, :, :], xt_b[j % 2][:, 0:2 * P].rearrange("p (c t) -> p c t", c=DC)).then_inc(xt_here, 1)

            def hidden(j, i):
                eng.wait_ge(sil_here, i + 1)
                V.tensor_tensor(h_in[:, j % 2, :], gu_b[j % 2][:, F:2 * F], sil_in[:, j % 2, :], ALU.mult).then_inc(h_here, 1)

            def keep_h(j, i):
                eng.wait_ge(h_turned, i + 1)
                if not isinstance(i, int) or i >= 2:
                    eng.wait_ge(y_done, i - 1)
                V.tensor_copy(ht_in[:, j % 2, :], ht_b[j % 2][0:F, 0:P]).then_inc(ht_here, 1)

            for j in range(GROUP):
                keep_turned(j, j)
                if j >= 1:
                    hidden(j - 1, j - 1)
                if j >= 2:
                    keep_h(j - 2, j - 2)
                take_rows(0, j, j)
            with eng.Fori(1, groups) as q:
                for j in range(GROUP):
                    i = q * GROUP + j
                    keep_turned(j, i)
                    hidden(j - 1, i - 1)
                    keep_h(j - 2, i - 2)
                    take_rows(q, j, i)
            end = groups * GROUP
            hidden(-1, end - 1)
            keep_h(-2, end - 2)
            keep_h(-1, end - 1)
            for T in range(NT):
                eng.wait_ge(y_loaded[T], 16)
                then(V.tensor_tensor(y_back[:, T, 0:2, :], y_back[:, T, 0:2, :], y_back[:, T, 2:4, :], ALU.add))
                then(V.tensor_tensor(y_back[:, T, 0, :], y_back[:, T, 0, :], y_back[:, T, 1, :], ALU.add))
                V.tensor_tensor(xres[:, T, :], xres[:, T, :], y_back[:, T, 0, :], ALU.add).then_inc(sum_ok, 1)

        @block.gpsimd
        def _(eng):
            G = nc.gpsimd
            steps = [0]

            def then(ins):
                steps[0] += 1
                ins.then_inc(pool, 1)
                eng.wait_ge(pool, steps[0])

            G.memset(neg_half[:, :], -0.5)
            then(G.memset(ident[:, :], 0.0))
            then(G.affine_select(out=ident[:, :], in_=ident[:, :], pattern=[[-1, P]], compare_op=ALU.not_equal, fill=1.0, base=0,
                                 channel_multiplier=1))
            eng.sem_inc(ident_ok, 1)

            def constants():
                G.memset(mask_b[:, :, :], 0.0)
                G.memset(ones[:, :], 1.0)
                G.memset(ones_b[:, :], 1.0)
                then(G.tensor_copy(ident_b[:, :], ident[:, :]))
                for v in v_ones:
                    then(G.memset(v[:, :, :, DK:32], 1.0))
                for st in stacks:
                    then(G.memset(st[96:99, 1, :, :], -1.0))
                then(G.memset(iota_p[:, :], 0.0))
                G.affine_select(out=mask_b[:, :, :], in_=mask_b[:, :, :], pattern=[[0, 2], [-1, P]], compare_op=ALU.is_ge, fill=MASKED, base=0,
                                channel_multiplier=1)
                then(G.affine_select(out=before_b[:, :], in_=ones_b[:, :], pattern=[[1, P]], compare_op=ALU.is_gt, fill=0.0, base=0,
                                     channel_multiplier=-1))
                G.affine_select(out=before[:, :], in_=ones[0:E, 0:E], pattern=[[1, E]], compare_op=ALU.is_gt, fill=0.0, base=0, channel_multiplier=-1)
                then(G.affine_select(out=upto[:, :], in_=ones[0:E, 0:E], pattern=[[1, E]], compare_op=ALU.is_ge, fill=0.0, base=0,
                                     channel_multiplier=-1))
                eng.sem_inc(consts, 1)

            def iotas():
                G.iota(iota_e[:, :], pattern=[[1, E]], base=0, channel_multiplier=0, allow_small_or_imprecise_dtypes=True)
                G.iota(iota_t[:, :], pattern=[[1, MAX_TILES]], base=0, channel_multiplier=0, allow_small_or_imprecise_dtypes=True)
                G.iota(iota_p[:, :], pattern=[[0, 1]], base=0, channel_multiplier=1, allow_small_or_imprecise_dtypes=True)
                then(G.iota(pair_info[:, :, 0].rearrange("p (t k) -> p t k", t=NT), pattern=[[P * TOP, NT], [1, TOP]], base=0,
                            channel_multiplier=TOP, allow_small_or_imprecise_dtypes=True))
                eng.sem_inc(iota_ok, 1)

            norm = 0
            for s in ORDER:
                stage, a = s[0], s[1:]
                if stage in ("ln1_stats", "ln2_stats", "ln3_stats"):
                    norm += 1
                    kind = int(stage[2]) - 1
                    eng.wait_ge(var_ok, norm)
                    then(G.tensor_tensor(rstd[:, kind, :], mv[:, kind, :, 1], neg_half[:, :], ALU.pow))
                    G.tensor_tensor(shift[:, kind, :], shift[:, kind, :], rstd[:, kind, :], ALU.mult).then_inc(rstd_ok, 1)
                    if norm == 1:
                        constants()
                        iotas()
                elif stage == "qk":
                    k, t = a
                    n = 2 * k + t
                    eng.wait_ge(part2_ok, n + 1)
                    if k >= 1:
                        misc_wait(eng, ("stack", k - 1, t, 1, 1))
                    r_ = rest.rearrange("p (x h d) -> p x h d", x=2, h=HEADS)
                    p2 = part2.rearrange("p (x h d) -> p x h d", x=2, h=HEADS)
                    G.tensor_tensor(stk[t][:, 0, :, 4, :], r_[:, 0], p2[:, 0], ALU.subtract)
                    G.tensor_tensor(stk[t][:, 1, :, 0, :], r_[:, 1], p2[:, 1], ALU.subtract).then_inc(stk3_ok, 1)
                elif stage == "hot":
                    k, = a
                    T0 = k * TB
                    misc_wait(eng, ("xattn", k))
                    eng.wait_ge(expd_ok, k + 1)
                    eng.wait_ge(hot_ok, k + 1)
                    for t in range(TB):
                        ins = G.tensor_tensor(exp_hot[:, t], chosen[:, T0 + t, :, :], expd[:, t, :].unsqueeze(1).to_broadcast([P, TOP, E]), ALU.mult)
                    ins.then_inc(exp_hot_ok, 1)
                elif stage == "causal":
                    k, i = a
                    eng.wait_ge(probs_used, k * HEADS + 2 * i + 2)
                    lo = (2 * i) % PT_SLOTS
                    v = pt[:, lo:lo + 2, :].rearrange("p s c -> p (s c)")[:, P:5 * P].rearrange("p (a c) -> p a c", a=4)
                    G.affine_select(out=v, in_=v, pattern=[[0, 4], [1, P]], compare_op=ALU.is_ge, fill=0.0, base=0,
                                    channel_multiplier=-1).then_inc(causal_ok, 1)
            eng.wait_ge(pos_ok, 1)
            for n in range(NT * TOP):
                slot = n % ROW_SLOTS
                eng.wait_ge(rows_filled, n + 1)
                G.indirect_dma_start(rows_dram, bass.IndirectOffsetOnAxis(pos_i[:, n:n + 1], 0), row_out[:, slot, :], None) \
                    .then_inc(row_sent[slot], 16)
            last = nc.gpsimd.value_load(tile_i[0:1, 2 * MAX_TILES:2 * MAX_TILES + 1], min_val=MIN_LAST, max_val=MAX_LAST)
            groups = last + 1

            bound = nc.gpsimd.to_reg(PAIRS - 1)

            def send(j, i):
                here = i + 1 if isinstance(i, int) else nc.gpsimd.to_reg(i + 1)
                eng.wait_ge(pos_ok, 1)
                eng.wait_ge(y_here, here)
                G.indirect_dma_start(y_dram, bass.IndirectOffsetOnAxis(pair_i[:, j:j + 1], 0), y_out[:, j % Y_SLOTS, :], None,
                                     bounds_check=bound, oob_is_err=False).then_inc(y_sent[j % Y_SLOTS], 16)

            for j in range(GROUP):
                send(j, j)
            with eng.Fori(1, groups) as q:
                for j in range(GROUP):
                    send(j, q * GROUP + j)


_INS = ['x', 'ctx_1024', 'L0_attn_Wq', 'L0_attn_Wk', 'L0_attn_Wv', 'L0_attn_Wo', 'L0_xattn_Wq', 'L0_xattn_bq', 'L0_xattn_Wk',
        'L0_xattn_bk', 'L0_ffn_router_w', 'L0_ffn_router_bias', 'L0_ffn_wg', 'L0_ffn_wu', 'L0_ffn_wd', 'L0_ffn_swg', 'L0_ffn_swu',
        'L0_ffn_swd']


def kernel(**inputs):
    import numpy as np
    import concourse.bacc as bacc
    from concourse.bass_utils import run_bass_kernel_spmd

    nc = bacc.Bacc("TRN2", target_bir_lowering=False, num_devices=1)
    arrays, args = {}, []
    for name in _INS:
        a = np.ascontiguousarray(inputs[name])
        arrays[f"in_{name}"] = a
        args.append(nc.dram_tensor(f"in_{name}", a.shape, mybir.dt.from_np(a.dtype), kind="ExternalInput").ap())
    args.append(nc.dram_tensor("out_0", arrays["in_x"].shape, F32, kind="ExternalOutput").ap())
    decoder_layer(nc, *args)
    r = run_bass_kernel_spmd(nc, [arrays], core_ids=[0])
    return r.results[0]["out_0"]
```

```python
from contextlib import ExitStack

import concourse.bass as bass
from concourse import mybir

P = 128
ALU = mybir.AluOpType
ACT = mybir.ActivationFunctionType
F32 = mybir.dt.float32
BF16 = mybir.dt.bfloat16
I32 = mybir.dt.int32
U32 = mybir.dt.uint32
AX = mybir.AxisListType

HEADS = 16
EPS = 1e-5
TOP = 4
MASKED = -1e30
PARTS = 6
MISC_BANKS = 4
GROUP = 8
Y_SLOTS = 4
PT_SLOTS = 8
SCALAR_STACKS = (1, 3, 6)
ROW_SLOTS = TOP
SKIPPED = 8192


def head(k, h):
    stages = [("probs", k, h)]
    if h % 2 == 1:
        stages.append(("causal", k, h // 2))
    if h % 4 == 2 and h > 4:
        stages.append(("pv", k, h // 4 - 1))
    return stages


def stage_order(batches):
    last = batches - 1
    order = [("ln1_stats", 0), ("ln1_apply", 0), ("x_turn", 0), ("qk", 0, 0), ("split", 0, 0), ("stack_parts", 0, 0), ("qk", 0, 1),
             ("split", 0, 1), ("v", 0), ("v_copy", 0),
             ("stack_parts", 0, 1), ("x_weights",)]
    for k in range(batches):
        for i in range(8):
            order.append(("stack", k, i // 4, i // 2 % 2, i % 2))
            if k >= 2 and i in (3, 5):
                order.append(("o_back", k - 2, i // 4))
        project = {0: [("ln1_stats", k + 1)], 2: [("ln1_apply", k + 1)], 4: [("x_turn", k + 1)], 6: [("qk", k + 1, 0)], 7: [("split", k + 1, 0)],
                   8: [("stack_parts", k + 1, 0)], 9: [("qk", k + 1, 1)], 10: [("split", k + 1, 1)], 11: [("stack_parts", k + 1, 1)]}
        context = {1: [("ctx_turn", k - 1)], 4: [("ctx_qk", k - 1)], 7: [("energy", k - 1)], 8: [("energy_max", k - 1)],
                   9: [("energy_exp", k - 1)], 11: [("att_scale", k - 1)], 13: [("att_turn", k - 1)]}
        after = {0: [("o_turn", k - 2)], 2: [("wo", k - 2)], 3: [("wo_add", k - 2), ("ln2_stats", k - 2)], 5: [("ln2_apply", k - 2)],
                 6: [("ln2_turn", k - 2)], 8: [("xattn", k - 2)], 9: [("xattn_add", k - 2), ("ln3_stats", k - 2)],
                 11: [("ln3_apply", k - 2)], 13: [("ln3_turn", k - 2)], 15: [("router", k - 2), ("top", k - 2), ("router_exp", k - 2)]}
        choice = {0: [("hot", k - 3)], 2: [("choose", k - 3)]}
        for h in range(HEADS):
            order.append(("scores", k, h))
            if k >= 1:
                order += head(k - 1, h)
            for here, stages in ((k >= 3, choice), (k >= 2, after), (k < last, project), (k >= 1, context)):
                order += stages.get(h, []) if here else []
        order.append(("m_parts", k))
        if k < last:
            order.append(("v", k + 1))
        if k >= 1:
            order.append(("pv", k - 1, HEADS // 4 - 1))
        if k < last:
            order.append(("v_copy", k + 1))
        order.append(("m_turn", k))
    a, b = last - 1, last
    order += [("ctx_turn", b), ("o_back", a, 0), ("o_back", a, 1), ("o_turn", a), ("hot", a - 1), ("ctx_qk", b)]
    after = {0: [("choose", a - 1)], 1: [("wo", a)], 2: [("wo_add", a), ("ln2_stats", a)], 3: [("energy", b)], 4: [("energy_max", b)],
             5: [("energy_exp", b)], 6: [("ln2_apply", a)], 7: [("ln2_turn", a)], 8: [("att_scale", b)], 10: [("xattn", a)],
             11: [("xattn_add", a), ("ln3_stats", a)], 12: [("att_turn", b)], 14: [("ln3_apply", a)]}
    for h in range(HEADS):
        order += head(b, h) + after.get(h, [])
    order += [("ln3_turn", a), ("pv", b, HEADS // 4 - 1), ("router", a), ("o_back", b, 0), ("o_back", b, 1), ("top", a), ("router_exp", a),
              ("o_turn", b), ("wo", b), ("sh_up", 0), ("wo_add", b), ("ln2_stats", b), ("hot", a), ("ln2_apply", b), ("sh_silu", 0),
              ("choose", a), ("sh_mul", 0), ("ln2_turn", b), ("xattn", b), ("sh_up", 1), ("xattn_add", b), ("ln3_stats", b), ("ln3_apply", b),
              ("sh_silu", 1), ("sh_mul", 1), ("ln3_turn", b), ("router", b), ("sh_up", 2), ("top", b), ("router_exp", b), ("hot", b),
              ("rank",), ("counts",), ("sh_silu", 2), ("choose", b), ("starts",)]

    def rows(*halves):
        return [("rows", i // 2, i % 2) for i in halves]

    def up(i):
        return [("sh_silu", i), ("sh_mul", i)]

    order += [("positions", 0)] + rows(0, 1) + [("sh_up", 3), ("positions", 1), ("sh_mul", 2)] + up(3) + rows(2) + [("positions", 2)]
    order += [("positions", T) for T in range(3, 8)] + rows(3, 4, 5) + [("sh_down", T) for T in range(4)] + rows(6)
    order += [("spans",), ("sh_up", 4)] + rows(7) + up(4) + [("sh_up", 5), ("tiles",)] + rows(8, 9) + up(5) + [("sh_up", 6)] + rows(10) + up(6)
    order += [("sh_up", 7)] + rows(11, 12) + up(7) + rows(13, 14, 15) + [("sh_down", T) for T in range(4, 8)]
    return order


IN_MISC = ("x_weights", "x_turn", "qk", "v", "m_turn", "ctx_turn", "ctx_qk", "stack", "energy", "att_turn",
           "o_back", "o_turn", "wo", "ln2_turn", "xattn", "ln3_turn", "router", "pv", "sh_down", "rank", "counts", "spans", "tiles")


def decoder_layer(nc, x, ctx, wq, wk, wv, wo, xwq, xbq, xwk, xbk, rw, rb, wg, wu, wd, swg, swu, swd, out):
    B, S, D = x.shape
    C = ctx.shape[2]
    E, _, F = wg.shape
    SH, _, HS = swg.shape
    DK = D // HEADS
    N = B * S
    NT = N // P
    TB = S // P
    DC = D // P
    HC = SH * HS // P
    PAIRS = N * TOP
    MAX_TILES = -(-(PAIRS // P + E) // GROUP) * GROUP
    MIN_LAST = (PAIRS // P - 1) // GROUP
    MAX_LAST = MAX_TILES // GROUP - 1
    ROW = D + 2
    SCALE = float(DK) ** -0.5
    assert TB == 2 and DC == 2 and C == P and HEADS * DK == D and F * 2 == P and D == 2 * P and HC == 4

    ORDER = stage_order(B)
    NORM = {s[0][:3] + str(s[1]): i for i, s in enumerate([s for s in ORDER if s[0].endswith("_stats")])}
    MISC = {s: i for i, s in enumerate([s for s in ORDER if s[0] in IN_MISC])}

    with ExitStack() as stack:
        def sb(name, shape, dt=F32):
            return stack.enter_context(nc.sbuf_tensor("sb_" + name, shape, dt))

        def sem(name):
            return stack.enter_context(nc.semaphore(name))

        def bank(name):
            return stack.enter_context(nc.psum_tensor("ps_" + name, [P, 512], F32))

        score_banks = [bank("s0"), bank("s1")]
        prob_banks = [bank("p0"), bank("p1")]
        misc = [bank(f"m{i}") for i in range(MISC_BANKS)]

        rows_dram = nc.dram_tensor("rows_scratch", (PAIRS + P, ROW), F32, kind="Internal").ap()
        y_dram = nc.dram_tensor("y_scratch", (PAIRS, D), F32, kind="Internal").ap()

        shared_region = sb("attention_or_down", [P, E * D])
        at = [0]

        def part(words):
            at[0] += words
            return shared_region[:, at[0] - words:at[0]]
        stacks = [part(2 * HEADS * S // 2).bitcast(BF16).rearrange("p (x h t) -> p x h t", x=2, h=HEADS) for _ in range(2)]
        pt = part(PT_SLOTS * 3 * P).rearrange("p (s c) -> p s c", s=PT_SLOTS)
        stk = [part(HEADS * PARTS * DK).bitcast(BF16).rearrange("p (x h r d) -> p x h r d", x=2, h=HEADS, r=PARTS)
               for _ in range(2)]
        v_ones = [part(TB * HEADS * 32).rearrange("p (t h j) -> p t h j", t=TB, h=HEADS) for _ in range(2)]
        down_w = shared_region[0:F, :].rearrange("p (e n) -> p e n", e=E)

        gate_up = sb("gate_up", [P, E, 2, DC * F])
        sh_g = sb("sh_g", [P, DC, SH * HS])
        sh_u = sb("sh_u", [P, DC, SH * HS])
        w_qkv = sb("w_qkv", [P, DC, 3 * D])
        wq_flat = w_qkv[:, :, :].rearrange("p c n -> p (c n)")
        sh_d = wq_flat[:, 0:HC * D].rearrange("p (j n) -> p j n", j=HC)
        w_o = sb("w_o", [P, DC, D])
        xres = sb("xres", [P, NT, D])
        flat = sb("flat", [P, NT, D])
        flat_t = sb("flat_t", [P, DC, N])
        rows_or_at = sb("rows_or_at", [P, ROW_SLOTS * ROW])
        att_t = rows_or_at[:, 0:2 * DC * S].rearrange("p (b c m) -> p b c m", b=2, c=DC)
        row_out = rows_or_at[:, :].rearrange("p (s r) -> p s r", s=ROW_SLOTS)
        chosen = sb("chosen", [P, NT, TOP, E], BF16)
        o_t = sb("o_t", [P, 4, S])
        tok = sb("tok", [P, TB, D])
        feat = sb("feat", [P, DC, S])
        early = sb("early", [P, 3 * 1024])
        part1 = early[:, 0:256].bitcast(BF16)
        part2 = early[:, 256:512].bitcast(BF16)
        rest = early[:, 512:1024]
        ctx_sb = early[:, 1024:1280].rearrange("p (t c) -> p t c", t=TB)
        ctx_t = early[:, 1280:1536]
        ctx_qk = early[:, 1536:2048].rearrange("p (x t) -> p x t", x=2)
        att = early[:, 2048:2560].rearrange("p (t n) -> p t n", t=TB)
        x_t = early[:, 2560:3072].rearrange("p (c t) -> p c t", c=DC)
        hid = early[:, 0:2048].rearrange("p (j t) -> p j t", j=HC)
        sil = early[:, 2048:3072].rearrange("p (s t) -> p s t", s=2)
        o_flat = o_t[:, :, :].rearrange("p g t -> p (g t)")
        x_w = o_flat[:, 0:2 * C].rearrange("p (x c) -> p x c", x=2)
        x_wt = sb("x_wt", [P, 2, C])
        x_bias = sb("x_bias", [P, 2])
        r_w = sb("r_w", [P, DC, E])
        r_bias = sb("r_bias", [P, E])

        ident = sb("ident", [P, P])
        ident_b = sb("ident_b", [P, P], BF16)
        mask_b = sb("mask_b", [P, 2, P], BF16)
        before_b = sb("before_b", [P, P], BF16)
        ones_b = sb("ones_b", [P, P], BF16)
        ones = sb("ones", [P, P])
        before = sb("before", [E, E])
        upto = sb("upto", [E, E])
        iota_e = sb("iota_e", [P, E])
        iota_t = sb("iota_t", [P, MAX_TILES])
        iota_p = sb("iota_p", [P, 1])
        neg_half = sb("neg_half", [P, 2])
        pair_info = sb("pair_info", [P, NT * TOP, 2])
        bn = sb("bn", [P, 3, TB, 6])
        mv = sb("mv", [P, 3, TB, 2])
        rstd = sb("rstd", [P, 3, TB])
        shift = sb("shift", [P, 3, TB])
        m_raw = sb("m_raw", [P, HEADS, 3])
        m_max = sb("m_max", [P, TB, HEADS])
        m_rest = sb("m_rest", [P, TB, HEADS])
        m_part = sb("m_part", [P, TB, 3, HEADS], BF16)
        m_t = sb("m_t", [3 * HEADS, S], BF16)
        o_rec = sb("o_rec", [P, HEADS])
        e_max = sb("e_max", [P, 4])
        e_sum = sb("e_sum", [P, 4])
        logits = sb("logits", [P, TB, E])
        biased = sb("biased", [P, TB, E])
        expd = sb("expd", [P, TB, E])
        top8 = sb("top8", [P, TB, 8])
        top_i = sb("top_i", [P, TB, 8], U32)
        top_f = sb("top_f", [P, TB, 8])
        r_max = sb("r_max", [P, 2])
        r_sum = sb("r_sum", [P, 2])
        top_s = sb("top_s", [P, TB, TOP])
        top_sum = sb("top_sum", [P, 2])
        chose = sb("chose", [P, NT, E], BF16)
        cnt = sb("cnt", [E, 8])
        cnt_i = sb("cnt_i", [E, 1], I32)
        cnt_q = sb("cnt_q", [P, 1], I32)
        wide = o_flat[0:E, 0:3 * P].rearrange("p (r c) -> p r c", r=3)
        in_tile = o_flat[0:E, 384:384 + 2 * MAX_TILES].rearrange("p (r c) -> p r c", r=2)
        tile_f = o_flat[:, 640:640 + 2 * MAX_TILES].rearrange("p (r c) -> p r c", r=2)
        penalty = sb("penalty", [P, MAX_TILES])
        tile_i = sb("tile_i", [P, 2 * MAX_TILES + 1], I32)
        pos_i = sb("pos_i", [P, NT * TOP], I32)
        prod = tok[:, :, :].rearrange("p t (k e) -> p t k e", k=TOP)
        exp_hot = wq_flat[:, 1024:1536].rearrange("p (t k e) -> p t k e", t=TB, k=TOP)
        pos_f = sb("pos_f", [P, NT * TOP])

        def row_in(j):
            return row_out[:, j, :] if j < ROW_SLOTS else early[:, (j - ROW_SLOTS) * ROW:(j - ROW_SLOTS + 1) * ROW]

        y_out = o_flat[:, 0:Y_SLOTS * D].rearrange("p (s n) -> p s n", s=Y_SLOTS)
        xt_in = wq_flat[:, 0:2 * D].rearrange("p (s c t) -> p s c t", s=2, c=DC)
        sil_in = wq_flat[:, 512:640].rearrange("p (s f) -> p s f", s=2)
        h_in = wq_flat[:, 640:768].rearrange("p (s f) -> p s f", s=2)
        ht_in = wq_flat[0:F, 768:1024].rearrange("p (s t) -> p s t", s=2)
        pair_i = sb("pair_i", [P, GROUP], I32)
        pair_w = sb("pair_w", [P, GROUP])
        y_back = gate_up[:, :, :, :].rearrange("p e x f -> p (e x f)")[:, 0:NT * TOP * D] \
            .rearrange("p (t k n) -> p t k n", t=NT, k=TOP)

        x_in = [sem(f"x_in{b}") for b in range(B)]
        qkv_in, wo_in, xw_in, xb_in, r_in, shg_in, shd_in = map(sem, ("qkv_in", "wo_in", "xw_in", "xb_in", "r_in", "shg_in", "shd_in"))
        gu_in, dw_in, tail_in = map(sem, ("gu_in", "dw_in", "tail_in"))
        ctx_in = sem("ctx_in")
        misc_full = [sem(f"misc_full{i}") for i in range(MISC_BANKS)]
        misc_free = [sem(f"misc_free{i}") for i in range(MISC_BANKS)]
        (consts, ident_ok, var_ok, rstd_ok, ln1_ok, tok_ok, feat_ok, xt_ok, part1_ok, rest_ok, part2_ok, stk_ok, stk3_ok,
         v_ok, stack_ok_d, stack_ok_a, m_part_ok, mt_ok, m_rows, dve, pool) = map(sem, (
             "consts", "ident_ok", "var_ok", "rstd_ok", "ln1_ok", "tok_ok", "feat_ok", "xt_ok", "part1_ok", "rest_ok", "part2_ok",
             "stk_ok", "stk3_ok", "v_ok", "stack_ok_d", "stack_ok_a", "m_part_ok", "mt_ok", "m_rows",
             "dve", "pool"))
        (scores_full, scores_used, probs_full, probs_used, causal_ok, pv_done, ot_ok, ctxt_ok, ctxqk_ok, emax_ok, esum_ok, att_ok,
         attt_ok, flatt_ok, logits_ok, expd_ok, chose_ok, info_ok) = map(sem, (
             "scores_full", "scores_used", "probs_full", "probs_used", "causal_ok", "pv_done", "ot_ok", "ctxt_ok", "ctxqk_ok",
             "emax_ok", "esum_ok", "att_ok", "attt_ok", "flatt_ok", "logits_ok", "expd_ok", "chose_ok", "info_ok"))
        (up_full, sil_ok, hid_ok, down_done, span_ok, tiles_ok, pos_ok, iota_ok, xwt_ok) = map(sem, (
            "up_full", "sil_ok", "hid_ok", "down_done", "span_ok", "tiles_ok", "pos_ok", "iota_ok", "xwt_ok"))
        erec_ok, hot_ok, picked_ok, exp_hot_ok = map(sem, ("erec_ok", "hot_ok", "picked_ok", "exp_hot_ok"))
        rows_filled = sem("rows_filled")
        row_sent = [sem(f"row_sent{i}") for i in range(ROW_SLOTS)]
        row_here = [sem(f"row_here{i}") for i in range(GROUP)]
        y_sent = [sem(f"y_sent{i}") for i in range(Y_SLOTS)]
        (turned, xt_here, gu_done, sil_here, h_here, h_turned, ht_here, y_done, y_here, pair_here) = map(sem, (
            "turned", "xt_here", "gu_done", "sil_here", "h_here", "h_turned", "ht_here", "y_done", "y_here", "pair_here"))
        y_loaded = [sem(f"y_loaded{T}") for T in range(NT)]
        sum_ok, stored = sem("sum_ok"), sem("stored")

        def misc_take(eng, s):
            i = MISC[s]
            if i >= MISC_BANKS:
                eng.wait_ge(misc_free[i % MISC_BANKS], i // MISC_BANKS)
            return misc[i % MISC_BANKS]

        def misc_wait(eng, s):
            i = MISC[s]
            eng.wait_ge(misc_full[i % MISC_BANKS], i // MISC_BANKS + 1)
            return misc[i % MISC_BANKS]

        def full(s):
            return misc_full[MISC[s] % MISC_BANKS]

        def free(s):
            return misc_free[MISC[s] % MISC_BANKS]

        def as_bf16(b):
            return b[:, :].bitcast(BF16)

        def key_blocks(blocks, h):
            v = blocks.rearrange("p (a c) -> p a c", a=3)
            return (v[:, 1::-1, :], v[:, 2, :]) if h % 2 == 0 else (v[:, 1:3, :], v[:, 0, :])

        block = stack.enter_context(nc.Block())
        NG = HEADS // 4

        @block.sync
        def _(sp):
            for b in range(B):
                sp.dma_start(xres[:, b * TB:(b + 1) * TB, :], x[b].rearrange("(t p) d -> p t d", p=P)).then_inc(x_in[b], 16)
                if b == 0:
                    for i, w in enumerate((wq, wk, wv)):
                        sp.dma_start(w_qkv[:, :, i * D:(i + 1) * D], w.rearrange("(c p) n -> p c n", p=P)).then_inc(qkv_in, 16)
            sp.dma_start(x_w[:, 0, :], xwq).then_inc(xw_in, 16)
            sp.dma_start(x_w[:, 1, :], xwk).then_inc(xw_in, 16)
            sp.dma_start(x_bias[:, 0:1], xbq.rearrange("(p o) -> p o", o=1)).then_inc(xb_in, 16)
            sp.dma_start(x_bias[:, 1:2], xbk.rearrange("(p o) -> p o", o=1)).then_inc(xb_in, 16)
            sp.dma_start(w_o[:, :, :], wo.rearrange("(c p) n -> p c n", p=P)).then_inc(wo_in, 16)
            sp.dma_start(r_w[:, :, :], rw.rearrange("(c p) n -> p c n", p=P)).then_inc(r_in, 16)
            sp.dma_start(r_bias[:, :], rb.rearrange("(o e) -> o e", o=1).broadcast_to([P, E])).then_inc(r_in, 16)
            for s in range(SH):
                sp.dma_start(sh_g[:, :, s * HS:(s + 1) * HS], swg[s].rearrange("(c p) h -> p c h", p=P)).then_inc(shg_in, 16)
                sp.dma_start(sh_u[:, :, s * HS:(s + 1) * HS], swu[s].rearrange("(c p) h -> p c h", p=P)).then_inc(shg_in, 16)
            late = [(e0, i, w) for e0 in range(0, E, 8) for i, w in enumerate((wg, wu))]
            loads = 0

            def load_experts(n):
                nonlocal loads
                for e0, i, w in late[loads:loads + n]:
                    sp.dma_start(gate_up[:, e0:e0 + 8, i, :], w[e0:e0 + 8].rearrange("e (p c) f -> p e (c f)", p=P)).then_inc(gu_in, 16)
                loads += n

            for s in ORDER:
                if s[0] == "m_turn":
                    b = s[1]
                    sp.wait_ge(mt_ok, b + 1)
                    load_experts(4)
                    if b == B - 1:
                        misc_wait(sp, ("v", B - 1))
                        for i in range(SH):
                            sp.dma_start(sh_d[:, i * (HS // P):(i + 1) * (HS // P), :],
                                         swd[i].rearrange("(j p) n -> p j n", p=P)).then_inc(shd_in, 16)
            sp.wait_ge(pv_done, B * NG)
            sp.wait_ge(ln1_ok, 2 * B)
            sp.dma_start(rows_dram[PAIRS:PAIRS + P, :], flat[:, :, :].rearrange("p t d -> p (t d)")[:, 0:ROW]).then_inc(tail_in, 16)
            for e0 in range(0, E, 16):
                sp.dma_start(down_w[:, e0:e0 + 16, :], wd[e0:e0 + 16].rearrange("e f n -> f e n")).then_inc(dw_in, 16)
            for i in range(ROW_SLOTS):
                sp.wait_ge(row_sent[i], 16 * NT * TOP // ROW_SLOTS)
            sp.wait_ge(tail_in, 16)
            sp.wait_ge(tiles_ok, 1)
            last = nc.sync.value_load(tile_i[0:1, 2 * MAX_TILES:2 * MAX_TILES + 1], min_val=MIN_LAST, max_val=MAX_LAST)
            groups = last + 1

            def load_rows(j, i):
                first = nc.sync.value_load(tile_i[0:1, bass.ds(i + MAX_TILES, 1)], min_val=0, max_val=PAIRS)
                if not isinstance(i, int):
                    sp.wait_ge(turned, i - GROUP + 1)
                    sp.wait_ge(pair_here, i - GROUP + 1)
                if isinstance(i, int) and i == ROW_SLOTS:
                    sp.wait_ge(down_done, NT)
                sp.dma_start(row_in(j), rows_dram[bass.ds(first, P), :]).then_inc(row_here[j], 16)

            for j in range(GROUP):
                load_rows(j, j)
            with sp.Fori(1, groups) as q:
                for j in range(GROUP):
                    load_rows(j, q * GROUP + j)
            for j in range(Y_SLOTS):
                sp.wait_ge(y_sent[j], groups * (16 * GROUP // Y_SLOTS))
            for T in range(NT):
                sp.dma_start(y_back[:, T, :, :], y_dram[T * P * TOP:(T + 1) * P * TOP, :].rearrange("(p k) n -> p k n", k=TOP)) \
                    .then_inc(y_loaded[T], 16)
            for T in range(NT):
                sp.wait_ge(sum_ok, T + 1)
                b, t = divmod(T, TB)
                sp.dma_start(out[b, t * P:(t + 1) * P, :], xres[:, T, :]).then_inc(stored, 16)
            sp.wait_ge(stored, 16 * NT)

        @block.tensor
        def _(pe):
            def turn(dst, src, idm, s, last):
                ins = pe.transpose(dst, src, idm)
                if last:
                    ins.then_inc(full(s), 1)

            def turn_feat(s, src):
                b = misc_take(pe, s)
                for c in range(DC):
                    for t in range(TB):
                        turn(b[:, (c * TB + t) * P:(c * TB + t + 1) * P], src[:, t, c * P:(c + 1) * P], ident[:, :], s,
                             c == DC - 1 and t == TB - 1)

            pe.wait_ge(ident_ok, 1)
            for s in ORDER:
                stage, a = s[0], s[1:]
                if stage == "x_weights":
                    pe.wait_ge(xw_in, 32)
                    b = misc_take(pe, s)
                    for i in range(2):
                        turn(b[:, i * P:(i + 1) * P], x_w[:, i, :], ident[:, :], s, i == 1)
                elif stage == "x_turn":
                    pe.wait_ge(ln1_ok, a[0] + 1)
                    turn_feat(s, flat[:, a[0] * TB:(a[0] + 1) * TB, :])
                elif stage == "qk":
                    k, t = a
                    if k == 0 and t == 0:
                        pe.wait_ge(qkv_in, 48)
                    pe.wait_ge(xt_ok, k + 1)
                    b = misc_take(pe, s)
                    for c in range(DC):
                        ins = pe.matmul(b[:, :], x_t[:, c, t * P:(t + 1) * P], w_qkv[:, c, 0:2 * D], start=c == 0, stop=c == DC - 1)
                    ins.then_inc(full(s), 1)
                elif stage == "v":
                    b = misc_take(pe, s)
                    for t in range(TB):
                        for c in range(DC):
                            ins = pe.matmul(b[:, t * D:(t + 1) * D], x_t[:, c, t * P:(t + 1) * P], w_qkv[:, c, 2 * D:3 * D],
                                            start=c == 0, stop=c == DC - 1)
                    ins.then_inc(full(s), 1)
                elif stage == "stack":
                    k, t, xx, half = a
                    if k == 0:
                        pe.wait_ge(consts, 1)
                    pe.wait_ge(stk_ok, 2 * k + t + 1)
                    pe.wait_ge(stk3_ok, 2 * k + t + 1)
                    b = as_bf16(misc_take(pe, s))
                    for i in range(8):
                        ins = pe.transpose(b[0:PARTS * DK, i * P:(i + 1) * P],
                                           stk[t][:, xx, half * 8 + i, :, :].rearrange("p r d -> p (r d)"), ident_b[:, :])
                    ins.then_inc(full(s), 1)
                elif stage == "scores":
                    k, h = a
                    n = k * HEADS + h
                    if h == 0:
                        pe.wait_ge(stack_ok_d, (8 - len(SCALAR_STACKS)) * (k + 1))
                        pe.wait_ge(stack_ok_a, len(SCALAR_STACKS) * (k + 1))
                    if n >= 2:
                        pe.wait_ge(scores_used, n - 1)
                    sq, b = stacks[k % 2], score_banks[n % 2]
                    R = PARTS * DK
                    pe.matmul(b[:, 0:2 * P], sq[0:R, 0, h, P:2 * P], sq[0:R, 1, h, :], start=True, stop=False, skip_group_check=True)
                    pe.matmul(b[:, 2 * P:3 * P], sq[0:R, 0, h, 0:P], sq[0:R, 1, h, 0:P], start=False, stop=False, skip_group_check=True)
                    pe.matmul(b[:, P:3 * P], ident_b[:, :], mask_b[:, :, :].rearrange("p a b -> p (a b)"),
                              start=False, stop=True, skip_group_check=True).then_inc(scores_full, 1)
                elif stage == "m_turn":
                    k, = a
                    pe.wait_ge(m_part_ok, k + 1)
                    b = as_bf16(misc_take(pe, s))
                    for t in range(TB):
                        turn(b[0:3 * HEADS, t * P:(t + 1) * P], m_part[:, t, :, :].rearrange("p r h -> p (r h)"), ident_b[:, :], s, t == 1)
                elif stage == "probs":
                    k, h = a
                    n = k * HEADS + h
                    if h == 0:
                        pe.wait_ge(m_rows, 16 * (k + 1))
                    if n >= 2:
                        pe.wait_ge(probs_used, n - 1)
                    sq, b = stacks[k % 2], prob_banks[n % 2]
                    R = PARTS * DK + 3
                    first, second = key_blocks(b[:, 0:3 * P], h)
                    pe.matmul(first, sq[0:R, 1, h, 0:P], sq[0:R, 0, h, :], start=True, stop=True, skip_group_check=True)
                    pe.matmul(second, sq[0:R, 1, h, P:2 * P], sq[0:R, 0, h, P:2 * P], start=False, stop=True,
                              skip_group_check=True).then_inc(probs_full, 1)
                elif stage == "pv":
                    k, g = a
                    pe.wait_ge(causal_ok, k * 8 + 2 * g + 2)
                    if g == 0:
                        pe.wait_ge(v_ok, k + 1)
                    b = misc_take(pe, s)
                    for j in range(4):
                        h = 4 * g + j
                        pe.matmul(b[32 * j:32 * j + 32, 0:2 * P], v_ones[k % 2][:, 0, h, :], key_blocks(pt[:, h % PT_SLOTS, :], h)[0],
                                  start=True, stop=False, skip_group_check=True)
                    for j in range(4):
                        h = 4 * g + j
                        ins = pe.matmul(b[32 * j:32 * j + 32, P:2 * P], v_ones[k % 2][:, 1, h, :], key_blocks(pt[:, h % PT_SLOTS, :], h)[1],
                                        start=False, stop=True, skip_group_check=True)
                    ins.then_inc(full(s), 1)
                elif stage == "o_back":
                    k, t = a
                    if t == 0:
                        pe.wait_ge(ot_ok, NG * (k + 1))
                    b = misc_take(pe, s)
                    for g in range(NG):
                        turn(b[:, g * P:(g + 1) * P], o_t[:, g, t * P:(t + 1) * P], ident[:, :], s, g == NG - 1)
                elif stage == "o_turn":
                    pe.wait_ge(tok_ok, 2 * a[0] + 1)
                    turn_feat(s, tok)
                elif stage == "wo":
                    k, = a
                    if k == 0:
                        pe.wait_ge(wo_in, 16)
                    pe.wait_ge(feat_ok, 2 * k + 1)
                    b = misc_take(pe, s)
                    for t in range(TB):
                        for c in range(DC):
                            ins = pe.matmul(b[:, t * D:(t + 1) * D], feat[:, c, t * P:(t + 1) * P], w_o[:, c, :], start=c == 0, stop=c == DC - 1)
                    ins.then_inc(full(s), 1)
                elif stage == "ln2_turn":
                    pe.wait_ge(tok_ok, 2 * a[0] + 2)
                    turn_feat(s, tok)
                elif stage == "ctx_turn":
                    k, = a
                    pe.wait_ge(ctx_in, 16 * (k + 1))
                    b = misc_take(pe, s)
                    for t in range(TB):
                        turn(b[:, t * P:(t + 1) * P], ctx_sb[:, t, :], ident[:, :], s, t == 1)
                elif stage == "ctx_qk":
                    k, = a
                    pe.wait_ge(ctxt_ok, k + 1)
                    if k == 0:
                        pe.wait_ge(xwt_ok, 1)
                    b = misc_take(pe, s)
                    for i in range(2):
                        ins = pe.matmul(b[:, i * S:(i + 1) * S], x_wt[:, i, :], ctx_t, start=True, stop=True)
                    ins.then_inc(full(s), 1)
                elif stage == "energy":
                    k, = a
                    pe.wait_ge(ctxqk_ok, k + 1)
                    b = misc_take(pe, s)
                    for t in range(TB):
                        ins = pe.matmul(b[:, t * S:(t + 1) * S], ctx_qk[:, 0, t * P:(t + 1) * P], ctx_qk[:, 1, :], start=True, stop=True)
                    ins.then_inc(full(s), 1)
                elif stage == "att_turn":
                    pe.wait_ge(att_ok, a[0] + 1)
                    turn_feat(s, att)
                elif stage == "xattn":
                    k, = a
                    pe.wait_ge(attt_ok, k + 1)
                    pe.wait_ge(feat_ok, 2 * k + 2)
                    b = misc_take(pe, s)
                    for t in range(TB):
                        for c in range(DC):
                            ins = pe.matmul(b[:, t * S:(t + 1) * S], feat[:, c, t * P:(t + 1) * P], att_t[:, k % 2, c, :],
                                            start=c == 0, stop=c == DC - 1)
                    ins.then_inc(full(s), 1)
                elif stage == "ln3_turn":
                    pe.wait_ge(ln1_ok, B + a[0] + 1)
                    turn_feat(s, flat[:, a[0] * TB:(a[0] + 1) * TB, :])
                elif stage == "router":
                    k, = a
                    if k == 0:
                        pe.wait_ge(r_in, 32)
                    pe.wait_ge(flatt_ok, k + 1)
                    b = misc_take(pe, s)
                    for t in range(TB):
                        T = k * TB + t
                        for c in range(DC):
                            ins = pe.matmul(b[:, t * E:(t + 1) * E], flat_t[:, c, T * P:(T + 1) * P], r_w[:, c, :], start=c == 0, stop=c == DC - 1)
                    ins.then_inc(full(s), 1)
                elif stage == "sh_up":
                    i, = a
                    tokens, j = divmod(i, HC)
                    if i == 0:
                        pe.wait_ge(shg_in, 16 * 2 * SH)
                        pe.wait_ge(scores_used, B * HEADS)
                        pe.wait_ge(probs_used, B * HEADS)
                    if i == HC:
                        pe.wait_ge(flatt_ok, B)
                    if i >= 2:
                        pe.wait_ge(hid_ok, i - 1)
                    bg, bu = (score_banks, prob_banks)[i % 2]
                    for b, w in ((bg, sh_g), (bu, sh_u)):
                        for c in range(DC):
                            ins = pe.matmul(b[:, :], w[:, c, j * P:(j + 1) * P], flat_t[:, c, tokens * 512:(tokens + 1) * 512],
                                            start=c == 0, stop=c == DC - 1)
                    ins.then_inc(up_full, 1)
                elif stage == "sh_down":
                    T, = a
                    if T == 0:
                        pe.wait_ge(shd_in, 16 * SH)
                    pe.wait_ge(hid_ok, HC * (T // 4 + 1))
                    b = misc_take(pe, s)
                    for j in range(HC):
                        ins = pe.matmul(b[:, 0:D], hid[:, j, (T % 4) * P:(T % 4 + 1) * P], sh_d[:, j, :], start=j == 0, stop=j == HC - 1)
                    ins.then_inc(full(s), 1)
                elif stage == "rank":
                    pe.wait_ge(picked_ok, B)
                    b = misc_take(pe, s)
                    for T in range(NT):
                        pe.matmul(b[:, T * E:(T + 1) * E], before_b[:, :], chose[:, T, :], start=T == 0, stop=False, skip_group_check=True)
                        for T2 in range(T):
                            pe.matmul(b[:, T * E:(T + 1) * E], ones_b[:, :], chose[:, T2, :], start=False, stop=False, skip_group_check=True)
                elif stage == "counts":
                    b = misc_take(pe, s)
                    for T in range(NT):
                        ins = pe.matmul(b[0:E, 0:1], chose[:, T, :], ones_b[:, 0:1], start=T == 0, stop=T == NT - 1)
                    ins.then_inc(full(s), 1)
                elif stage == "starts":
                    pe.wait_ge(span_ok, 1)
                    b = misc[MISC[("rank",)] % MISC_BANKS]
                    pe.matmul(b[:, :], wide[:, 0, :], before[:, :].unsqueeze(1).to_broadcast([E, NT, E]), start=False, stop=True,
                              skip_group_check=True).then_inc(full(("rank",)), 1)
                elif stage == "spans":
                    pe.wait_ge(span_ok, 2)
                    b = misc_take(pe, s)
                    pe.matmul(b[0:E, 0:1], upto[:, :], cnt[:, 1:2], start=True, stop=True)
                    pe.matmul(b[0:E, 1:2], before[:, :], cnt[:, 0:1], start=True, stop=True).then_inc(full(s), 1)
                elif stage == "tiles":
                    pe.wait_ge(span_ok, 3)
                    b = misc_take(pe, s)
                    M = MAX_TILES
                    pe.matmul(b[:, 0:M], ones[0:E, :], in_tile[:, 0, :], start=True, stop=True)
                    pe.matmul(b[:, M:2 * M], wide[:, 1, :], in_tile[:, 1, :], start=True, stop=True)
                    pe.matmul(b[:, 2 * M:3 * M], wide[:, 2, :], in_tile[:, 1, :], start=True, stop=True)
                    pe.matmul(b[:, 3 * M:3 * M + 1], ones[0:E, :], cnt[:, 1:2], start=True, stop=True).then_inc(full(s), 1)

            pe.wait_ge(tiles_ok, 1)
            for i in range(MISC_BANKS):
                pe.wait_ge(misc_free[i], len([u for u in MISC.values() if u % MISC_BANKS == i]))
            pe.wait_ge(hid_ok, 2 * HC)
            pe.wait_ge(gu_in, 16 * 2 * (E // 8))
            pe.wait_ge(dw_in, 16 * (E // 16))
            last = nc.tensor.value_load(tile_i[0:1, 2 * MAX_TILES:2 * MAX_TILES + 1], min_val=MIN_LAST, max_val=MAX_LAST)
            groups = last + 1
            xt_b, gu_b, ht_b, y_b = score_banks, prob_banks, misc[0:2], misc[2:4]

            expert = [nc.tensor.alloc_register(f"expert_{j}") for j in range(GROUP)]

            def read_expert(j, i):
                nc.tensor.reg_load(expert[j], tile_i[0:1, bass.ds(i, 1)])

            def expert_of(j):
                return nc.tensor.snap(expert[j], min_val=0, max_val=E - 1)

            def turn_rows(q, j, i):
                pe.wait_ge(row_here[j], q * 16 + 16)
                rows = row_in(j)[:, 0:D].rearrange("p (m c) -> p c m", c=DC)
                pe.transpose(xt_b[j % 2][:, 0:P], rows[:, 0, :], ident[:, :])
                pe.transpose(xt_b[j % 2][:, P:2 * P], rows[:, 1, :], ident[:, :]).then_inc(turned, 1)

            def gate_and_up(j, i):
                e = expert_of(j)
                pe.wait_ge(xt_here, i + 1)
                b = gu_b[j % 2]
                for c in range(DC):
                    ins = pe.matmul(b[:, 0:2 * F], xt_in[:, j % 2, c, :], gate_up[:, bass.ds(e, 1), :, c * F:(c + 1) * F],
                                    start=c == 0, stop=c == DC - 1)
                ins.then_inc(gu_done, 1)

            def turn_h(j, i):
                here = i + 1 if isinstance(i, int) else nc.tensor.to_reg(i + 1)
                pe.wait_ge(tiles_ok, 1)
                pe.wait_ge(h_here, here)
                pe.transpose(ht_b[j % 2][0:F, 0:P], h_in[:, j % 2, :], ident[:, :]).then_inc(h_turned, 1)

            def down(j, i):
                e = expert_of(j)
                pe.wait_ge(ht_here, i + 1)
                if not isinstance(i, int) or i >= 2:
                    pe.wait_ge(y_here, i - 1)
                pe.matmul(y_b[j % 2][:, 0:D], ht_in[:, j % 2, :], down_w[:, bass.ds(e, 1), :], start=True, stop=True).then_inc(y_done, 1)

            for j in range(GROUP):
                read_expert(j, j)
                turn_rows(0, j, j)
                if j >= 1:
                    gate_and_up(j - 1, j - 1)
                if j >= 2:
                    turn_h(j - 2, j - 2)
                if j >= 3:
                    down(j - 3, j - 3)
            with pe.Fori(1, groups) as q:
                for j in range(GROUP):
                    i = q * GROUP + j
                    read_expert(j, i)
                    turn_rows(q, j, i)
                    gate_and_up(j - 1, i - 1)
                    turn_h(j - 2, i - 2)
                    down(j - 3, i - 3)
            end = groups * GROUP
            gate_and_up(-1, end - 1)
            turn_h(-2, end - 2)
            down(-3, end - 3)
            turn_h(-1, end - 1)
            down(-2, end - 2)
            down(-1, end - 1)

        @block.scalar
        def _(eng):
            A = nc.scalar

            def load_context(b_):
                eng.dma_start(ctx_sb, ctx[b_].rearrange("(t p) c -> p t c", p=P)).then_inc(ctx_in, 16)

            load_context(0)
            for s in ORDER:
                stage, a = s[0], s[1:]
                if stage in ("ln1_apply", "ln2_apply", "ln3_apply"):
                    k, = a
                    kind = int(stage[2]) - 1
                    eng.wait_ge(rstd_ok, NORM[stage[:3] + str(k)] + 1)
                    dst, done = (tok, tok_ok) if kind == 1 else (flat[:, k * TB:(k + 1) * TB, :], ln1_ok)
                    for t in range(TB):
                        ins = A.activation(dst[:, t, :], xres[:, k * TB + t, :], ACT.Identity, bias=shift[:, kind, t:t + 1],
                                           scale=rstd[:, kind, t:t + 1])
                    ins.then_inc(done, 1)
                if stage == "x_weights":
                    b = misc_wait(eng, s)
                    A.copy(x_wt[:, :, :], b[:, 0:2 * C].rearrange("p (x c) -> p x c", x=2)).then_inc(xwt_ok, 1)
                    eng.wait_ge(xwt_ok, 1)
                    eng.sem_inc(free(s), 1)
                elif stage == "x_turn":
                    k, = a
                    b = misc_wait(eng, s)
                    if k >= 1:
                        misc_wait(eng, ("v", k - 1))
                    A.copy(x_t, b[:, :].rearrange("p (c t) -> p c t", c=DC)).then_inc(xt_ok, 1)
                    eng.wait_ge(xt_ok, k + 1)
                    eng.sem_inc(free(s), 1)
                elif stage == "qk":
                    k, t = a
                    b = misc_wait(eng, s)
                    n = 2 * k + t
                    if n >= 1:
                        eng.wait_ge(stk_ok, n)
                    A.copy(part1, b[:, :]).then_inc(part1_ok, 1)
                elif stage == "v_copy":
                    k, = a
                    b = misc_wait(eng, ("v", k))
                    if k >= 2:
                        eng.wait_ge(pv_done, NG * (k - 1))
                    if k == 0:
                        eng.wait_ge(consts, 1)
                    A.copy(v_ones[k % 2][:, :, :, 0:DK], b[:, :].rearrange("p (t h d) -> p t h d", t=TB, h=HEADS)).then_inc(v_ok, 1)
                    eng.wait_ge(v_ok, k + 1)
                    eng.sem_inc(free(("v", k)), 1)
                elif stage == "stack":
                    k, t, xx, half = a
                    i = 4 * t + 2 * xx + half
                    if i in SCALAR_STACKS:
                        b = as_bf16(misc_wait(eng, s))
                        if k >= 2:
                            eng.wait_ge(probs_full, HEADS * (k - 1))
                        A.copy(stacks[k % 2][0:PARTS * DK, xx, 8 * half:8 * half + 8, t * P:(t + 1) * P],
                               b[0:PARTS * DK, :].rearrange("p (h t) -> p h t", h=8)).then_inc(stack_ok_a, 1)
                        eng.wait_ge(stack_ok_a, len(SCALAR_STACKS) * k + SCALAR_STACKS.index(i) + 1)
                        eng.sem_inc(free(s), 1)
                elif stage == "m_turn":
                    k, = a
                    b = as_bf16(misc_wait(eng, s))
                    if k >= 1:
                        eng.wait_ge(m_rows, 16 * k)
                    A.copy(m_t[:, :], b[0:3 * HEADS, 0:S]).then_inc(mt_ok, 1)
                    eng.wait_ge(mt_ok, k + 1)
                    eng.sem_inc(free(s), 1)
                    eng.dma_start(stacks[k % 2][96:99, 0, :, :], m_t[:, :]).then_inc(m_rows, 16)
                elif stage == "probs":
                    k, h = a
                    n = k * HEADS + h
                    eng.wait_ge(probs_full, n + 1)
                    if n >= PT_SLOTS:
                        eng.wait_ge(pv_done, (n - PT_SLOTS) // 4 + 1)
                    A.activation(pt[:, h % PT_SLOTS, :], prob_banks[n % 2][:, 0:3 * P], ACT.Exp, scale=SCALE).then_inc(probs_used, 1)
                elif stage == "pv":
                    k, g = a
                    b = misc_wait(eng, s)
                    eng.sem_inc(pv_done, 1)
                    if g == 0 and k >= 1:
                        misc_wait(eng, ("o_back", k - 1, 1))
                    A.copy(o_t[:, g, :], b[:, 0:S]).then_inc(ot_ok, 1)
                    eng.wait_ge(ot_ok, NG * k + g + 1)
                    eng.sem_inc(free(s), 1)
                elif stage in ("o_turn", "ln2_turn"):
                    k, = a
                    b = misc_wait(eng, s)
                    n = 2 * k + (stage == "ln2_turn") + 1
                    if n >= 2:
                        misc_wait(eng, ("wo", k) if stage == "ln2_turn" else ("xattn", k - 1))
                    A.copy(feat[:, :, :], b[:, :].rearrange("p (c t) -> p c t", c=DC)).then_inc(feat_ok, 1)
                    eng.wait_ge(feat_ok, n)
                    eng.sem_inc(free(s), 1)
                elif stage == "ctx_turn":
                    k, = a
                    b = misc_wait(eng, s)
                    if k >= 1:
                        misc_wait(eng, ("ctx_qk", k - 1))
                    A.copy(ctx_t, b[:, 0:S]).then_inc(ctxt_ok, 1)
                    eng.wait_ge(ctxt_ok, k + 1)
                    eng.sem_inc(free(s), 1)
                    if k + 1 < B:
                        load_context(k + 1)
                elif stage == "ctx_qk":
                    k, = a
                    if k == 0:
                        eng.wait_ge(xb_in, 32)
                    b = misc_wait(eng, s)
                    if k >= 1:
                        misc_wait(eng, ("energy", k - 1))
                    A.activation(ctx_qk[:, 0, :], b[:, 0:S], ACT.Identity, bias=x_bias[:, 0:1])
                    A.activation(ctx_qk[:, 1, :], b[:, S:2 * S], ACT.Identity, bias=x_bias[:, 1:2]).then_inc(ctxqk_ok, 1)
                    eng.wait_ge(ctxqk_ok, k + 1)
                    eng.sem_inc(free(s), 1)
                elif stage == "energy_exp":
                    k, = a
                    eng.wait_ge(emax_ok, k + 1)
                    b = misc_wait(eng, ("energy", k))
                    if k >= 1:
                        misc_wait(eng, ("att_turn", k - 1))
                    for t in range(TB):
                        ins = A.activation(att[:, t, :], b[:, t * S:(t + 1) * S], ACT.Exp, bias=e_max[:, 2 + t:3 + t],
                                           accum_out=e_sum[:, t:t + 1])
                    ins.then_inc(esum_ok, 1)
                    eng.wait_ge(esum_ok, k + 1)
                    eng.sem_inc(free(("energy", k)), 1)
                elif stage == "att_scale":
                    k, = a
                    eng.wait_ge(erec_ok, k + 1)
                    for t in range(TB):
                        ins = A.activation(att[:, t, :], att[:, t, :], ACT.Copy, scale=e_sum[:, 2 + t:3 + t])
                    ins.then_inc(att_ok, 1)
                elif stage == "att_turn":
                    k, = a
                    b = misc_wait(eng, s)
                    if k >= 2:
                        misc_wait(eng, ("xattn", k - 2))
                    A.copy(att_t[:, k % 2, :, :], b[:, :].rearrange("p (c m) -> p c m", c=DC)).then_inc(attt_ok, 1)
                    eng.wait_ge(attt_ok, k + 1)
                    eng.sem_inc(free(s), 1)
                elif stage == "ln3_turn":
                    k, = a
                    b = misc_wait(eng, s)
                    A.copy(flat_t[:, :, k * S:(k + 1) * S], b[:, :].rearrange("p (c t) -> p c t", c=DC)).then_inc(flatt_ok, 1)
                    eng.wait_ge(flatt_ok, k + 1)
                    eng.sem_inc(free(s), 1)
                elif stage == "router_exp":
                    k, = a
                    eng.wait_ge(logits_ok, k + 1)
                    if k >= 1:
                        eng.wait_ge(chose_ok, k)
                    for t in range(TB):
                        ins = A.activation(expd[:, t, :], logits[:, t, :], ACT.Exp, bias=r_max[:, t:t + 1], accum_out=r_sum[:, t:t + 1])
                    ins.then_inc(expd_ok, 1)
                elif stage == "sh_silu":
                    i, = a
                    eng.wait_ge(up_full, i + 1)
                    if i >= 2:
                        eng.wait_ge(hid_ok, i - 1)
                    b = (score_banks, prob_banks)[i % 2][0]
                    A.activation(sil[:, i % 2, :], b[:, :], ACT.Silu).then_inc(sil_ok, 1)
                elif stage == "rows":
                    T, half = a
                    if T == 0:
                        eng.wait_ge(info_ok, B)
                        misc_wait(eng, ("xattn", B - 1))
                    for slot in range(2 * half, 2 * half + 2):
                        if T >= 1:
                            eng.wait_ge(row_sent[slot], 16 * T)
                        A.copy(row_out[:, slot, 0:D], flat[:, T, :])
                        A.copy(row_out[:, slot, D:ROW], pair_info[:, T * TOP + slot, :]).then_inc(rows_filled, 1)
            eng.wait_ge(tiles_ok, 1)
            last = nc.scalar.value_load(tile_i[0:1, 2 * MAX_TILES:2 * MAX_TILES + 1], min_val=MIN_LAST, max_val=MAX_LAST)
            groups = last + 1
            gu_b, y_b = prob_banks, misc[2:4]

            SENT = 16 * GROUP // Y_SLOTS

            def silu(j, i):
                eng.wait_ge(gu_done, i + 1)
                if not isinstance(i, int) or i >= 2:
                    eng.wait_ge(h_here, i - 1)
                A.activation(sil_in[:, j % 2, :], gu_b[j % 2][:, 0:F], ACT.Silu).then_inc(sil_here, 1)

            def weigh(q, j, i):
                eng.wait_ge(y_done, i + 1)
                if not isinstance(i, int) or i >= Y_SLOTS:
                    eng.wait_ge(y_sent[j % Y_SLOTS], q * SENT + j // Y_SLOTS * 16)
                A.activation(y_out[:, j % Y_SLOTS, :], y_b[j % 2][:, 0:D], ACT.Copy, scale=pair_w[:, j:j + 1]).then_inc(y_here, 1)

            for j in range(1, GROUP):
                silu(j - 1, j - 1)
                if j >= 3:
                    weigh(0, j - 3, j - 3)
            with eng.Fori(1, groups) as q:
                for j in range(GROUP):
                    i = q * GROUP + j
                    silu(j - 1, i - 1)
                    if j >= 3:
                        weigh(q, j - 3, i - 3)
                    else:
                        weigh(q - 1, j - 3 + GROUP, i - 3)
            end = groups * GROUP
            silu(-1, end - 1)
            for j in range(GROUP - 3, GROUP):
                weigh(last, j, last * GROUP + j)

        @block.vector
        def _(eng):
            V = nc.vector
            steps = [0]

            def then(ins):
                steps[0] += 1
                ins.then_inc(dve, 1)
                eng.wait_ge(dve, steps[0])

            def stats(kind, k):
                for t in range(TB):
                    ins = V.bn_stats(bn[:, kind, t, :], xres[:, k * TB + t, :])
                then(ins)
                for t in range(TB):
                    ins = V.bn_aggr(mv[:, kind, t, :], bn[:, kind, t, :])
                then(ins)
                V.tensor_scalar(shift[:, kind, :], mv[:, kind, :, 0], -1.0, None, ALU.mult)
                V.tensor_scalar(mv[:, kind, :, 1], mv[:, kind, :, 1], EPS, None, ALU.add).then_inc(var_ok, 1)

            for s in ORDER:
                stage, a = s[0], s[1:]
                if stage in ("ln1_stats", "ln2_stats", "ln3_stats"):
                    k, = a
                    if stage == "ln1_stats":
                        eng.wait_ge(x_in[k], 16)
                    stats(int(stage[2]) - 1, k)
                elif stage == "split":
                    k, t = a
                    n = 2 * k + t
                    eng.wait_ge(part1_ok, n + 1)
                    b = misc_wait(eng, ("qk", k, t))
                    if n >= 1:
                        eng.wait_ge(stk3_ok, n)
                    V.tensor_tensor(rest, b[:, :], part1, ALU.subtract).then_inc(rest_ok, 1)
                    eng.wait_ge(rest_ok, n + 1)
                    eng.sem_inc(free(("qk", k, t)), 1)
                    V.tensor_copy(part2, rest).then_inc(part2_ok, 1)
                elif stage == "stack_parts":
                    k, t = a
                    n = 2 * k + t
                    if k >= 1:
                        misc_wait(eng, ("stack", k - 1, t, 1, 1))
                    p1 = part1.rearrange("p (x h d) -> p x h d", x=2, h=HEADS)
                    p2 = part2.rearrange("p (x h d) -> p x h d", x=2, h=HEADS)

                    def three(v):
                        return v.unsqueeze(2).to_broadcast([P, HEADS, 3, DK])

                    def two(v):
                        return v.unsqueeze(2).to_broadcast([P, HEADS, 2, DK])

                    q_, k_ = stk[t][:, 0], stk[t][:, 1]
                    V.tensor_copy(q_[:, :, 0:3, :], three(p1[:, 0]))
                    V.tensor_copy(k_[:, :, 2:5, :], three(p1[:, 1]))
                    eng.wait_ge(part2_ok, n + 1)
                    V.tensor_copy(q_[:, :, 3::2, :], two(p2[:, 0]))
                    ins = V.tensor_copy(k_[:, :, 1::4, :], two(p2[:, 1]))
                    ins.then_inc(stk_ok, 1)
                elif stage == "stack":
                    k, t, xx, half = a
                    i = 4 * t + 2 * xx + half
                    if i not in SCALAR_STACKS:
                        b = as_bf16(misc_wait(eng, s))
                        if k >= 2:
                            eng.wait_ge(probs_full, HEADS * (k - 1))
                        V.tensor_copy(stacks[k % 2][0:PARTS * DK, xx, 8 * half:8 * half + 8, t * P:(t + 1) * P],
                                      b[0:PARTS * DK, :].rearrange("p (h t) -> p h t", h=8)).then_inc(stack_ok_d, 1)
                        mine = [n for n in range(8) if n not in SCALAR_STACKS]
                        eng.wait_ge(stack_ok_d, len(mine) * k + mine.index(i) + 1)
                        eng.sem_inc(free(s), 1)
                elif stage == "scores":
                    k, h = a
                    n = k * HEADS + h
                    eng.wait_ge(scores_full, n + 1)
                    V.reduce_max(m_raw[:, h, :], score_banks[n % 2][:, 0:3 * P].rearrange("p (a b) -> p a b", a=3), AX.X) \
                        .then_inc(scores_used, 1)
                elif stage == "m_parts":
                    k, = a
                    eng.wait_ge(scores_used, HEADS * (k + 1))
                    if k >= 1:
                        misc_wait(eng, ("m_turn", k - 1))
                    V.tensor_copy(m_max[:, 0, :], m_raw[:, :, 2])
                    then(V.tensor_tensor(m_max[:, 1, :], m_raw[:, :, 0], m_raw[:, :, 1], ALU.max))
                    then(V.tensor_copy(m_part[:, :, 0, :], m_max[:, :, :]))
                    then(V.tensor_tensor(m_rest[:, :, :], m_max[:, :, :], m_part[:, :, 0, :], ALU.subtract))
                    then(V.tensor_copy(m_part[:, :, 1, :], m_rest[:, :, :]))
                    V.tensor_tensor(m_part[:, :, 2, :], m_rest[:, :, :], m_part[:, :, 1, :], ALU.subtract).then_inc(m_part_ok, 1)
                elif stage == "o_back":
                    k, t = a
                    b = misc_wait(eng, s)
                    heads = b[:, :].rearrange("p (h j) -> p h j", j=32)
                    if t == 0 and k >= 1:
                        misc_wait(eng, ("ln2_turn", k - 1))
                    then(V.reciprocal(o_rec[:, :], heads[:, :, DK]))
                    ins = V.tensor_tensor(tok[:, t, :].rearrange("p (h d) -> p h d", h=HEADS), heads[:, :, 0:DK],
                                          o_rec[:, :].unsqueeze(2).to_broadcast([P, HEADS, DK]), ALU.mult)
                    then(ins)
                    eng.sem_inc(free(s), 1)
                    if t == 1:
                        eng.sem_inc(tok_ok, 1)
                elif stage in ("wo_add", "xattn_add"):
                    k, = a
                    product = (stage[:-4], k)
                    b = misc_wait(eng, product)
                    xs = xres[:, k * TB:(k + 1) * TB, :]
                    then(V.tensor_tensor(xs, b[:, :].rearrange("p (t n) -> p t n", t=TB), xs, ALU.add))
                    eng.sem_inc(free(product), 1)
                elif stage == "energy_max":
                    k, = a
                    b = misc_wait(eng, ("energy", k))
                    then(V.reduce_max(e_max[:, 0:2], b[:, :].rearrange("p (t n) -> p t n", t=TB), AX.X))
                    V.tensor_scalar(e_max[:, 2:4], e_max[:, 0:2], -1.0, None, ALU.mult).then_inc(emax_ok, 1)
                elif stage == "att_scale":
                    k, = a
                    eng.wait_ge(esum_ok, k + 1)
                    V.reciprocal(e_sum[:, 2:4], e_sum[:, 0:2]).then_inc(erec_ok, 1)
                elif stage == "top":
                    k, = a
                    b = misc_wait(eng, ("router", k))
                    if k == 0:
                        eng.wait_ge(r_in, 32)
                    then(V.tensor_copy(logits[:, :, :], b[:, 0:TB * E].rearrange("p (t e) -> p t e", t=TB)))
                    eng.sem_inc(free(("router", k)), 1)
                    then(V.reduce_max(r_max[:, :], logits[:, :, :], AX.X))
                    V.tensor_scalar(r_max[:, :], r_max[:, :], -1.0, None, ALU.mult).then_inc(logits_ok, 1)
                    then(V.tensor_tensor(biased[:, :, :], logits[:, :, :], r_bias[:, :].unsqueeze(1).to_broadcast([P, TB, E]), ALU.add))
                    for t in range(TB):
                        ins = V.max(top8[:, t, :], biased[:, t, :])
                    then(ins)
                    for t in range(TB):
                        ins = V.max_index(top_i[:, t, :], top8[:, t, :], biased[:, t, :])
                    then(ins)
                    then(V.tensor_copy(top_f[:, :, :], top_i[:, :, :]))
                elif stage == "hot":
                    k, = a
                    T0 = k * TB
                    eng.wait_ge(iota_ok, 1)
                    for t in range(TB):
                        ins = V.tensor_tensor(chosen[:, T0 + t, :, :], iota_e[:, :].unsqueeze(1).to_broadcast([P, TOP, E]),
                                              top_f[:, t, 0:TOP].unsqueeze(2).to_broadcast([P, TOP, E]), ALU.is_equal)
                    then(ins)
                    eng.sem_inc(hot_ok, 1)
                    for t in range(TB):
                        with nc.allow_low_precision(reason="sums of at most four ones"):
                            ins = V.reduce_sum(chose[:, T0 + t, :], chosen[:, T0 + t, :, :].rearrange("p k e -> p e k"), AX.X)
                    ins.then_inc(picked_ok, 1)
                elif stage == "choose":
                    k, = a
                    T0 = k * TB
                    eng.wait_ge(exp_hot_ok, k + 1)
                    V.reduce_sum(top_s[:, :, :], exp_hot, AX.X)
                    then(V.reciprocal(r_sum[:, :], r_sum[:, :]))
                    then(V.tensor_tensor(top_s[:, :, :], top_s[:, :, :], r_sum[:, :].unsqueeze(2).to_broadcast([P, TB, TOP]), ALU.mult))
                    then(V.reduce_sum(top_sum[:, :], top_s[:, :, :], AX.X))
                    then(V.reciprocal(top_sum[:, :], top_sum[:, :]))
                    then(V.tensor_tensor(pair_info[:, T0 * TOP:(T0 + TB) * TOP, 1].rearrange("p (t k) -> p t k", t=TB), top_s[:, :, :],
                                         top_sum[:, :].unsqueeze(2).to_broadcast([P, TB, TOP]), ALU.mult))
                    eng.sem_inc(chose_ok, 1)
                    eng.sem_inc(info_ok, 1)
                elif stage == "sh_mul":
                    i, = a
                    tokens, j = divmod(i, HC)
                    eng.wait_ge(sil_ok, i + 1)
                    if i == HC:
                        misc_wait(eng, ("sh_down", 3))
                    b = (score_banks, prob_banks)[i % 2][1]
                    V.tensor_tensor(hid[:, j, :], b[:, :], sil[:, i % 2, :], ALU.mult).then_inc(hid_ok, 1)
                elif stage == "sh_down":
                    T, = a
                    b = misc_wait(eng, s)
                    then(V.tensor_tensor(xres[:, T, :], b[:, 0:D], xres[:, T, :], ALU.add))
                    eng.sem_inc(free(s), 1)
                    eng.sem_inc(down_done, 1)
                elif stage == "counts":
                    b = misc_wait(eng, s)
                    then(V.tensor_copy(cnt[:, 0:1], b[0:E, 0:1]))
                    eng.sem_inc(free(s), 1)
                    then(V.tensor_scalar(wide[:, 0, :], ones[0:E, :], cnt[:, 0:1], None, ALU.mult))
                    eng.sem_inc(span_ok, 1)
                    then(V.tensor_scalar(cnt_i[:, :], cnt[:, 0:1], float(P - 1), None, ALU.add))
                    then(V.tensor_scalar(cnt_i[:, :], cnt_i[:, :], P.bit_length() - 1, None, ALU.arith_shift_right))
                    then(V.tensor_copy(cnt[:, 1:2], cnt_i[:, :]))
                    eng.sem_inc(span_ok, 1)
                elif stage == "spans":
                    b = misc_wait(eng, s)
                    then(V.tensor_copy(cnt[:, 2:4], b[0:E, 0:2]))
                    eng.sem_inc(free(s), 1)
                    then(V.tensor_tensor(cnt[:, 4:5], cnt[:, 2:3], cnt[:, 1:2], ALU.subtract))
                    then(V.tensor_scalar(cnt[:, 5:6], cnt[:, 4:5], float(P), None, ALU.mult))
                    V.tensor_tensor(cnt[:, 6:7], cnt[:, 3:4], cnt[:, 5:6], ALU.subtract)
                    then(V.tensor_tensor(cnt[:, 7:8], cnt[:, 0:1], cnt[:, 5:6], ALU.add))
                    for i in range(2):
                        V.tensor_scalar(wide[:, 1 + i, :], ones[0:E, :], cnt[:, 6 + i:7 + i], None, ALU.mult)
                    V.tensor_scalar(in_tile[:, 0, :], iota_t[0:E, :], cnt[:, 2:3], None, ALU.is_ge)
                    then(V.tensor_scalar(in_tile[:, 1, :], iota_t[0:E, :], cnt[:, 4:5], None, ALU.is_ge))
                    then(V.tensor_tensor(in_tile[:, 1, :], in_tile[:, 1, :], in_tile[:, 0, :], ALU.subtract))
                    eng.sem_inc(span_ok, 1)
                elif stage == "tiles":
                    M = MAX_TILES
                    b = misc_wait(eng, s)
                    V.tensor_scalar(tile_i[:, 0:M], b[:, 0:M], float(E - 1), None, ALU.min)
                    V.scalar_tensor_tensor(out=tile_f[:, 0, :], in0=iota_t[:, :], scalar=float(P), in1=b[:, M:2 * M], op0=ALU.mult, op1=ALU.add)
                    V.scalar_tensor_tensor(out=tile_f[:, 1, :], in0=iota_t[:, :], scalar=-float(P), in1=b[:, 2 * M:3 * M], op0=ALU.mult, op1=ALU.add)
                    then(V.tensor_scalar(cnt_q[:, :], b[:, 3 * M:3 * M + 1], -1.0, None, ALU.add))
                    eng.sem_inc(free(s), 1)
                    V.tensor_scalar(tile_i[:, 2 * M:2 * M + 1], cnt_q[:, :], GROUP.bit_length() - 1, None, ALU.arith_shift_right)
                    V.tensor_scalar(tile_i[:, M:2 * M], tile_f[:, 0, :], float(PAIRS), None, ALU.min)
                    then(V.tensor_scalar(penalty[:, :], tile_f[:, 1, :], iota_p[:, 0:1], float(SKIPPED), ALU.is_le, ALU.mult))
                    eng.sem_inc(tiles_ok, 1)
                elif stage == "positions":
                    T, = a
                    rank_b = misc_wait(eng, ("rank",))
                    buf = prod[:, T % 2]
                    then(V.tensor_tensor(buf, chosen[:, T, :, :], rank_b[:, T * E:(T + 1) * E].unsqueeze(1).to_broadcast([P, TOP, E]), ALU.mult))
                    if T == NT - 1:
                        eng.sem_inc(free(("rank",)), 1)
                    then(V.reduce_sum(pos_f[:, T * TOP:(T + 1) * TOP], buf, AX.X))
                    V.tensor_copy(pos_i[:, T * TOP:(T + 1) * TOP], pos_f[:, T * TOP:(T + 1) * TOP]).then_inc(pos_ok, 1)
            xt_b, gu_b, ht_b = score_banks, prob_banks, misc[0:2]
            last = nc.vector.value_load(tile_i[0:1, 2 * MAX_TILES:2 * MAX_TILES + 1], min_val=MIN_LAST, max_val=MAX_LAST)
            groups = last + 1

            def take_rows(q, j, i):
                eng.wait_ge(row_here[j], q * 16 + 16)
                if not isinstance(i, int):
                    eng.wait_ge(y_sent[j % Y_SLOTS], q * (16 * GROUP // Y_SLOTS) + 16 * (j // Y_SLOTS - 1))
                V.tensor_copy(pair_w[:, j:j + 1], row_in(j)[:, D + 1:D + 2])
                V.tensor_tensor(pair_i[:, j:j + 1], row_in(j)[:, D:D + 1], penalty[:, bass.ds(i, 1)], ALU.add).then_inc(pair_here, 1)

            def keep_turned(j, i):
                eng.wait_ge(turned, i + 1)
                V.tensor_copy(xt_in[:, j % 2, :, :], xt_b[j % 2][:, 0:2 * P].rearrange("p (c t) -> p c t", c=DC)).then_inc(xt_here, 1)

            def hidden(j, i):
                eng.wait_ge(sil_here, i + 1)
                V.tensor_tensor(h_in[:, j % 2, :], gu_b[j % 2][:, F:2 * F], sil_in[:, j % 2, :], ALU.mult).then_inc(h_here, 1)

            def keep_h(j, i):
                eng.wait_ge(h_turned, i + 1)
                if not isinstance(i, int) or i >= 2:
                    eng.wait_ge(y_done, i - 1)
                V.tensor_copy(ht_in[:, j % 2, :], ht_b[j % 2][0:F, 0:P]).then_inc(ht_here, 1)

            for j in range(GROUP):
                keep_turned(j, j)
                if j >= 1:
                    hidden(j - 1, j - 1)
                if j >= 2:
                    keep_h(j - 2, j - 2)
                take_rows(0, j, j)
            with eng.Fori(1, groups) as q:
                for j in range(GROUP):
                    i = q * GROUP + j
                    keep_turned(j, i)
                    hidden(j - 1, i - 1)
                    keep_h(j - 2, i - 2)
                    take_rows(q, j, i)
            end = groups * GROUP
            hidden(-1, end - 1)
            keep_h(-2, end - 2)
            keep_h(-1, end - 1)
            for T in range(NT):
                eng.wait_ge(y_loaded[T], 16)
                then(V.tensor_tensor(y_back[:, T, 0:2, :], y_back[:, T, 0:2, :], y_back[:, T, 2:4, :], ALU.add))
                then(V.tensor_tensor(y_back[:, T, 0, :], y_back[:, T, 0, :], y_back[:, T, 1, :], ALU.add))
                V.tensor_tensor(xres[:, T, :], xres[:, T, :], y_back[:, T, 0, :], ALU.add).then_inc(sum_ok, 1)

        @block.gpsimd
        def _(eng):
            G = nc.gpsimd
            steps = [0]

            def then(ins):
                steps[0] += 1
                ins.then_inc(pool, 1)
                eng.wait_ge(pool, steps[0])

            G.memset(neg_half[:, :], -0.5)
            then(G.memset(ident[:, :], 0.0))
            then(G.affine_select(out=ident[:, :], in_=ident[:, :], pattern=[[-1, P]], compare_op=ALU.not_equal, fill=1.0, base=0,
                                 channel_multiplier=1))
            eng.sem_inc(ident_ok, 1)

            def constants():
                G.memset(mask_b[:, :, :], 0.0)
                G.memset(ones[:, :], 1.0)
                G.memset(ones_b[:, :], 1.0)
                then(G.tensor_copy(ident_b[:, :], ident[:, :]))
                for v in v_ones:
                    then(G.memset(v[:, :, :, DK:32], 1.0))
                for st in stacks:
                    then(G.memset(st[96:99, 1, :, :], -1.0))
                then(G.memset(iota_p[:, :], 0.0))
                G.affine_select(out=mask_b[:, :, :], in_=mask_b[:, :, :], pattern=[[0, 2], [-1, P]], compare_op=ALU.is_ge, fill=MASKED, base=0,
                                channel_multiplier=1)
                then(G.affine_select(out=before_b[:, :], in_=ones_b[:, :], pattern=[[1, P]], compare_op=ALU.is_gt, fill=0.0, base=0,
                                     channel_multiplier=-1))
                G.affine_select(out=before[:, :], in_=ones[0:E, 0:E], pattern=[[1, E]], compare_op=ALU.is_gt, fill=0.0, base=0, channel_multiplier=-1)
                then(G.affine_select(out=upto[:, :], in_=ones[0:E, 0:E], pattern=[[1, E]], compare_op=ALU.is_ge, fill=0.0, base=0,
                                     channel_multiplier=-1))
                eng.sem_inc(consts, 1)

            def iotas():
                G.iota(iota_e[:, :], pattern=[[1, E]], base=0, channel_multiplier=0, allow_small_or_imprecise_dtypes=True)
                G.iota(iota_t[:, :], pattern=[[1, MAX_TILES]], base=0, channel_multiplier=0, allow_small_or_imprecise_dtypes=True)
                G.iota(iota_p[:, :], pattern=[[0, 1]], base=0, channel_multiplier=1, allow_small_or_imprecise_dtypes=True)
                then(G.iota(pair_info[:, :, 0].rearrange("p (t k) -> p t k", t=NT), pattern=[[P * TOP, NT], [1, TOP]], base=0,
                            channel_multiplier=TOP, allow_small_or_imprecise_dtypes=True))
                eng.sem_inc(iota_ok, 1)

            norm = 0
            for s in ORDER:
                stage, a = s[0], s[1:]
                if stage in ("ln1_stats", "ln2_stats", "ln3_stats"):
                    norm += 1
                    kind = int(stage[2]) - 1
                    eng.wait_ge(var_ok, norm)
                    then(G.tensor_tensor(rstd[:, kind, :], mv[:, kind, :, 1], neg_half[:, :], ALU.pow))
                    G.tensor_tensor(shift[:, kind, :], shift[:, kind, :], rstd[:, kind, :], ALU.mult).then_inc(rstd_ok, 1)
                    if norm == 1:
                        constants()
                        iotas()
                elif stage == "split":
                    k, t = a
                    n = 2 * k + t
                    eng.wait_ge(part2_ok, n + 1)
                    if k >= 1:
                        misc_wait(eng, ("stack", k - 1, t, 1, 1))
                    r_ = rest.rearrange("p (x h d) -> p x h d", x=2, h=HEADS)
                    p2 = part2.rearrange("p (x h d) -> p x h d", x=2, h=HEADS)
                    G.tensor_tensor(stk[t][:, 0, :, 4, :], r_[:, 0], p2[:, 0], ALU.subtract)
                    G.tensor_tensor(stk[t][:, 1, :, 0, :], r_[:, 1], p2[:, 1], ALU.subtract).then_inc(stk3_ok, 1)
                elif stage == "hot":
                    k, = a
                    T0 = k * TB
                    if k >= 1:
                        eng.wait_ge(chose_ok, k)
                    misc_wait(eng, ("v", B - 1))
                    eng.wait_ge(expd_ok, k + 1)
                    eng.wait_ge(hot_ok, k + 1)
                    for t in range(TB):
                        ins = G.tensor_tensor(exp_hot[:, t], chosen[:, T0 + t, :, :], expd[:, t, :].unsqueeze(1).to_broadcast([P, TOP, E]), ALU.mult)
                    ins.then_inc(exp_hot_ok, 1)
                elif stage == "causal":
                    k, i = a
                    eng.wait_ge(probs_used, k * HEADS + 2 * i + 2)
                    lo = (2 * i) % PT_SLOTS
                    v = pt[:, lo:lo + 2, :].rearrange("p s c -> p (s c)")[:, P:5 * P].rearrange("p (a c) -> p a c", a=4)
                    G.affine_select(out=v, in_=v, pattern=[[0, 4], [1, P]], compare_op=ALU.is_ge, fill=0.0, base=0,
                                    channel_multiplier=-1).then_inc(causal_ok, 1)
            for n in range(NT * TOP):
                slot = n % ROW_SLOTS
                if slot == 0:
                    eng.wait_ge(pos_ok, n // TOP + 1)
                eng.wait_ge(rows_filled, n + 1)
                G.indirect_dma_start(rows_dram, bass.IndirectOffsetOnAxis(pos_i[:, n:n + 1], 0), row_out[:, slot, :], None) \
                    .then_inc(row_sent[slot], 16)
            eng.wait_ge(tiles_ok, 1)
            last = nc.gpsimd.value_load(tile_i[0:1, 2 * MAX_TILES:2 * MAX_TILES + 1], min_val=MIN_LAST, max_val=MAX_LAST)
            groups = last + 1

            bound = nc.gpsimd.to_reg(PAIRS - 1)

            def send(j, i):
                here = i + 1 if isinstance(i, int) else nc.gpsimd.to_reg(i + 1)
                eng.wait_ge(pos_ok, 1)
                eng.wait_ge(y_here, here)
                G.indirect_dma_start(y_dram, bass.IndirectOffsetOnAxis(pair_i[:, j:j + 1], 0), y_out[:, j % Y_SLOTS, :], None,
                                     bounds_check=bound, oob_is_err=False).then_inc(y_sent[j % Y_SLOTS], 16)

            for j in range(GROUP):
                send(j, j)
            with eng.Fori(1, groups) as q:
                for j in range(GROUP):
                    send(j, q * GROUP + j)


_INS = ['x', 'ctx_1024', 'L0_attn_Wq', 'L0_attn_Wk', 'L0_attn_Wv', 'L0_attn_Wo', 'L0_xattn_Wq', 'L0_xattn_bq', 'L0_xattn_Wk',
        'L0_xattn_bk', 'L0_ffn_router_w', 'L0_ffn_router_bias', 'L0_ffn_wg', 'L0_ffn_wu', 'L0_ffn_wd', 'L0_ffn_swg', 'L0_ffn_swu',
        'L0_ffn_swd']


def kernel(**inputs):
    import numpy as np
    import concourse.bacc as bacc
    from concourse.bass_utils import run_bass_kernel_spmd

    nc = bacc.Bacc("TRN2", target_bir_lowering=False, num_devices=1)
    arrays, args = {}, []
    for name in _INS:
        a = np.ascontiguousarray(inputs[name])
        arrays[f"in_{name}"] = a
        args.append(nc.dram_tensor(f"in_{name}", a.shape, mybir.dt.from_np(a.dtype), kind="ExternalInput").ap())
    args.append(nc.dram_tensor("out_0", arrays["in_x"].shape, F32, kind="ExternalOutput").ap())
    decoder_layer(nc, *args)
    r = run_bass_kernel_spmd(nc, [arrays], core_ids=[0])
    return r.results[0]["out_0"]
```
